# Optimizing a Trainium2 kernel written in Bass

```python
import numpy as np
import jax
import jax.numpy as jnp

def _softmax(x, axis=-1):
    return jax.nn.softmax(x, axis=axis)

def _gelu(x):
    return jax.nn.gelu(x, approximate=True)

def _silu(x):
    return jax.nn.silu(x)

def _sigmoid(x):
    return jax.nn.sigmoid(x)

def _layernorm(x, axis=-1, eps=1e-05):
    m = jnp.mean(x, axis=axis, keepdims=True)
    v = jnp.var(x, axis=axis, keepdims=True)
    return (x - m) / jnp.sqrt(v + eps)

def _scatter_add(tgt, idx, src, axis=0):
    return tgt.at[idx].add(src)

def _segment_sum(src, seg, n):
    return jax.ops.segment_sum(src, seg, n)
kernel_name = 'mk_gnn_resnorm_d4_gnn_r64_3db954'

def setup_inputs(seed: int=0):
    np.random.seed(seed)
    _w = jnp.asarray

    def _rec_inputs():
        import jax
        import jax.numpy as jnp
        _gk = jax.random.key(seed)
        x = -0.0001006 + 1 * jax.random.normal(jax.random.fold_in(_gk, 1), (100000, 96), jnp.float32)
        src = jax.random.randint(jax.random.fold_in(_gk, 2), (25000,), 0, 100000, jnp.int32)
        dst = jnp.minimum((100000 * jax.random.uniform(jax.random.fold_in(_gk, 3), (25000,)) ** 2.0).astype(jnp.int32), 99999)
        _o = jnp.argsort(dst, stable=True)
        src = src[_o]
        dst = dst[_o]
        edge_attr_96 = 5.93493e-05 + 1.00006 * jax.random.normal(jax.random.fold_in(_gk, 12), (25000, 96), jnp.float32)
        return (x, src, dst, edge_attr_96)
    x, src, dst, edge_attr_96 = _rec_inputs()

    def _L0_gnn_setup():
        import jax, jax.numpy as jnp
        import numpy as np
        N_NODES = 50000
        N_EDGES = 12500
        D_IN = 96
        D_OUT = 96
        key = jax.random.key(seed)
        k1, k2, k3, k4 = jax.random.split(key, 4)
        x = jax.random.normal(k1, (N_NODES, D_IN), dtype=jnp.float32)
        edge_index = jax.random.randint(k2, (2, N_EDGES), 0, N_NODES, dtype=jnp.int64)
        W = jax.random.normal(k3, (D_IN, D_OUT), dtype=jnp.float32) * (1.0 / np.sqrt(D_IN))
        b = jax.random.normal(k4, (D_OUT,), dtype=jnp.float32) * 0.01
        return {'x': x, 'edge_index': edge_index, 'W': W, 'b': b}
    _L0_gnn_all = _L0_gnn_setup()
    _L0_gnn_in = {k: v for k, v in _L0_gnn_all.items() if k in ('W', 'b')}
    del _L0_gnn_all

    def _L1_gnn_setup():
        import jax, jax.numpy as jnp
        import numpy as np
        EPS = 1e-07
        BETA = 1.0
        key = jax.random.key(seed)
        k1, k2, k3, k4 = jax.random.split(key, 4)
        N, E, D_IN, D_OUT = (50000, 12500, 96, 96)
        feat = jax.random.normal(k1, (N, D_IN), dtype=jnp.float32)
        src = jax.random.randint(k2, (E,), 0, N, dtype=jnp.int32)
        dst = jax.random.randint(k3, (E,), 0, N, dtype=jnp.int32)
        W = jax.random.normal(k4, (D_IN, D_OUT), dtype=jnp.float32) / np.sqrt(D_IN)
        b = jnp.zeros((D_OUT,), dtype=jnp.float32)
        return {'feat': feat, 'src': src, 'dst': dst, 'W': W, 'b': b}
    _L1_gnn_all = _L1_gnn_setup()
    _L1_gnn_in = {k: v for k, v in _L1_gnn_all.items() if k in ('W', 'b')}
    del _L1_gnn_all

    def _L2_gnn_setup():
        import jax, jax.numpy as jnp
        import numpy as np
        N_NODES = 50000
        N_FEAT = 96
        N_EDGES = 12500
        K_HOPS = 2
        key = jax.random.key(seed)
        k1, k2 = jax.random.split(key)
        x = jax.random.normal(k1, (N_NODES, N_FEAT), dtype=jnp.float32)
        edge_index = jax.random.randint(k2, (2, N_EDGES), 0, N_NODES, dtype=jnp.int64)
        return {'x': x, 'edge_index': edge_index}
    _L2_gnn_all = _L2_gnn_setup()
    _L2_gnn_in = {k: v for k, v in _L2_gnn_all.items() if k in ()}
    del _L2_gnn_all

    def _L3_gnn_setup():
        import jax, jax.numpy as jnp
        import numpy as np
        N_NODES = 50000
        N_EDGES = 12500
        IN_DIM = 96
        NUM_HEADS = 8
        HEAD_DIM = IN_DIM // NUM_HEADS
        key = jax.random.key(seed)
        ks = jax.random.split(key, 11)
        s = 1.0 / np.sqrt(IN_DIM)
        return {'x': jax.random.normal(ks[0], (N_NODES, IN_DIM), dtype=jnp.float32), 'edge_index': jax.random.randint(ks[1], (2, N_EDGES), 0, N_NODES, dtype=jnp.int64), 'edge_attr': jax.random.normal(ks[2], (N_EDGES, IN_DIM), dtype=jnp.float32), 'Wq': jax.random.normal(ks[3], (IN_DIM, IN_DIM), dtype=jnp.float32) * s, 'bq': jax.random.normal(ks[4], (IN_DIM,), dtype=jnp.float32) * s, 'Wk': jax.random.normal(ks[5], (IN_DIM, IN_DIM), dtype=jnp.float32) * s, 'bk': jax.random.normal(ks[6], (IN_DIM,), dtype=jnp.float32) * s, 'We': jax.random.normal(ks[7], (IN_DIM, IN_DIM), dtype=jnp.float32) * s, 'be': jax.random.normal(ks[8], (IN_DIM,), dtype=jnp.float32) * s, 'Wv': jax.random.normal(ks[9], (IN_DIM, IN_DIM), dtype=jnp.float32) * s, 'bv': jax.random.normal(ks[10], (IN_DIM,), dtype=jnp.float32) * s}
    _L3_gnn_all = _L3_gnn_setup()
    _L3_gnn_in = {k: v for k, v in _L3_gnn_all.items() if k in ('Wq', 'bq', 'Wk', 'bk', 'We', 'be', 'Wv', 'bv')}
    del _L3_gnn_all
    return {'x': x, 'src': src, 'dst': dst, 'edge_attr_96': edge_attr_96, 'L0_gnn_W': _L0_gnn_in['W'], 'L0_gnn_b': _L0_gnn_in['b'], 'L1_gnn_W': _L1_gnn_in['W'], 'L1_gnn_b': _L1_gnn_in['b'], 'L3_gnn_Wq': _L3_gnn_in['Wq'], 'L3_gnn_bq': _L3_gnn_in['bq'], 'L3_gnn_Wk': _L3_gnn_in['Wk'], 'L3_gnn_bk': _L3_gnn_in['bk'], 'L3_gnn_We': _L3_gnn_in['We'], 'L3_gnn_be': _L3_gnn_in['be'], 'L3_gnn_Wv': _L3_gnn_in['Wv'], 'L3_gnn_bv': _L3_gnn_in['bv']}

def reference(x, src, dst, edge_attr_96, L0_gnn_W, L0_gnn_b, L1_gnn_W, L1_gnn_b, L3_gnn_Wq, L3_gnn_bq, L3_gnn_Wk, L3_gnn_bk, L3_gnn_We, L3_gnn_be, L3_gnn_Wv, L3_gnn_bv):
    import jax
    import jax.numpy as jnp

    def _L0_gnn_ref(x, edge_index, W, b):
        import jax, jax.numpy as jnp
        import numpy as np
        N_NODES = 50000
        N_EDGES = 12500
        D_IN = 96
        D_OUT = 96
        num_nodes = x.shape[0]
        src, dst = (edge_index[0], edge_index[1])
        messages = x[src] @ W + b
        out = jax.ops.segment_sum(messages, dst, num_segments=num_nodes)
        deg = jax.ops.segment_sum(jnp.ones((dst.shape[0],), dtype=x.dtype), dst, num_segments=num_nodes)
        deg = jnp.clip(deg, 1.0, None)
        return out / deg[:, None]

    def _L1_gnn_ref(feat, src, dst, W, b):
        import jax, jax.numpy as jnp
        import numpy as np
        EPS = 1e-07
        BETA = 1.0
        N = feat.shape[0]
        m = jax.nn.relu(feat[src]) + EPS
        logits = BETA * m
        seg_max = jax.ops.segment_max(logits, dst, num_segments=N)
        ex = jnp.exp(logits - seg_max[dst])
        denom = jax.ops.segment_sum(ex, dst, num_segments=N)
        a = ex / denom[dst]
        msg = jax.ops.segment_sum(a * m, dst, num_segments=N)
        feats = feat + msg
        return feats @ W + b

    def _L2_gnn_ref(x, edge_index):
        import jax, jax.numpy as jnp
        import numpy as np
        N_NODES = 50000
        N_FEAT = 96
        N_EDGES = 12500
        K_HOPS = 2
        N = x.shape[0]
        loops = jnp.arange(N, dtype=edge_index.dtype)
        src = jnp.concatenate([edge_index[0], loops])
        dst = jnp.concatenate([edge_index[1], loops])
        ew = jnp.ones(src.shape[0], dtype=x.dtype)
        deg = jax.ops.segment_sum(ew, dst, num_segments=N)
        deg_inv_sqrt = jnp.where(deg > 0, jax.lax.rsqrt(deg), jnp.zeros_like(deg))
        norm = deg_inv_sqrt[src] * ew * deg_inv_sqrt[dst]

        def hop(h):
            return jax.ops.segment_sum(norm[:, None] * h[src], dst, num_segments=N)
        h = x
        for _ in range(K_HOPS):
            h = hop(h)
        return h

    def _L3_gnn_ref(x, edge_index, edge_attr, Wq, bq, Wk, bk, We, be, Wv, bv):
        import jax, jax.numpy as jnp
        import numpy as np
        N_NODES = 50000
        N_EDGES = 12500
        IN_DIM = 96
        NUM_HEADS = 8
        HEAD_DIM = IN_DIM // NUM_HEADS
        N = x.shape[0]
        H, D = (NUM_HEADS, HEAD_DIM)
        Q_h = (x @ Wq + bq).reshape(N, H, D)
        K_h = (x @ Wk + bk).reshape(N, H, D)
        V_h = (x @ Wv + bv).reshape(N, H, D)
        E = (edge_attr @ We + be).reshape(-1, H, D)
        src_idx = edge_index[0]
        dst_idx = edge_index[1]
        src = K_h[src_idx]
        dest = Q_h[dst_idx]
        score = src * dest / jnp.sqrt(jnp.asarray(D, x.dtype))
        score = score * E
        score = jnp.exp(jnp.clip(score.sum(-1, keepdims=True), -5.0, 5.0))
        msg = V_h[src_idx] * score
        wV = jax.ops.segment_sum(msg, dst_idx, num_segments=N)
        Z = jax.ops.segment_sum(score, dst_idx, num_segments=N)
        h_out = wV / (Z + 1e-06)
        return h_out.reshape(N, H * D)
    edge_index = jnp.stack([src, dst])
    x = _layernorm(x + _L0_gnn_ref(x, edge_index, L0_gnn_W, L0_gnn_b), axis=-1)
    x = _layernorm(x + _L1_gnn_ref(x, src, dst, L1_gnn_W, L1_gnn_b), axis=-1)
    x = _layernorm(x + _L2_gnn_ref(x, edge_index), axis=-1)
    x = _layernorm(x + _L3_gnn_ref(x, edge_index, edge_attr_96, L3_gnn_Wq, L3_gnn_bq, L3_gnn_Wk, L3_gnn_bk, L3_gnn_We, L3_gnn_be, L3_gnn_Wv, L3_gnn_bv), axis=-1)
    return x

_drawn_inputs = setup_inputs


def setup_inputs(seed=0):
    import zlib

    import numpy as np

    out = dict(_drawn_inputs(seed))
    spreads = {'L1_gnn_b': (0.0, 0.1)}
    factors = {'L0_gnn_b': 27.805, 'L3_gnn_bq': 8.0, 'L3_gnn_bk': 8.0, 'L3_gnn_be': 8.0}
    for name, (base, spread) in spreads.items():
        noise = np.random.default_rng([zlib.crc32(name.encode()), seed]).standard_normal(out[name].shape)
        drawn = base * np.exp(spread * noise) if base else spread * noise
        out[name] = jnp.asarray(drawn.astype(out[name].dtype))
    for name, factor in factors.items():
        out[name] = (out[name] * factor).astype(out[name].dtype)
    return out
```

```python
from contextlib import ExitStack

import concourse.bass as bass
from concourse import mybir

F32 = mybir.dt.float32
I32 = mybir.dt.int32
ALU = mybir.AluOpType
ACT = mybir.ActivationFunctionType
AX = mybir.AxisListType.X

P = 128
N, D, E = 100000, 96, 25000
COLS = 200
EP = E // COLS
TC = COLS + 1
C = 4
CHUNKS = COLS // C
RING = 4
HEADS, HD = 8, D // 8
W4 = D + HEADS
EPS = 1e-5
BIG = 1 << 20
DC = 12
DG = DC // C
DCOLS = N // P // DC * DC
DCHUNKS = DCOLS // DC
DREST = N - P * DCOLS
DRP = DREST // 2
assert EP * COLS == E and DRP * 2 == DREST and DRP <= P
ROUNDS = range(5)


class Chunk:

    def __init__(self, n, ring, slot, turn):
        self.n, self.ring, self.slot, self.turn = n, ring, slot, turn

    def before(self, k=1):
        slot = (self.slot - k) % self.ring
        return Chunk(self.n - k, self.ring, slot, self.turn - (1 if slot > self.slot or k == self.ring else 0))

    @property
    def exists(self):
        return not isinstance(self.n, int) or self.n >= 0

    @property
    def parity(self):
        return self.slot % 2


def each_chunk(eng, count, ring, step, steps=()):
    before = [s.count for s in steps]
    for n in range(ring):
        if n == ring - 1:
            before = [s.count for s in steps]
        step(Chunk(n, ring, n, 1))
    per = [(s.count - b) * ring for s, b in zip(steps, before)]
    turns = count // ring
    with eng.Fori(1, turns) as i:
        for s, stride in zip(steps, per):
            s.enter(i, stride)
        for slot in range(ring):
            step(Chunk(i * ring + slot, ring, slot, i + 1))
        for s in steps:
            s.leave(turns - 1)
    for n in range(turns * ring, count):
        step(Chunk(n, ring, n % ring, n // ring + 1))


class Steps:

    def __init__(self, eng, sem):
        self.eng, self.sem, self.count, self.offset, self.base, self.stride = eng, sem, 0, None, 0, 0
        self.sent = None

    def enter(self, i, stride):
        self.base, self.stride = self.count, stride
        self.offset = (i - 1) * stride
        self.sent = None

    def leave(self, turns):
        assert self.count - self.base == self.stride, (self.count - self.base, self.stride)
        self.count, self.offset, self.sent = self.base + turns * self.stride, None, None

    def mark(self, instruction):
        instruction.then_inc(self.sem, 1)
        self.count += 1
        self.sent = None

    def send(self, instruction, signal, value):
        instruction.then_inc(signal, 1)
        self.sent = signal, value

    def wait(self):
        if self.sent:
            self.eng.wait_ge(*self.sent)
            return
        value = self.count if self.offset is None else self.offset + self.count
        self.eng.wait_ge(self.sem, value)


def build(nc, x, src, dst, edge_attr, W0, b0, W1, b1, Wq, bq, Wk, bk, We, be, Wv, bv, out):
    with ExitStack() as ctx:
        def sb(name, shape, dt=F32):
            return ctx.enter_context(nc.sbuf_tensor(name, shape, dt))

        def sem(name):
            return ctx.enter_context(nc.semaphore(name))

        def ring_sems(name, n=RING):
            return [sem(f"{name}_{i}") for i in range(n)]

        table = {r: nc.dram_tensor(f"table{r}", (P * TC, D), F32).ap() for r in (1, 2, 3, 4)}
        table_v = {r: t.rearrange("(p t) d -> p t d", t=TC) for r, t in table.items()}
        plain = {r: nc.dram_tensor(f"plain{r}", (P, COLS, D), F32).ap() for r in (1, 2, 4)}
        row_of = nc.dram_tensor("row_of", (N, 1), I32).ap()

        ident = sb("ident", [P, P])
        ones = sb("ones", [P, P])
        w0 = sb("w0", [P, D])
        w1 = sb("w1", [P, D])
        w1c = sb("w1c", [P, D])
        wkv = sb("wkv", [P, 2 * D])
        wq = sb("wq", [P, D])
        we = sb("we", [P, D])
        wsum = sb("wsum", [P, 1])

        src_i = sb("src_i", [P, COLS], I32)
        dst_i = sb("dst_i", [P, TC], I32)
        dst_f = sb("dst_f", [P, TC])
        keep_fwd = sb("keep_fwd", [P, COLS])
        keep_rev = sb("keep_rev", [P, COLS])
        head = sb("head", [P, COLS])
        tail = sb("tail", [P, COLS])
        own = sb("own", [P, COLS])
        pull = sb("pull", [P, COLS])
        tmp_a = sb("tmp_a", [P, TC])
        tmp_b = sb("tmp_b", [P, TC])
        rep_i = sb("rep_i", [P, TC], I32)
        out_i = sb("out_i", [P, TC], I32)
        rowid = sb("rowid", [P, TC], I32)
        src_row = sb("src_row", [P, COLS], I32)
        eq_head = sb("eq_head", [P, P])
        eq_tail = sb("eq_tail", [P, P])
        deg = sb("deg", [P, TC])
        rdeg = sb("rdeg", [P, TC])
        dinv = sb("dinv", [P, TC])
        dinv2 = sb("dinv2", [P, TC])
        sdeg = sb("sdeg", [P, TC])
        bigs = sb("bigs", [P, N // EP], I32)

        V = [sb(f"V{k}", [P, C, D + 1]) for k in range(RING)]
        XD = [sb(f"XD{k}", [P, C, D]) for k in range(RING)]
        XE = [sb(f"XE{k}", [P, C, D]) for k in range(RING)]
        OT = [sb(f"OT{k}", [P, C, D]) for k in range(RING)]
        PL1 = [sb(f"PL1{k}", [P, C, D]) for k in range(2)]
        PL2 = [sb(f"PL2{k}", [P, C, D]) for k in range(2)]
        PL4 = [sb(f"PL4{k}", [P, C, D]) for k in range(2)]
        AG = [sb(f"AG{k}", [P, C, 2 * D]) for k in range(2)]
        MS = [sb(f"MS{k}", [P, C, 2 * D]) for k in range(2)]
        MM = [sb(f"MM{k}", [P, C, D]) for k in range(2)]
        AM = [sb(f"AM{k}", [P, C, D]) for k in range(2)]
        UB = sb("UB", [P, C, D])
        U2 = sb("U2", [P, C, D])
        SQ = [sb(f"SQ{k}", [P, C, D]) for k in range(2)]
        MB = [sb(f"MB{k}", [P, C, P]) for k in range(2)]
        XB = [sb(f"XB{k}", [P, C, D]) for k in range(2)]
        XA = [sb(f"XA{k}", [P, C, D]) for k in range(2)]
        QS = sb("QS", [P, C, D])
        SC = sb("SC", [P, C, HEADS])
        SC2 = sb("SC2", [P, C, HEADS])
        ZR = sb("ZR", [P, C, HEADS])
        XT = [sb(f"XT{k}", [P, C * P]) for k in range(3)]
        xseam = sb("xseam", [P, D])
        xnext = sb("xnext", [P, D])
        SG = sb("SG", [P, 1, 2 * D])
        idx = [sb(f"idx{k}", [P, C], I32) for k in range(RING)]
        idx2 = [sb(f"idx2{k}", [P, C], I32) for k in range(RING)]
        rid = [sb(f"rid{k}", [P, C], I32) for k in range(RING)]
        rst = [sb(f"rst{k}", [P, C], I32) for k in range(RING)]
        DX = [sb(f"DX{k}", [P, DC, D]) for k in range(2)]
        DY = [sb(f"DY{k}", [P, DC, D]) for k in range(2)]
        DO = [sb(f"DO{k}", [P, DC, D]) for k in range(2)]
        DSQ = [sb(f"DSQ{k}", [P, DG, C * D]) for k in range(2)]
        st = sb("st", [P, DC, 6])
        small = sb("small", [P, 8, TC])
        arg = sb("arg", [P, TC])
        lnarg = sb("lnarg", [P, TC])
        guess = sb("guess", [P, TC])
        rs = sb("rs", [P, TC])
        rs2 = sb("rs2", [P, TC])

        bank = [ctx.enter_context(nc.psum_tensor(f"bank{i}", [P, 512], F32)) for i in range(8)]
        psTA, psTB, psS = bank[0], bank[1], bank[2]
        psU = [bank[3], bank[4]]
        psY = [bank[5], bank[6]]
        psK = [bank[3], bank[4]]
        psQ, psE = bank[5], bank[6]
        dT = [bank[0], bank[1]]
        dY = [[bank[2], bank[3], bank[4]], [bank[5], bank[6], bank[7]]]

        dve_step, act_step, pool_step = sem("dve_step"), sem("act_step"), sem("pool_step")
        passed = {nc.sync.engine: sem("sp_passed"), nc.gpsimd.engine: sem("pool_passed")}
        loaded = sem("loaded")
        bigs_ready, bigs_stored = sem("bigs_ready"), sem("bigs_stored")
        consts_ready = sem("consts_ready")
        tiles_set = sem("tiles_set")
        edges_ready = sem("edges_ready")
        firsts_done = sem("firsts_done")
        prep_done = sem("prep_done")
        arg_ready, root_ready = sem("arg_ready"), sem("root_ready")
        row_entered = ring_sems("row_entered")
        row_found = ring_sems("row_found")
        d_loaded, d_stored = ring_sems("d_loaded", 2), ring_sems("d_stored", 2)
        d_arg, d_root = sem("d_arg"), sem("d_root")
        y_arg, y_root = sem("y_arg"), sem("y_root")
        d_mean = sem("d_mean")
        d_norm = sem("d_norm")
        d_turned, d_evac, d_mult = sem("d_turned"), sem("d_evac"), sem("d_mult")
        d_sq, d_out = sem("d_sq"), sem("d_out")

        v_loaded, xd_loaded = ring_sems("v_loaded"), ring_sems("xd_loaded")
        gathered, stored = ring_sems("gathered"), ring_sems("stored")

        class Round:

            def __init__(self, r):
                def s(name):
                    return sem(f"{name}{r}")
                turns = [len(range(k, CHUNKS, RING)) for k in range(RING)]
                seam = [int(k == CHUNKS % RING) for k in range(RING)]

                def ongoing(sems, per, seams):
                    return [(sems[k], sum(per[q] * turns[k] + seams[q] * seam[k] for q in range(r)))
                            for k in range(RING)]
                self.v_loaded = ongoing(v_loaded, [0, 16, 16, 16, 16], [0] * 5)
                self.xd_loaded = ongoing(xd_loaded, [0, 16, 16, 32, 32], [0, 16, 16, 32, 0])
                self.gathered = ongoing(gathered, [2 * 16 * C] + [16 * C] * 4, [16, 0, 0, 0, 0])
                self.stored = ongoing(stored, [16] * 4 + [0], [16] * 4 + [0])
                self.mask_ready = s("mask_ready")
                self.front = s("front")
                self.seam_added = s("seam_added")
                self.seam_total = s("seam_total")
                self.updated = s("updated")
                if r in (0, 1, 3, 4):
                    self.arg, self.root = s("arg"), s("root")
                if r in (0, 1):
                    self.am_ready, self.am_turned = s("am_ready"), s("am_turned")
                    self.am_evac, self.am_mult = s("am_evac"), s("am_mult")
                if r == 0:
                    self.x1_arg, self.x1_root = s("x1_arg"), s("x1_root")
                    self.x1_turned, self.x1_evac, self.x1_mult = s("x1_turned"), s("x1_evac"), s("x1_mult")
                    self.squared = s("squared")
                    self.plain_stored = ring_sems("plain_stored", 2)
                    self.deg_arg, self.deg_root = s("deg_arg"), s("deg_root")
                if r == 1:
                    self.relu_done, self.exp_ready = s("relu_done"), s("exp_ready")
                    self.msg_ready = s("msg_ready")
                if r == 4:
                    self.scaled, self.xb_ready = s("scaled"), s("xb_ready")
                    self.turned, self.evac = s("turned"), s("evac")
                    self.mult, self.q_ready = s("mult"), s("q_ready")
                    self.score_ready, self.exp_ready = s("score_ready"), s("exp_ready")
                    self.msg_ready = s("msg_ready")
                    self.seam_loaded = s("seam_loaded")
                    self.scattered = ring_sems("scattered")

        S = [Round(r) for r in ROUNDS]
        SEAM = Chunk(CHUNKS, RING, CHUNKS % RING, CHUNKS // RING + 1)

        def cols(r, c):
            if c is SEAM:
                return COLS
            return C * c.n if r < 4 else (COLS - C) - C * c.n

        def width(c):
            return 1 if c is SEAM else C

        def stand_alone(eng):
            if eng.engine in passed:
                eng.sem_inc(passed[eng.engine], 1)

        def done(eng, s, c, per=1, more=0):
            if c.exists:
                eng.wait_ge(s, (c.n + 1) * per + more)
                stand_alone(eng)

        def used(eng, s, c, per=16):
            if c.exists:
                signal, base = s[c.slot] if isinstance(s[c.slot], tuple) else (s[c.slot], 0)
                eng.wait_ge(signal, c.turn * per + base)
                stand_alone(eng)

        block = ctx.enter_context(nc.Block())

        @block.sync
        def _(sp):
            sp.wait_ge(tiles_set, 1)
            sp.dma_start(src_i[0:EP, :], src.rearrange("(p t) -> p t", t=COLS)).then_inc(loaded, 16)
            sp.dma_start(dst_i[0:EP, 0:COLS], dst.rearrange("(p t) -> p t", t=COLS)).then_inc(loaded, 16)
            sp.dma_start(dst_i[0:EP - 1, COLS:TC],
                         dst.rearrange("(p t) -> p t", t=COLS)[1:EP, 0:1],
                         allow_slow_non_contiguous=True).then_inc(loaded, 16)
            for tile, lo, w, b in ((w0, 0, W0, b0), (w1, 0, W1, b1), (wkv, 0, Wk, bk), (wkv, D, Wv, bv),
                                   (wq, 0, Wq, bq), (we, 0, We, be)):
                sp.dma_start(tile[0:D, lo:lo + D], w).then_inc(loaded, 16)
                sp.dma_start(tile[D:D + 1, lo:lo + D], b.rearrange("(o d) -> o d", o=1)).then_inc(loaded, 16)
            sp.wait_ge(bigs_ready, 1)
            sp.dma_start(row_of.rearrange("(p t) o -> p (t o)", p=EP), bigs[0:EP, :]).then_inc(bigs_stored, 16)

            xv = x[0:P * DCOLS, :].rearrange("(p t) d -> p t d", t=DCOLS)
            ov = out[0:P * DCOLS, :].rearrange("(p t) d -> p t d", t=DCOLS)

            def dense_store(c):
                done(sp, d_out, c)
                sp.dma_start(ov[:, bass.ds(c.n * DC, DC), :], DO[c.slot][:, :, :]).then_inc(d_stored[c.slot], 16)

            def dense(c):
                done(sp, d_norm, c.before(2))
                sp.dma_start(DX[c.slot][:, :, :], xv[:, bass.ds(c.n * DC, DC), :]).then_inc(d_loaded[c.slot], 16)
                if c.before(2).exists:
                    dense_store(c.before(2))

            each_chunk(sp, DCHUNKS, 2, dense)
            last = Chunk(DCHUNKS, 2, DCHUNKS % 2, DCHUNKS // 2 + 1)
            done(sp, d_norm, last.before(2))
            sp.dma_start(DX[last.slot][0:DRP, 0:2, :],
                         x[P * DCOLS:N, :].rearrange("(p t) d -> p t d", t=2)).then_inc(d_loaded[last.slot], 16)
            dense_store(last.before(2))
            dense_store(last.before(1))
            done(sp, d_out, last)
            sp.dma_start(out[P * DCOLS:N, :].rearrange("(p t) d -> p t d", t=2),
                         DO[last.slot][0:DRP, 0:2, :]).then_inc(d_stored[last.slot], 16)

            ea = edge_attr.rearrange("(p t) d -> p t d", t=COLS)

            def store(r, c):
                s = S[r]
                at, w = cols(r, c), width(c)
                done(sp, s.updated, c)
                sp.dma_start(table_v[r + 1][:, bass.ds(at, w), :], OT[c.slot][:, 0:w, :]).then_inc(s.stored[c.slot][0], 16)
                if r == 0 and c is not SEAM:
                    for rr, tile in ((1, PL1), (2, PL2), (4, PL4)):
                        sp.dma_start(plain[rr][:, bass.ds(at, C), :],
                                     tile[c.parity][:, :, :]).then_inc(s.plain_stored[c.parity], 16)

            def load(r, c):
                s, old = S[r], c.before(RING)
                at = cols(r, c)
                if c is not SEAM:
                    if r in (2, 3):
                        done(sp, s.front, old)
                        done(sp, s.seam_added, old)
                    if r == 1:
                        done(sp, s.relu_done, old)
                    if r == 4:
                        done(sp, s.turned, old, 3)
                    sp.dma_start(V[c.slot][:, :, 0:D], plain[{1: 1, 2: 2, 3: 2, 4: 4}[r]][:, bass.ds(at, C), :]
                                 ).then_inc(s.v_loaded[c.slot][0], 16)
                if r < 4 or c is not SEAM:
                    done(sp, s.updated, old)
                    w = width(c)
                    sp.dma_start(XD[c.slot][:, 0:w, :], table_v[r][:, bass.ds(at, w), :]
                                 ).then_inc(s.xd_loaded[c.slot][0], 16)
                    if r == 3:
                        sp.dma_start(XE[c.slot][:, 0:w, :], table_v[2][:, bass.ds(at, w), :]
                                     ).then_inc(s.xd_loaded[c.slot][0], 16)
                    if r == 4:
                        sp.dma_start(XE[c.slot][0:EP, :, :], ea[:, bass.ds(at, C), :]
                                     ).then_inc(s.xd_loaded[c.slot][0], 16)

            for r in ROUNDS:
                if r:
                    for k in range(RING):
                        signal, base = S[r - 1].stored[k]
                        sp.wait_ge(signal, base + 16 * len(range(k, CHUNKS + 1, RING)))
                    if r == 1:
                        for k in range(2):
                            sp.wait_ge(S[0].plain_stored[k], 16 * 3 * (CHUNKS // 2))
                if r == 4:
                    seam_rows = table_v[4][:, COLS:TC, :].rearrange("p t d -> p (t d)")
                    sp.dma_start(xseam[:, :], seam_rows).then_inc(S[4].seam_loaded, 16)
                    sp.dma_start(xnext[0:P - 1, :], seam_rows[1:P, :]).then_inc(S[4].seam_loaded, 16)

                def step(c):
                    if r:
                        load(r, c)
                    if r < 4 and c.before(2).exists:
                        store(r, c.before(2))

                each_chunk(sp, CHUNKS, RING, step)
                if r:
                    load(r, SEAM)
                if r < 4:
                    store(r, SEAM.before(2))
                    store(r, SEAM.before(1))
                    store(r, SEAM)
            for k in range(2):
                sp.wait_ge(d_stored[k], 16 * len(range(k, DCHUNKS + 1, 2)))
            for k in range(RING):
                full, seams = len(range(k, CHUNKS, RING)), int(k == SEAM.slot)
                sp.wait_ge(S[4].scattered[k], 16 * (C * full + seams))

        @block.gpsimd
        def _(pool):
            me = Steps(pool, pool_step)
            last_node, last_entry = pool.to_reg(N - 1), pool.to_reg(P * TC - 1)
            me.mark(pool.memset(src_i[:, :], 0))
            me.wait()
            pool.memset(dst_i[:, :], BIG).then_inc(tiles_set, 1)
            pool.wait_ge(tiles_set, 1)
            pool.memset(bigs[:, :], BIG).then_inc(bigs_ready, 1)
            pool.wait_ge(bigs_ready, 1)
            me.mark(pool.memset(ident[:, :], 0.0))
            me.wait()
            me.mark(pool.iota(rowid[:, :], pattern=[[1, TC]], base=0, channel_multiplier=TC))
            me.wait()
            pool.affine_select(out=ident[:, :], in_=ident[:, :], compare_op=ALU.not_equal, fill=1.0, base=0,
                               pattern=[[-1, P]], channel_multiplier=1).then_inc(consts_ready, 1)

            def stage(to, of, at, w):
                me.mark(pool.tensor_copy(to[:, 0:w], of[:, bass.ds(at, w)]))

            pool.wait_ge(edges_ready, 1)
            pool.wait_ge(bigs_stored, 16)

            def enter_rows(c):
                at, w = cols(0, c), width(c)
                used(pool, row_entered, c.before(RING), 16 * C)
                stage(idx[c.slot], rep_i, at, w)
                stage(rid[c.slot], rowid, at, w)
                me.wait()
                stand_alone(pool)
                for j in range(w):
                    pool.indirect_dma_start(
                        out=row_of, out_offset=bass.IndirectOffsetOnAxis(ap=idx[c.slot][:, j:j + 1], axis=0),
                        in_=rid[c.slot][:, j:j + 1], in_offset=None, bounds_check=last_node,
                        oob_is_err=False).then_inc(row_entered[c.slot], 16)

            each_chunk(pool, CHUNKS, RING, enter_rows, [me])
            enter_rows(SEAM)
            for k in range(RING):
                pool.wait_ge(row_entered[k], 16 * (C * len(range(k, CHUNKS, RING)) + int(k == SEAM.slot)))

            def keep_rows(c):
                used(pool, row_found, c, 16 * C)
                me.mark(pool.tensor_copy(src_row[:, bass.ds(cols(0, c), C)], rst[c.slot][:, :]))

            def find_rows(c):
                stage(idx[c.slot], src_i, cols(0, c), C)
                me.wait()
                stand_alone(pool)
                for j in range(C):
                    pool.indirect_dma_start(
                        out=rst[c.slot][:, j:j + 1], out_offset=None, in_=row_of,
                        in_offset=bass.IndirectOffsetOnAxis(ap=idx[c.slot][:, j:j + 1], axis=0),
                        bounds_check=last_node, oob_is_err=False).then_inc(row_found[c.slot], 16)
                if c.before(1).exists:
                    keep_rows(c.before(1))

            each_chunk(pool, CHUNKS, RING, find_rows, [me])
            keep_rows(SEAM.before(1))

            def gather(c, w, to, indices, at, of, last_row, ix, signal):
                stage(ix[c.slot], indices, at, w)
                me.wait()
                stand_alone(pool)
                for j in range(w):
                    pool.indirect_dma_start(
                        out=to[c.slot][:, j, 0:D], out_offset=None, in_=of,
                        in_offset=bass.IndirectOffsetOnAxis(ap=ix[c.slot][:, j:j + 1], axis=0),
                        bounds_check=last_row, oob_is_err=False).then_inc(signal[c.slot][0], 16)

            def gather_x(c):
                s, old = S[0], c.before(RING)
                done(pool, s.front, old)
                done(pool, s.seam_added, old)
                gather(c, C, V, src_i, cols(0, c), x, last_node, idx, s.gathered)
                done(pool, s.updated, old)
                gather(c, C, XD, dst_i, cols(0, c), x, last_node, idx2, s.gathered)

            each_chunk(pool, CHUNKS, RING, gather_x, [me])
            done(pool, S[0].updated, SEAM.before(RING))
            gather(SEAM, 1, XD, dst_i, 0, x, last_node, idx2, S[0].gathered)

            def scatter(c):
                s, at, w = S[4], cols(4, c), width(c)
                done(pool, s.updated, c)
                used(pool, s.scattered, c.before(RING), 16 * C)
                stage(idx2[c.slot], out_i, at, w)
                me.wait()
                stand_alone(pool)
                for j in range(w):
                    pool.indirect_dma_start(
                        out=out, out_offset=bass.IndirectOffsetOnAxis(ap=idx2[c.slot][:, j:j + 1], axis=0),
                        in_=OT[c.slot][:, j, :], in_offset=None, bounds_check=last_node,
                        oob_is_err=False).then_inc(s.scattered[c.slot], 16)

            for r in range(1, 5):
                for k in range(RING):
                    signal, base = S[r - 1].stored[k]
                    pool.wait_ge(signal, base + 16 * len(range(k, CHUNKS + 1, RING)))
                if r == 4:
                    for k in range(2):
                        pool.wait_ge(d_stored[k], 16 * len(range(k, DCHUNKS + 1, 2)))

                def step(c):
                    used(pool, S[r].v_loaded, c)
                    gather(c, C, V, src_row, cols(r, c), table[r], last_entry, idx, S[r].gathered)
                    if r == 4 and c.before(3).exists:
                        scatter(c.before(3))

                each_chunk(pool, CHUNKS, RING, step, [me])
            for k in (3, 2, 1):
                scatter(SEAM.before(k))
            scatter(SEAM)

        @block.tensor
        def _(pe):
            pe.wait_ge(consts_ready, 1)
            pe.wait_ge(edges_ready, 1)
            pe.matmul(psS[:, 0:P], ones[:, :], MB[0][:, 0, :], start=True, stop=True).then_inc(firsts_done, 1)

            def turn(to, of, n):
                for j in range(n):
                    last = pe.transpose(to[0:D, j * P:(j + 1) * P], of[:, j, :], ident[:, :])
                return last

            def times(to, xt, w, n):
                for j in range(n):
                    last = pe.matmul(to[:, j * D:(j + 1) * D], xt[0:D + 1, j * P:(j + 1) * P], w[0:D + 1, :],
                                     start=True, stop=True)
                return last

            pe.wait_ge(prep_done, 1)

            def dense(c, n=DC):
                groups = [(g, min(C, n - g * C)) for g in range((n + C - 1) // C)]
                done(pe, d_norm, c)
                for g, m in groups:
                    q = c.n * DG + g
                    if g >= 2 or not (isinstance(c.n, int) and c.n == 0):
                        pe.wait_ge(d_evac, q - 1)
                    turn(dT[g % 2], DY[c.slot][:, g * C:(g + 1) * C, :], m).then_inc(d_turned, 1)
                    if g >= 1:
                        multiply(c, g - 1, C)
                multiply(c, *groups[-1])

            def multiply(c, g, m):
                q = c.n * DG + g
                if g == 0:
                    done(pe, d_out, c.before(2))
                pe.wait_ge(d_evac, q + 1)
                times(dY[c.slot][g], XT[g % 3], w1c, m).then_inc(d_mult, 1)

            each_chunk(pe, DCHUNKS, 2, dense)
            dense(Chunk(DCHUNKS, 2, DCHUNKS % 2, DCHUNKS // 2 + 1), 2)

            def seam(r, c, values, w):
                s = S[r]
                done(pe, s.mask_ready, c)
                order = range(C)
                for j in order:
                    first = isinstance(c.n, int) and c.n == 0 and j == 0
                    last = pe.matmul(psS[:, 0:w], MB[c.parity][:, j, :], values[:, j, 0:w], start=first, stop=False)
                last.then_inc(s.seam_added, 1)

            for r in ROUNDS:
                s = S[r]
                w = {0: D + 1, 1: 2 * D, 2: D, 3: D, 4: W4}[r]

                def am(c):
                    n = width(c)
                    done(pe, s.am_ready, c)
                    done(pe, s.am_evac, c.before(1))
                    turn(psTB, AM[c.parity], n).then_inc(s.am_turned, 1)
                    done(pe, s.am_evac, c)
                    done(pe, s.updated, c.before(2))
                    times(psU[c.parity], XT[1], {0: w0, 1: w1}[r], n).then_inc(s.am_mult, 1)

                def x1(c):
                    done(pe, s.front, c)
                    done(pe, s.x1_evac, c.before(1))
                    turn(psTA, PL1[c.parity], C).then_inc(s.x1_turned, 1)
                    done(pe, s.x1_evac, c)
                    times(psY[c.parity], XT[0], w1c, C).then_inc(s.x1_mult, 1)

                def attend(c):
                    used(pe, s.gathered, c, 16 * C)
                    if c.before(1).exists:
                        pe.wait_ge(s.evac, c.before(1).n * 3 + 3)
                    turn(psTA, V[c.slot][:, :, 0:D], C).then_inc(s.turned, 1)
                    used(pe, s.xd_loaded, c, 32)
                    turn(psTB, XE[c.slot], C).then_inc(s.turned, 1)
                    done(pe, s.xb_ready, c)
                    pe.wait_ge(s.evac, c.n * 3 + 1)
                    turn(psTA, XB[c.parity], C).then_inc(s.turned, 1)
                    done(pe, s.msg_ready, c.before(1))
                    for j in range(C):
                        pe.matmul(psK[j // 2][:, j % 2 * 2 * D:(j % 2 + 1) * 2 * D], XT[0][0:D + 1, j * P:(j + 1) * P],
                                  wkv[0:D + 1, :], start=True, stop=True)
                    pe.wait_ge(s.evac, c.n * 3 + 2)
                    times(psE, XT[1], we, C)
                    pe.wait_ge(s.evac, c.n * 3 + 3)
                    times(psQ, XT[2], wq, C).then_inc(s.mult, 1)

                def step(c):
                    if r == 0:
                        am(c)
                        x1(c)
                        seam(r, c, V[c.slot], w)
                    if r == 1:
                        done(pe, s.msg_ready, c)
                        seam(r, c, MS[c.parity], w)
                        am(c)
                    if r in (2, 3):
                        done(pe, s.front, c)
                        seam(r, c, V[c.slot], w)
                    if r == 4:
                        attend(c)
                        if c.before(1).exists:
                            done(pe, s.msg_ready, c.before(1))
                            seam(r, c.before(1), MS[1 - c.parity], w)

                each_chunk(pe, CHUNKS, RING, step)
                final = SEAM.before(1)
                if r == 4:
                    done(pe, s.msg_ready, final)
                    seam(r, final, MS[final.parity], w)
                done(pe, s.updated, final)
                if r < 4:
                    pe.matmul(psS[:, 0:w], eq_tail[:, :], AG[final.parity][:, C - 1, 0:w], start=False,
                              stop=True).then_inc(s.seam_total, 1)
                else:
                    pe.matmul(psS[:, 0:w], eq_head[:, :], AG[final.parity][:, 0, 0:w], start=False,
                              stop=True).then_inc(s.seam_total, 1)
                if r in (0, 1):
                    am(SEAM)

        @block.scalar
        def _(act):
            me = Steps(act, act_step)
            act.preload_act_table_set("natural_log_exp_and_others")

            def root(n, lo=0):
                me.mark(act.activation(lnarg[:, lo:lo + n], arg[:, lo:lo + n], ACT.Ln))
                me.wait()
                return act.activation(guess[:, lo:lo + n], lnarg[:, lo:lo + n], ACT.Exp, scale=-0.5)

            act.wait_ge(arg_ready, 1)
            root(COLS).then_inc(root_ready, 1)

            def dense_front(c, n=DC):
                done(act, d_arg, c)
                root(n).then_inc(d_root, 1)
                done(act, d_mean, c)
                done(act, d_mult, c.before(2), DG)
                for j in range(n):
                    last = act.activation(DY[c.slot][:, j, :], DX[c.slot][:, j, :], ACT.Identity,
                                          bias=small[:, 6, j:j + 1], scale=rs[:, j:j + 1])
                last.then_inc(d_norm, 1)
                for g in range((n + C - 1) // C):
                    m = min(C, n - g * C)
                    q = c.n * DG + g
                    act.wait_ge(d_turned, q + 1)
                    act.activation(XT[g % 3][0:D, 0:m * P], dT[g % 2][0:D, 0:m * P], ACT.Copy).then_inc(d_evac, 1)

            def dense_square(c, n=DC):
                g = (n + C - 1) // C
                act.wait_ge(d_mult, c.n * DG + g)
                for k in range(g):
                    m = min(C, n - k * C)
                    last = act.activation(DSQ[c.slot][:, k, 0:m * D], dY[c.slot][k][:, 0:m * D], ACT.Square)
                last.then_inc(d_sq, 1)

            def dense_back(c, n=DC):
                done(act, y_arg, c)
                root(n).then_inc(y_root, 1)

            def dense(c):
                dense_front(c)
                if c.before(1).exists:
                    dense_square(c.before(1))
                    dense_back(c.before(1))

            each_chunk(act, DCHUNKS, 2, dense, [me])
            last = Chunk(DCHUNKS, 2, DCHUNKS % 2, DCHUNKS // 2 + 1)
            dense_front(last, 2)
            dense_square(last.before(1))
            dense_back(last.before(1))
            dense_square(last, 2)
            dense_back(last, 2)

            def masks(r, c):
                s = S[r]
                done(act, s.seam_added, c.before(2))
                for j in range(C):
                    m, eq = (head, eq_head) if r < 4 else (tail, eq_tail)
                    last = act.activation(MB[c.parity][:, j, :], eq[:, :], ACT.Copy, scale=m[:, bass.ds(cols(r, c) + j, 1)])
                last.then_inc(s.mask_ready, 1)

            for r in ROUNDS:
                s = S[r]

                if r:
                    act.wait_ge(S[r - 1].seam_total, 1)

                def evac(to, of, n, turned, value, signal):
                    act.wait_ge(turned, value)
                    act.activation(to[0:D, 0:n * P], of[0:D, 0:n * P], ACT.Copy).then_inc(signal, 1)

                def am(c):
                    done(act, s.am_mult, c.before(1))
                    evac(XT[1], psTB, width(c), s.am_turned, c.n + 1, s.am_evac)

                def front(c):
                    if r == 0:
                        done(act, s.x1_arg, c)
                        root(C).then_inc(s.x1_root, 1)
                        masks(r, c)
                        am(c)
                        done(act, s.x1_mult, c.before(1))
                        evac(XT[0], psTA, C, s.x1_turned, c.n + 1, s.x1_evac)
                    if r == 1:
                        used(act, s.gathered, c, 16 * C)
                        done(act, s.msg_ready, c.before(2))
                        done(act, s.seam_added, c.before(2))
                        act.activation(MM[c.parity][:, :, :], V[c.slot][:, :, 0:D], ACT.Relu).then_inc(s.relu_done, 1)
                        done(act, s.relu_done, c)
                        act.activation(MS[c.parity][:, :, D:2 * D], MM[c.parity][:, :, :], ACT.Exp
                                       ).then_inc(s.exp_ready, 1)
                        masks(r, c)
                        am(c)
                    if r in (2, 3):
                        masks(r, c)
                    if r == 4:
                        used(act, s.xd_loaded, c, 32)
                        done(act, s.xb_ready, c.before(2))
                        for j in range(C):
                            last = act.activation(XA[c.parity][:, j, :], XD[c.slot][:, j, :], ACT.Copy,
                                                  scale=own[:, bass.ds(cols(r, c) + j, 1)])
                        last.then_inc(s.scaled, 1)
                        masks(r, c)
                        done(act, s.mult, c.before(1))
                        evac(XT[0], psTA, C, s.turned, c.n * 3 + 1, s.evac)
                        evac(XT[1], psTB, C, s.turned, c.n * 3 + 2, s.evac)
                        evac(XT[2], psTA, C, s.turned, c.n * 3 + 3, s.evac)

                def back(c):
                    n = width(c)
                    if r == 0 and c is not SEAM:
                        done(act, s.x1_mult, c)
                        act.activation(SQ[c.parity][:, :, :], psY[c.parity][:, 0:C * D], ACT.Square
                                       ).then_inc(s.squared, 1)
                    if r == 4 and c is not SEAM:
                        done(act, s.score_ready, c)
                        act.activation(MS[c.parity][:, :, D:W4], SC2[:, :, :], ACT.Exp).then_inc(s.exp_ready, 1)
                    if r in (0, 1, 3, 4):
                        done(act, s.arg, c)
                        root(3 * C if r == 0 and c is not SEAM else n).then_inc(s.root, 1)

                def step(c):
                    front(c)
                    if c.before(1).exists:
                        back(c.before(1))
                    if r == 4:
                        done(act, s.mult, c)
                        act.activation(QS[:, :, :], psQ[:, 0:C * D], ACT.Copy).then_inc(s.q_ready, 1)

                each_chunk(act, CHUNKS, RING, step, [me])
                back(SEAM.before(1))
                if r == 0:
                    act.wait_ge(s.deg_arg, 1)
                    root(1).then_inc(s.deg_root, 1)
                if r in (0, 1):
                    am(SEAM)
                if r in (0, 1, 3, 4):
                    back(SEAM)

        @block.vector
        def _(dve):
            me = Steps(dve, dve_step)

            def wide(a, at, n, w=D):
                return a[:, bass.ds(at, n)].unsqueeze(2).to_broadcast([P, n, w])

            def stats(rows, n, lo=0):
                me.wait()
                for j in range(n):
                    last = dve.bn_stats(out=st[:, j, :], in_=rows[:, j, 0:D])
                me.mark(last)
                me.wait()
                even, odd = st[:, 0:n, 1], st[:, 0:n, 4]
                me.mark(dve.tensor_tensor(small[:, 0, 0:n], even, odd, ALU.subtract))
                me.mark(dve.tensor_tensor(small[:, 5, lo:lo + n], even, odd, ALU.add))
                me.mark(dve.tensor_tensor(small[:, 1, 0:n], st[:, 0:n, 2], st[:, 0:n, 5], ALU.add))
                me.wait()
                me.mark(dve.tensor_tensor(small[:, 2, 0:n], small[:, 0, 0:n], small[:, 0, 0:n], ALU.mult))
                me.wait()
                me.mark(dve.scalar_tensor_tensor(out=small[:, 3, 0:n], in0=small[:, 2, 0:n], scalar=D / 4.0,
                                                 in1=small[:, 1, 0:n], op0=ALU.mult, op1=ALU.add))
                me.wait()
                return dve.tensor_scalar(arg[:, lo:lo + n], small[:, 3, 0:n], 1.0 / D, EPS, ALU.mult, ALU.add)

            def refine(n, signal, value):
                dve.wait_ge(signal, value)
                me.wait()
                me.mark(dve.tensor_tensor(small[:, 0, 0:n], guess[:, 0:n], guess[:, 0:n], ALU.mult))
                me.wait()
                me.mark(dve.scalar_tensor_tensor(out=small[:, 1, 0:n], in0=small[:, 0, 0:n], scalar=-0.5,
                                                 in1=arg[:, 0:n], op0=ALU.mult, op1=ALU.mult))
                me.wait()
                me.mark(dve.scalar_tensor_tensor(out=rs[:, 0:n], in0=small[:, 1, 0:n], scalar=1.5,
                                                 in1=guess[:, 0:n], op0=ALU.add, op1=ALU.mult))
                me.wait()

            me.mark(dve.memset(ones[:, :], 1.0))
            for k in range(3):
                me.mark(dve.memset(XT[k][D:D + 1, :], 1.0))
            for k in range(RING):
                me.mark(dve.memset(V[k][:, :, D:D + 1], 1.0))
                me.mark(dve.memset(XD[k][:, :, :], 0.0))
                me.mark(dve.memset(XE[k][:, :, :], 0.0))
            for k in range(2):
                me.mark(dve.memset(AG[k][:, :, :], 0.0))
            me.mark(dve.memset(xnext[:, :], 0.0))
            dve.wait_ge(loaded, 16 * 15)
            dve.wait_ge(consts_ready, 1)
            me.mark(dve.tensor_copy(dst_f[:, :], dst_i[:, :]))
            me.wait()
            d, d0, dn = dst_f[:, 0:COLS], dst_f[:, 0:1], dst_f[:, COLS:TC]
            me.mark(dve.memset(keep_fwd[:, 0:1], 0.0))
            me.mark(dve.memset(keep_rev[:, COLS - 1:COLS], 0.0))
            me.mark(dve.tensor_tensor(keep_fwd[:, 1:COLS], dst_f[:, 1:COLS], dst_f[:, 0:COLS - 1], ALU.is_equal))
            me.mark(dve.tensor_tensor(keep_rev[:, 0:COLS - 1], dst_f[:, 0:COLS - 1], dst_f[:, 1:COLS], ALU.is_equal))
            me.mark(dve.tensor_scalar(head[:, :], d, d0, None, ALU.is_equal))
            me.mark(dve.tensor_scalar(tail[:, :], d, dst_f[:, COLS - 1:COLS], None, ALU.is_equal))
            me.mark(dve.tensor_scalar(MB[0][:, 0, :], ident[:, :], d0, None, ALU.mult))
            me.mark(dve.tensor_tensor(tmp_a[:, 0:COLS], d, dst_f[:, 1:TC], ALU.not_equal))
            me.mark(dve.tensor_scalar(tmp_b[:, 0:COLS], d, d0, None, ALU.not_equal))
            me.wait()
            me.mark(dve.tensor_tensor(own[:, :], tmp_a[:, 0:COLS], tmp_b[:, 0:COLS], ALU.mult))
            me.wait()
            me.mark(dve.tensor_tensor(pull[:, :], tmp_b[:, 0:COLS], own[:, :], ALU.subtract))
            me.wait()
            me.mark(dve.tensor_scalar(tmp_b[:, 0:COLS], d, float(-BIG), None, ALU.add))
            me.wait()
            me.mark(dve.tensor_tensor(tmp_a[:, 0:COLS], tmp_b[:, 0:COLS], own[:, :], ALU.mult))
            me.mark(dve.tensor_tensor(small[:, 0, 0:1], d0, dn, ALU.not_equal))
            me.wait()
            me.mark(dve.tensor_tensor(tmp_a[:, COLS:TC], tmp_b[:, 0:1], small[:, 0, 0:1], ALU.mult))
            me.wait()
            me.mark(dve.tensor_scalar(rep_i[:, :], tmp_a[:, :], float(BIG), None, ALU.add))
            me.wait()
            me.mark(dve.tensor_scalar(small[:, 1, 0:COLS], d, dn, None, ALU.not_equal))
            me.mark(dve.tensor_scalar(small[:, 2, 0:COLS], keep_fwd[:, :], -1.0, 1.0, ALU.mult, ALU.add))
            me.wait()
            me.mark(dve.tensor_tensor(small[:, 3, 0:COLS], small[:, 1, 0:COLS], small[:, 2, 0:COLS], ALU.mult))
            me.wait()
            me.mark(dve.tensor_tensor(tmp_a[:, 0:COLS], tmp_b[:, 0:COLS], small[:, 3, 0:COLS], ALU.mult))
            me.wait()
            me.mark(dve.memset(tmp_a[:, 0:1], 0.0))
            me.wait()
            me.mark(dve.tensor_scalar(out_i[:, :], tmp_a[:, :], float(BIG), None, ALU.add))
            me.wait()
            me.send(dve.tensor_copy(small[:, 4, 0:1], d0), edges_ready, 1)
            dve.wait_ge(firsts_done, 1)
            me.mark(dve.tensor_scalar(eq_head[:, :], psS[:, 0:P], d0, None, ALU.is_equal))
            me.mark(dve.tensor_scalar(MB[1][:, 0, :], psS[:, 0:P], dst_f[:, COLS - 1:COLS], None, ALU.is_equal))
            me.mark(dve.tensor_tensor(small[:, 6, 0:1], dst_f[:, COLS - 1:COLS], d0, ALU.not_equal))
            me.wait()
            me.mark(dve.tensor_scalar(eq_tail[:, :], MB[1][:, 0, :], small[:, 6, 0:1], None, ALU.mult))
            me.mark(dve.memset(small[:, 0, :], 1.0))
            me.mark(dve.memset(deg[:, COLS:TC], 1.0))
            me.wait()
            me.mark(dve.tensor_tensor_scan(deg[:, 0:COLS], keep_fwd[:, :], small[:, 0, 0:COLS], 0.0,
                                           ALU.mult, ALU.add))

            def degree_values(at, n):
                me.mark(dve.reciprocal(rdeg[:, at:at + n], deg[:, at:at + n]))
                me.mark(dve.tensor_copy(dinv[:, at:at + n], rs[:, 0:n]))
                me.mark(dve.tensor_tensor(dinv2[:, at:at + n], rs[:, 0:n], rs[:, 0:n], ALU.mult))
                me.mark(dve.tensor_tensor(sdeg[:, at:at + n], rs[:, 0:n], arg[:, 0:n], ALU.mult))
                me.wait()

            me.wait()
            me.send(dve.tensor_scalar(arg[:, 0:COLS], deg[:, 0:COLS], 1.0, None, ALU.add), arg_ready, 1)
            refine(COLS, root_ready, 1)
            degree_values(0, COLS)
            me.mark(dve.tensor_tensor(w1c[0:D, :], w1[0:D, :], ident[0:D, 0:D], ALU.add))
            me.mark(dve.tensor_copy(w1c[D:D + 1, :], w1[D:D + 1, :]))
            me.wait()
            me.mark(dve.tensor_reduce(wsum[0:D + 1, :], w1c[0:D + 1, :], AX, ALU.add))
            me.wait()
            me.mark(dve.tensor_scalar(small[0:D + 1, 7, 0:1], wsum[0:D + 1, :], 1.0 / D, None, ALU.mult))
            me.wait()
            me.send(dve.tensor_scalar(w1c[0:D + 1, :], w1c[0:D + 1, :], small[0:D + 1, 7, 0:1], None,
                              ALU.subtract), prep_done, 1)

            def dense_front(c, n=DC):
                used(dve, d_loaded, c)
                me.send(stats(DX[c.slot], n), d_arg, c.n + 1)
                refine(n, d_root, c.n + 1)
                me.send(dve.scalar_tensor_tensor(out=small[:, 6, 0:n], in0=small[:, 5, 0:n], scalar=-0.5, in1=rs[:, 0:n],
                                         op0=ALU.mult, op1=ALU.mult), d_mean, c.n + 1)

            def dense_back(c, n=DC):
                g = (n + C - 1) // C
                done(dve, d_sq, c)
                sq = DSQ[c.slot][:, :, :].rearrange("p g (m d) -> p (g m) d", d=D)[:, 0:n, :]
                me.mark(dve.tensor_reduce(small[:, 7, 0:n], sq, AX, ALU.add))
                me.wait()
                me.send(dve.tensor_scalar(arg[:, 0:n], small[:, 7, 0:n], (1 + EPS / 2) ** 2 / D, EPS ** 3 / 4,
                                  ALU.mult, ALU.add), y_arg, c.n + 1)
                refine(n, y_root, c.n + 1)
                used(dve, d_stored, c.before(2))
                for k in range(g):
                    m = min(C, n - k * C)
                    last = dve.tensor_tensor(DO[c.slot][:, k * C:k * C + m, :],
                                             dY[c.slot][k][:, 0:m * D].rearrange("p (m d) -> p m d", d=D),
                                             wide(rs, k * C, m), ALU.mult)
                me.send(last, d_out, c.n + 1)

            def dense(c):
                dense_front(c)
                if c.before(1).exists:
                    dense_back(c.before(1))

            each_chunk(dve, DCHUNKS, 2, dense, [me])
            last = Chunk(DCHUNKS, 2, DCHUNKS % 2, DCHUNKS // 2 + 1)
            dense_front(last, 2)
            dense_back(last.before(1))
            dense_back(last, 2)

            for r in ROUNDS:
                s = S[r]
                w = {0: D + 1, 1: 2 * D, 2: D, 3: D, 4: W4}[r]

                def running(c, values, signal=None):
                    keep = keep_fwd if r < 4 else keep_rev
                    b = c.parity
                    order = list(range(C)) if r < 4 else list(reversed(range(C)))
                    for j in order:
                        if r < 4:
                            prev = AG[b][:, j - 1, 0:w] if j else AG[1 - b][:, C - 1, 0:w]
                        else:
                            prev = AG[b][:, j + 1, 0:w] if j < C - 1 else AG[1 - b][:, 0, 0:w]
                        me.wait()
                        summed = dve.scalar_tensor_tensor(out=AG[b][:, j, 0:w], in0=prev,
                                                          scalar=keep[:, bass.ds(cols(r, c) + j, 1)],
                                                          in1=values[:, j, 0:w], op0=ALU.mult, op1=ALU.add)
                        if signal and j == order[-1]:
                            me.send(summed, signal, c.n + 1)
                        else:
                            me.mark(summed)

                def dst_input(c, ag):
                    b, n, at = c.parity, width(c), cols(r, c)
                    done(dve, s.am_turned, c.before(2))
                    me.wait()
                    if r == 0:
                        me.send(dve.tensor_tensor(AM[b][:, 0:n, :], ag[:, 0:n, 0:D], wide(rdeg, at, n), ALU.mult), s.am_ready, c.n + 1)
                    else:
                        used(dve, s.xd_loaded, c)
                        me.mark(dve.reciprocal(UB[:, 0:n, :], ag[:, 0:n, D:2 * D]))
                        me.wait()
                        me.mark(dve.tensor_tensor(U2[:, 0:n, :], ag[:, 0:n, 0:D], UB[:, 0:n, :], ALU.mult))
                        me.wait()
                        me.send(dve.tensor_tensor(AM[b][:, 0:n, :], U2[:, 0:n, :], XD[c.slot][:, 0:n, :], ALU.add), s.am_ready, c.n + 1)

                def hop(c, ag):
                    n, at = width(c), cols(r, c)
                    used(dve, s.xd_loaded, c, 16 if r == 2 else 32)
                    me.wait()
                    me.mark(dve.tensor_tensor(U2[:, 0:n, :], ag[:, 0:n, 0:D], XD[c.slot][:, 0:n, :], ALU.add))
                    me.wait()
                    if r == 2:
                        if c.before(RING).exists:
                            used(dve, s.stored, c.before(RING))
                        me.send(dve.tensor_tensor(OT[c.slot][:, 0:n, :], U2[:, 0:n, :], wide(dinv2, at, n), ALU.mult), s.updated, c.n + 1)
                    else:
                        me.mark(dve.tensor_tensor(MM[c.parity][:, 0:n, :], U2[:, 0:n, :], wide(dinv, at, n), ALU.mult))
                        me.mark(dve.tensor_tensor(AM[c.parity][:, 0:n, :], XE[c.slot][:, 0:n, :], wide(sdeg, at, n), ALU.mult))
                        me.wait()
                        me.mark(dve.tensor_tensor(UB[:, 0:n, :], AM[c.parity][:, 0:n, :], MM[c.parity][:, 0:n, :], ALU.add))
                        me.send(stats(UB, n), s.arg, c.n + 1)

                def normalise(c, n, rows, lo, scale=None):
                    if c.before(RING).exists:
                        used(dve, s.scattered if r == 4 else s.stored, c.before(RING), 16 * C if r == 4 else 16)
                    me.mark(dve.tensor_scalar(small[:, 6, 0:n], small[:, 5, lo:lo + n], 0.5, None, ALU.mult))
                    if scale is not None:
                        me.mark(dve.tensor_tensor(rs2[:, lo:lo + n], rs[:, lo:lo + n], scale, ALU.mult))
                    me.wait()
                    by = rs if scale is None else rs2
                    for j in range(n):
                        last = dve.tensor_scalar(OT[c.slot][:, j, :], rows[:, j, :], small[:, 6, j:j + 1],
                                                 by[:, lo + j:lo + j + 1], ALU.subtract, ALU.mult)
                    me.send(last, s.updated, c.n + 1)

                def front(c):
                    b = c.parity
                    if r == 0:
                        used(dve, s.gathered, c, 2 * 16 * C)
                        me.send(stats(V[c.slot], C), s.x1_arg, c.n + 1)
                        running(c, V[c.slot])
                        dst_input(c, AG[b])
                        refine(C, s.x1_root, c.n + 1)
                        me.mark(dve.tensor_scalar(small[:, 6, 0:C], small[:, 5, 0:C], 0.5, None, ALU.mult))
                        me.wait()
                        used_parity(c)
                        done(dve, s.x1_turned, c.before(2))
                        for j in range(C):
                            last = dve.tensor_scalar(PL1[b][:, j, :], V[c.slot][:, j, 0:D], small[:, 6, j:j + 1],
                                                     rs[:, j:j + 1], ALU.subtract, ALU.mult)
                        me.send(last, s.front, c.n + 1)
                    if r == 1:
                        done(dve, s.exp_ready, c)
                        me.send(dve.scalar_tensor_tensor(out=MS[b][:, :, 0:D], in0=MM[b][:, :, :], scalar=1e-7,
                                                 in1=MS[b][:, :, D:2 * D], op0=ALU.add, op1=ALU.mult), s.msg_ready, c.n + 1)
                        done(dve, s.msg_ready, c)
                        running(c, MS[b])
                        dst_input(c, AG[b])
                    if r in (2, 3):
                        used(dve, s.gathered, c, 16 * C)
                        running(c, V[c.slot], s.front)
                        if r == 2:
                            hop(c, AG[b])
                    if r == 4:
                        used(dve, s.xd_loaded, c, 32)
                        done(dve, s.scaled, c)
                        done(dve, s.turned, c.before(2), 3)
                        for j in range(C):
                            me.mark(dve.scalar_tensor_tensor(out=XA[b][:, j, :], in0=xseam[:, :],
                                                             scalar=head[:, bass.ds(cols(r, c) + j, 1)],
                                                             in1=XA[b][:, j, :], op0=ALU.mult, op1=ALU.add))
                        for j in reversed(range(C)):
                            prev = XB[b][:, j + 1, :] if j < C - 1 else XB[1 - b][:, 0, :]
                            me.wait()
                            row = dve.scalar_tensor_tensor(out=XB[b][:, j, :], in0=prev,
                                                           scalar=pull[:, bass.ds(cols(r, c) + j, 1)],
                                                           in1=XA[b][:, j, :], op0=ALU.mult, op1=ALU.add)
                            if j:
                                me.mark(row)
                            else:
                                me.send(row, s.xb_ready, c.n + 1)

                def used_parity(c):
                    old = c.before(2)
                    if old.exists:
                        turn = old.n // 2 + 1 if isinstance(old.n, int) else (c.turn - 1) * 2 + (c.slot - 2) // 2 + 1
                        dve.wait_ge(s.plain_stored[old.parity], turn * 48)

                def back(c, sums=None):
                    b, n, at = c.parity, width(c), cols(r, c)
                    seam = c is SEAM
                    me.wait()
                    if r in (0, 1):
                        if r == 0 and not seam:
                            done(dve, s.squared, c)
                            me.mark(dve.tensor_reduce(small[:, 7, 0:n], SQ[b][:, :, :], AX, ALU.add))
                        done(dve, s.am_mult, c)
                        if seam and r == 0:
                            dve.wait_ge(s.gathered[c.slot][0], (c.turn - 1) * 2 * 16 * C + 16)
                        me.mark(dve.tensor_tensor(UB[:, 0:n, :], psU[b][:, 0:n * D].rearrange("p (m d) -> p m d", d=D),
                                                  XD[c.slot][:, 0:n, :], ALU.add))
                        lo = 2 * C if r == 0 and not seam else 0
                        if r == 0 and not seam:
                            me.wait()
                            me.mark(dve.tensor_scalar(arg[:, 0:C], small[:, 7, 0:C], 1.0 / D, EPS, ALU.mult, ALU.add))
                            me.mark(dve.tensor_scalar(arg[:, C:2 * C], small[:, 7, 0:C], (1 + EPS / 4) / D, EPS * EPS / 4,
                                              ALU.mult, ALU.add))
                        me.send(stats(UB, n, lo), s.arg, c.n + 1)
                        refine(lo + n, s.root, c.n + 1)
                        if r == 0 and not seam:
                            y = psY[b][:, 0:C * D].rearrange("p (m d) -> p m d", d=D)
                            me.mark(dve.tensor_tensor(PL2[b][:, :, :], y, wide(rs, 0, C), ALU.mult))
                            me.mark(dve.tensor_tensor(PL4[b][:, :, :], y, wide(rs, C, C), ALU.mult))
                        normalise(c, n, UB, lo, dinv[:, bass.ds(at, n)] if r == 1 else None)
                    if r == 3:
                        if not seam:
                            hop(c, AG[b])
                        refine(n, s.root, c.n + 1)
                        normalise(c, n, UB, 0)
                    if r == 4:
                        if not seam:
                            done(dve, s.q_ready, c)
                            t, k4 = UB, QS
                            for h in range(2):
                                kk = psK[h][:, 0:4 * D].rearrange("p (m w) -> p m w", w=2 * D)[:, :, 0:D]
                                last = dve.tensor_tensor(t[:, 2 * h:2 * h + 2, :], kk, k4[:, 2 * h:2 * h + 2, :], ALU.mult)
                            me.mark(last)
                            me.wait()
                            me.mark(dve.tensor_tensor(U2[:, :, :], psE[:, 0:C * D].rearrange("p (m d) -> p m d", d=D),
                                                      t[:, :, :], ALU.mult))
                            me.wait()
                            me.mark(dve.tensor_reduce(SC[:, :, :].rearrange("p m h -> p (m h)"),
                                                      U2[:, :, :].rearrange("p m (h e) -> p (m h) e", e=HD), AX, ALU.add))
                            me.wait()
                            me.mark(dve.tensor_scalar(SC[:, :, :], SC[:, :, :], float(HD) ** -0.5, 5.0, ALU.mult, ALU.min))
                            me.wait()
                            done(dve, s.seam_added, c.before(2))
                            me.send(dve.tensor_scalar(SC2[:, :, :], SC[:, :, :], -5.0, None, ALU.max), s.score_ready, c.n + 1)
                            done(dve, s.exp_ready, c)
                            for j in range(C):
                                vv = psK[j // 2][:, j % 2 * 2 * D + D:(j % 2 + 1) * 2 * D]
                                last = dve.tensor_tensor(
                                    MS[b][:, j, 0:D].rearrange("p (h e) -> p h e", e=HD),
                                    vv.rearrange("p (h e) -> p h e", e=HD),
                                    MS[b][:, j, D:W4].unsqueeze(2).to_broadcast([P, HEADS, HD]), ALU.mult)
                            me.send(last, s.msg_ready, c.n + 1)
                            done(dve, s.msg_ready, c)
                            running(c, MS[b])
                            sums = AG[b]
                        me.wait()
                        me.mark(dve.tensor_scalar(SC[:, 0:n, :], sums[:, 0:n, D:W4], 1e-6, None, ALU.add))
                        me.wait()
                        me.mark(dve.reciprocal(ZR[:, 0:n, :], SC[:, 0:n, :]))
                        me.wait()
                        for j in range(n):
                            last = dve.tensor_tensor(
                                U2[:, j, :].rearrange("p (h e) -> p h e", e=HD),
                                sums[:, j, 0:D].rearrange("p (h e) -> p h e", e=HD),
                                ZR[:, j, :].unsqueeze(2).to_broadcast([P, HEADS, HD]), ALU.mult)
                        me.mark(last)
                        me.wait()
                        xb = xseam[:, :].unsqueeze(1) if seam else XB[b][:, :, :]
                        me.mark(dve.tensor_tensor(UB[:, 0:n, :], U2[:, 0:n, :], xb, ALU.add))
                        me.send(stats(UB, n), s.arg, c.n + 1)
                        refine(n, s.root, c.n + 1)
                        normalise(c, n, UB, 0)

                def step(c):
                    front(c)
                    if r != 2 and c.before(1).exists:
                        back(c.before(1))

                if r == 4:
                    dve.wait_ge(s.seam_loaded, 32)
                    me.mark(dve.tensor_copy(XB[1][:, 0, :], xnext[:, :]))
                each_chunk(dve, CHUNKS, RING, step, [me])
                if r != 2:
                    back(SEAM.before(1))

                dve.wait_ge(s.seam_total, 1)
                me.mark(dve.tensor_copy(SG[:, 0, 0:w], psS[:, 0:w]))
                me.wait()
                if r == 0:
                    me.mark(dve.tensor_copy(deg[:, COLS:TC], SG[:, 0, D:D + 1]))
                    me.wait()
                    me.send(dve.tensor_scalar(arg[:, 0:1], SG[:, 0, D:D + 1], 1.0, None, ALU.add), s.deg_arg, 1)
                    refine(1, s.deg_root, 1)
                    degree_values(COLS, 1)
                if r in (0, 1):
                    dst_input(SEAM, SG)
                if r in (2, 3):
                    hop(SEAM, SG)
                if r in (0, 1, 3, 4):
                    back(SEAM, SG)


_INS = ["x", "src", "dst", "edge_attr_96", "L0_gnn_W", "L0_gnn_b", "L1_gnn_W", "L1_gnn_b", "L3_gnn_Wq", "L3_gnn_bq",
        "L3_gnn_Wk", "L3_gnn_bk", "L3_gnn_We", "L3_gnn_be", "L3_gnn_Wv", "L3_gnn_bv"]


def kernel(**inputs):
    import numpy as _np
    import concourse.bacc as _bacc
    from concourse import mybir as _mybir
    from concourse.bass_utils import run_bass_kernel_spmd as _run

    nc = _bacc.Bacc("TRN2", target_bir_lowering=False, num_devices=1)
    arrays, args = {}, []
    for name in _INS:
        a = _np.ascontiguousarray(inputs[name])
        arrays[f"in_{name}"] = a
        args.append(nc.dram_tensor(f"in_{name}", a.shape, _mybir.dt.from_np(a.dtype), kind="ExternalInput").ap())
    result = nc.dram_tensor("out_dram", (N, D), _mybir.dt.float32, kind="ExternalOutput").ap()
    build(nc, *args, result)
    r = _run(nc, [arrays], core_ids=[0])
    return r.results[0]["out_dram"]
```

```python
from contextlib import ExitStack

import concourse.bass as bass
from concourse import mybir

F32 = mybir.dt.float32
I32 = mybir.dt.int32
ALU = mybir.AluOpType
ACT = mybir.ActivationFunctionType
AX = mybir.AxisListType.X

P = 128
N, D, E = 100000, 96, 25000
COLS = 200
EP = E // COLS
TC = COLS + 1
C = 8
G = 4
CHUNKS = COLS // C
RING = 4
HEADS, HD = 8, D // 8
W4 = D + HEADS
EPS = 1e-5
BIG = 1 << 20
DC = 30
DG = -(-DC // G)
DCOLS = N // P // DC * DC
DCHUNKS = DCOLS // DC
DREST = N - P * DCOLS
DRP = DREST // 2
assert EP * COLS == E and DRP * 2 == DREST and DRP <= P
ROUNDS = range(5)


class Chunk:

    def __init__(self, n, ring, slot, turn):
        self.n, self.ring, self.slot, self.turn = n, ring, slot, turn

    def before(self, k=1):
        slot = (self.slot - k) % self.ring
        return Chunk(self.n - k, self.ring, slot, self.turn - (1 if slot > self.slot or k == self.ring else 0))

    @property
    def exists(self):
        return not isinstance(self.n, int) or self.n >= 0

    @property
    def parity(self):
        return self.slot % 2


def each_chunk(eng, count, ring, step, steps=()):
    before = [s.count for s in steps]
    for n in range(ring):
        if n == ring - 1:
            before = [s.count for s in steps]
        step(Chunk(n, ring, n, 1))
    per = [(s.count - b) * ring for s, b in zip(steps, before)]
    turns = count // ring
    with eng.Fori(1, turns) as i:
        for s, stride in zip(steps, per):
            s.enter(i, stride)
        for slot in range(ring):
            step(Chunk(i * ring + slot, ring, slot, i + 1))
        for s in steps:
            s.leave(turns - 1)
    for n in range(turns * ring, count):
        step(Chunk(n, ring, n % ring, n // ring + 1))


class Steps:

    def __init__(self, eng, sem):
        self.eng, self.sem, self.count, self.offset, self.base, self.stride = eng, sem, 0, None, 0, 0
        self.sent = None

    def enter(self, i, stride):
        self.base, self.stride = self.count, stride
        self.offset = (i - 1) * stride
        self.sent = None

    def leave(self, turns):
        assert self.count - self.base == self.stride, (self.count - self.base, self.stride)
        self.count, self.offset, self.sent = self.base + turns * self.stride, None, None

    def mark(self, instruction):
        instruction.then_inc(self.sem, 1)
        self.count += 1
        self.sent = None

    def send(self, instruction, signal, value):
        instruction.then_inc(signal, 1)
        self.sent = signal, value

    def wait(self):
        if self.sent:
            self.eng.wait_ge(*self.sent)
            return
        value = self.count if self.offset is None else self.offset + self.count
        self.eng.wait_ge(self.sem, value)


def build(nc, x, src, dst, edge_attr, W0, b0, W1, b1, Wq, bq, Wk, bk, We, be, Wv, bv, out):
    with ExitStack() as ctx:
        def sb(name, shape, dt=F32):
            return ctx.enter_context(nc.sbuf_tensor(name, shape, dt))

        def sem(name):
            return ctx.enter_context(nc.semaphore(name))

        def ring_sems(name, n=RING):
            return [sem(f"{name}_{i}") for i in range(n)]

        table = {r: nc.dram_tensor(f"table{r}", (P * TC, D), F32).ap() for r in (1, 2, 3, 4)}
        table_v = {r: t.rearrange("(p t) d -> p t d", t=TC) for r, t in table.items()}
        plain = {r: nc.dram_tensor(f"plain{r}", (P, COLS, D), F32).ap() for r in (1, 2, 4)}
        row_of = nc.dram_tensor("row_of", (N, 1), I32).ap()

        ident = sb("ident", [P, P])
        ones = sb("ones", [P, P])
        w0 = sb("w0", [P, D])
        w1 = sb("w1", [P, D])
        w1c = sb("w1c", [P, D])
        wkv = sb("wkv", [P, 2 * D])
        wq = sb("wq", [P, D])
        we = sb("we", [P, D])
        wsum = sb("wsum", [P, 1])

        src_i = sb("src_i", [P, COLS], I32)
        dst_i = sb("dst_i", [P, TC], I32)
        dst_f = sb("dst_f", [P, TC])
        keep_fwd = sb("keep_fwd", [P, COLS])
        keep_rev = sb("keep_rev", [P, COLS])
        head = sb("head", [P, COLS])
        tail = sb("tail", [P, COLS])
        own = sb("own", [P, COLS])
        pull = sb("pull", [P, COLS])
        tmp_a = sb("tmp_a", [P, TC])
        tmp_b = sb("tmp_b", [P, TC])
        rep_i = sb("rep_i", [P, TC], I32)
        out_i = sb("out_i", [P, TC], I32)
        rowid = sb("rowid", [P, TC], I32)
        src_row = sb("src_row", [P, COLS], I32)
        eq_head = sb("eq_head", [P, P])
        eq_tail = sb("eq_tail", [P, P])
        deg = sb("deg", [P, TC])
        rdeg = sb("rdeg", [P, TC])
        dinv = sb("dinv", [P, TC])
        dinv2 = sb("dinv2", [P, TC])
        sdeg = sb("sdeg", [P, TC])
        bigs = sb("bigs", [P, N // EP], I32)

        V = [sb(f"V{k}", [P, C, D + 1]) for k in range(RING)]
        XD = [sb(f"XD{k}", [P, C, D]) for k in range(RING)]
        XE = [sb(f"XE{k}", [P, C, D]) for k in range(RING)]
        OT = [sb(f"OT{k}", [P, C, D]) for k in range(RING)]
        idx = [sb(f"idx{k}", [P, C], I32) for k in range(RING)]
        idx2 = [sb(f"idx2{k}", [P, C], I32) for k in range(RING)]
        rid = [sb(f"rid{k}", [P, C], I32) for k in range(RING)]
        rst = [sb(f"rst{k}", [P, C], I32) for k in range(RING)]
        DX = [sb(f"DX{k}", [P, DC, D]) for k in range(2)]

        space = sb("space", [P, 19200])
        place = [0]

        def carve(rows, width, again=False):
            if again:
                place[0] = 0
            at = place[0]
            place[0] += rows * width
            assert place[0] <= space.shape[1], place
            return space[:, at:at + rows * width].rearrange("p (t d) -> p t d", d=width)

        DY = [carve(DC, D, again=k == 0) for k in range(2)]
        DO = [carve(DC, D) for k in range(2)]
        DSQ = carve(DC, D)
        AG = [carve(C, 2 * D, again=k == 0) for k in range(2)]
        MS = [carve(C, 2 * D) for k in range(2)]
        MM = [carve(C, D) for k in range(2)]
        AM = [carve(C, D) for k in range(2)]
        PL1 = [MS[k][:, :, 0:D] for k in range(2)]
        PL2 = [MS[k][:, :, D:2 * D] for k in range(2)]
        PL4 = [carve(C, D) for k in range(2)]
        UB = [carve(C, D) for k in range(2)]
        U2 = carve(C, D)
        U3 = carve(C, D)
        SQ = carve(C, D)
        MB = [carve(C, P) for k in range(2)]
        SC = carve(C, HEADS)
        SC2 = carve(C, HEADS)
        ZR = carve(C, HEADS)
        SG = carve(1, 2 * D)
        XA, XB = AM, [carve(C, D) for k in range(2)]
        QS, VS = MM, PL4
        XT = [sb(f"XT{k}", [P, G * P]) for k in range(6)]
        xseam = sb("xseam", [P, D])
        xnext = sb("xnext", [P, D])
        b1c = sb("b1c", [P, D])
        w1x = sb("w1x", [P, D])
        centre = sb("centre", [P, D])

        class Small:

            def __init__(self, name, n):
                self.st = sb(f"{name}_st", [P, DC, 6])
                self.t = sb(f"{name}_t", [P, 6, n])
                self.mean, self.shift = sb(f"{name}_mean", [P, n]), sb(f"{name}_shift", [P, n])
                self.arg, self.ln = sb(f"{name}_arg", [P, n]), sb(f"{name}_ln", [P, n])
                self.guess, self.root = sb(f"{name}_guess", [P, n]), sb(f"{name}_root", [P, n])
                self.by = sb(f"{name}_by", [P, n])

        first, second = Small("first", TC), Small("second", 32)

        bank = [ctx.enter_context(nc.psum_tensor(f"bank{i}", [P, 512], F32)) for i in range(8)]
        psT = [bank[0], bank[1]]
        psS = bank[2]
        psU = [bank[3], bank[4]]
        psY = [bank[5], bank[6]]
        psK, psE, psQV = [bank[3], bank[4]], [bank[5], bank[6]], bank[7]
        dY = [bank[2], bank[3], bank[4], bank[5]]

        dve_step, act_step, pool_step = sem("dve_step"), sem("act_step"), sem("pool_step")
        passed = {nc.sync.engine: sem("sp_passed"), nc.gpsimd.engine: sem("pool_passed")}
        loaded = sem("loaded")
        bigs_ready, bigs_stored = sem("bigs_ready"), sem("bigs_stored")
        consts_ready = sem("consts_ready")
        tiles_set = sem("tiles_set")
        edges_ready = sem("edges_ready")
        firsts_done = sem("firsts_done")
        prep_done = sem("prep_done")
        arg_ready, root_ready = sem("arg_ready"), sem("root_ready")
        centre_ready, w1c_ready, w1x_done = sem("centre_ready"), sem("w1c_ready"), sem("w1x_done")
        row_entered = ring_sems("row_entered")
        row_found = ring_sems("row_found")
        d_loaded, d_stored = ring_sems("d_loaded", 2), ring_sems("d_stored", 2)
        d_arg, d_root = sem("d_arg"), sem("d_root")
        y_arg, y_root = sem("y_arg"), sem("y_root")
        d_turned, d_evac, d_mult, d_read = sem("d_turned"), sem("d_evac"), sem("d_mult"), sem("d_read")
        d_sq, d_scale, d_out = sem("d_sq"), sem("d_scale"), sem("d_out")
        v_loaded, xd_loaded = ring_sems("v_loaded"), ring_sems("xd_loaded")
        gathered, stored = ring_sems("gathered"), ring_sems("stored")

        class Round:

            def __init__(self, r):
                def s(name):
                    return sem(f"{name}{r}")
                turns = [len(range(k, CHUNKS, RING)) for k in range(RING)]
                seam = [int(k == CHUNKS % RING) for k in range(RING)]

                def ongoing(sems, per, seams):
                    return [(sems[k], sum(per[q] * turns[k] + seams[q] * seam[k] for q in range(r)))
                            for k in range(RING)]
                self.v_loaded = ongoing(v_loaded, [0, 16, 16, 16, 16], [0] * 5)
                self.xd_loaded = ongoing(xd_loaded, [0, 16, 16, 32, 32], [0, 16, 16, 32, 0])
                self.gathered = ongoing(gathered, [2 * 16 * C] + [16 * C] * 4, [16, 0, 0, 0, 0])
                self.stored = ongoing(stored, [16] * 4 + [0], [16] * 4 + [0])
                self.mask_ready = s("mask_ready")
                self.front = s("front")
                self.seam_added = s("seam_added")
                self.seam_total = s("seam_total")
                self.updated = s("updated")
                if r in (0, 1, 3, 4):
                    self.arg, self.root = s("arg"), s("root")
                if r in (1, 3, 4):
                    self.norm_ready = s("norm_ready")
                if r in (0, 1, 4):
                    self.turned, self.evac = s("turned"), s("evac")
                    self.groups = {0: 4, 1: 2, 4: 6}[r]
                if r in (0, 1):
                    self.am_ready, self.mult = s("am_ready"), s("mult")
                if r == 0:
                    self.x1_arg, self.x1_root = s("x1_arg"), s("x1_root")
                    self.squared = s("squared")
                    self.plain_stored = ring_sems("plain_stored", 2)
                    self.deg_arg, self.deg_root = s("deg_arg"), s("deg_root")
                if r == 1:
                    self.relu_done, self.exp_ready = s("relu_done"), s("exp_ready")
                    self.msg_ready = s("msg_ready")
                if r == 4:
                    self.scaled, self.xb_ready = s("scaled"), s("xb_ready")
                    self.q_mult, self.ke_mult, self.v_mult = s("q_mult"), s("ke_mult"), s("v_mult")
                    self.q_copied, self.v_copied, self.ke_read = s("q_copied"), s("v_copied"), s("ke_read")
                    self.score_ready, self.exp_ready = s("score_ready"), s("exp_ready")
                    self.msg_ready = s("msg_ready")
                    self.seam_loaded = s("seam_loaded")
                    self.scattered = ring_sems("scattered")

        S = [Round(r) for r in ROUNDS]
        SEAM = Chunk(CHUNKS, RING, CHUNKS % RING, CHUNKS // RING + 1)

        def cols(r, c):
            if c is SEAM:
                return COLS
            return C * c.n if r < 4 else (COLS - C) - C * c.n

        def width(c):
            return 1 if c is SEAM else C

        def stand_alone(eng):
            if eng.engine in passed:
                eng.sem_inc(passed[eng.engine], 1)

        def done(eng, s, c, per=1, more=0):
            if c.exists:
                eng.wait_ge(s, (c.n + 1) * per + more)
                stand_alone(eng)

        def count(eng, s, value):
            if not isinstance(value, int) or value > 0:
                eng.wait_ge(s, value)
                stand_alone(eng)

        def used(eng, s, c, per=16):
            if c.exists:
                signal, base = s[c.slot] if isinstance(s[c.slot], tuple) else (s[c.slot], 0)
                eng.wait_ge(signal, c.turn * per + base)
                stand_alone(eng)

        block = ctx.enter_context(nc.Block())

        @block.sync
        def _(sp):
            sp.wait_ge(tiles_set, 1)
            sp.dma_start(src_i[0:EP, :], src.rearrange("(p t) -> p t", t=COLS)).then_inc(loaded, 16)
            sp.dma_start(dst_i[0:EP, 0:COLS], dst.rearrange("(p t) -> p t", t=COLS)).then_inc(loaded, 16)
            sp.dma_start(dst_i[0:EP - 1, COLS:TC],
                         dst.rearrange("(p t) -> p t", t=COLS)[1:EP, 0:1],
                         allow_slow_non_contiguous=True).then_inc(loaded, 16)
            for tile, lo, w, b in ((w0, 0, W0, b0), (w1, 0, W1, b1), (wkv, 0, Wk, bk), (wkv, D, Wv, bv),
                                   (wq, 0, Wq, bq), (we, 0, We, be)):
                sp.dma_start(tile[0:D, lo:lo + D], w).then_inc(loaded, 16)
                sp.dma_start(tile[D:D + 1, lo:lo + D], b.rearrange("(o d) -> o d", o=1)).then_inc(loaded, 16)
            sp.dma_start(b1c[:, :], b1.rearrange("(o d) -> o d", o=1).to_broadcast([P, D])).then_inc(loaded, 16)
            sp.wait_ge(bigs_ready, 1)
            sp.dma_start(row_of.rearrange("(p t) o -> p (t o)", p=EP), bigs[0:EP, :]).then_inc(bigs_stored, 16)

            xv = x[0:P * DCOLS, :].rearrange("(p t) d -> p t d", t=DCOLS)
            ov = out[0:P * DCOLS, :].rearrange("(p t) d -> p t d", t=DCOLS)

            def dense_store(c):
                done(sp, d_out, c)
                sp.dma_start(ov[:, bass.ds(c.n * DC, DC), :], DO[c.slot]).then_inc(d_stored[c.slot], 16)

            def dense_free(c):
                done(sp, d_arg, c)
                done(sp, d_turned, c, DG)

            def dense(c):
                dense_free(c.before(2))
                sp.dma_start(DX[c.slot][:, :, :], xv[:, bass.ds(c.n * DC, DC), :]).then_inc(d_loaded[c.slot], 16)
                if c.before(2).exists:
                    dense_store(c.before(2))

            each_chunk(sp, DCHUNKS, 2, dense)
            last = Chunk(DCHUNKS, 2, DCHUNKS % 2, DCHUNKS // 2 + 1)
            dense_free(last.before(2))
            sp.dma_start(DX[last.slot][0:DRP, 0:2, :],
                         x[P * DCOLS:N, :].rearrange("(p t) d -> p t d", t=2)).then_inc(d_loaded[last.slot], 16)
            dense_store(last.before(2))
            dense_store(last.before(1))
            done(sp, d_out, last)
            sp.dma_start(out[P * DCOLS:N, :].rearrange("(p t) d -> p t d", t=2),
                         DO[last.slot][0:DRP, 0:2, :]).then_inc(d_stored[last.slot], 16)

            ea = edge_attr.rearrange("(p t) d -> p t d", t=COLS)

            def store(r, c):
                s = S[r]
                at, w = cols(r, c), width(c)
                done(sp, s.updated, c)
                sp.dma_start(table_v[r + 1][:, bass.ds(at, w), :], OT[c.slot][:, 0:w, :]).then_inc(s.stored[c.slot][0], 16)
                if r == 0 and c is not SEAM:
                    for rr, tile in ((1, PL1), (2, PL2), (4, PL4)):
                        sp.dma_start(plain[rr][:, bass.ds(at, C), :],
                                     tile[c.parity]).then_inc(s.plain_stored[c.parity], 16)

            def load(r, c):
                s, old = S[r], c.before(RING)
                at = cols(r, c)
                if c is not SEAM:
                    if r in (2, 3):
                        done(sp, s.front, old)
                        done(sp, s.seam_added, old)
                    if r == 1:
                        done(sp, s.relu_done, old)
                    if r == 4:
                        done(sp, s.turned, old, 6)
                    sp.dma_start(V[c.slot][:, :, 0:D], plain[{1: 1, 2: 2, 3: 2, 4: 4}[r]][:, bass.ds(at, C), :]
                                 ).then_inc(s.v_loaded[c.slot][0], 16)
                if r < 4 or c is not SEAM:
                    if r == 4:
                        done(sp, s.scaled, old)
                    else:
                        done(sp, s.updated, old)
                    w = width(c)
                    sp.dma_start(XD[c.slot][:, 0:w, :], table_v[r][:, bass.ds(at, w), :]
                                 ).then_inc(s.xd_loaded[c.slot][0], 16)
                    if r == 3:
                        sp.dma_start(XE[c.slot][:, 0:w, :], table_v[2][:, bass.ds(at, w), :]
                                     ).then_inc(s.xd_loaded[c.slot][0], 16)
                    if r == 4:
                        sp.dma_start(XE[c.slot][0:EP, :, :], ea[:, bass.ds(at, C), :]
                                     ).then_inc(s.xd_loaded[c.slot][0], 16)

            for r in ROUNDS:
                if r:
                    for k in range(RING):
                        signal, base = S[r - 1].stored[k]
                        sp.wait_ge(signal, base + 16 * len(range(k, CHUNKS + 1, RING)))
                    if r == 1:
                        for k in range(2):
                            sp.wait_ge(S[0].plain_stored[k], 16 * 3 * len(range(k, CHUNKS, 2)))
                if r == 4:
                    seam_rows = table_v[4][:, COLS:TC, :].rearrange("p t d -> p (t d)")
                    sp.dma_start(xseam[:, :], seam_rows).then_inc(S[4].seam_loaded, 16)
                    sp.dma_start(xnext[0:P - 1, :], seam_rows[1:P, :]).then_inc(S[4].seam_loaded, 16)

                def step(c):
                    if r:
                        load(r, c)
                    if r < 4 and c.before(2).exists:
                        store(r, c.before(2))

                each_chunk(sp, CHUNKS, RING, step)
                if r:
                    load(r, SEAM)
                if r < 4:
                    store(r, SEAM.before(2))
                    store(r, SEAM.before(1))
                    store(r, SEAM)
            for k in range(2):
                sp.wait_ge(d_stored[k], 16 * len(range(k, DCHUNKS + 1, 2)))
            for k in range(RING):
                full, seams = len(range(k, CHUNKS, RING)), int(k == SEAM.slot)
                sp.wait_ge(S[4].scattered[k], 16 * (C * full + seams))

        @block.gpsimd
        def _(pool):
            me = Steps(pool, pool_step)
            last_node, last_entry = pool.to_reg(N - 1), pool.to_reg(P * TC - 1)
            me.mark(pool.memset(src_i[:, :], 0))
            me.wait()
            pool.memset(dst_i[:, :], BIG).then_inc(tiles_set, 1)
            pool.wait_ge(tiles_set, 1)
            pool.memset(bigs[:, :], BIG).then_inc(bigs_ready, 1)
            pool.wait_ge(bigs_ready, 1)
            me.mark(pool.memset(ident[:, :], 0.0))
            me.wait()
            me.mark(pool.iota(rowid[:, :], pattern=[[1, TC]], base=0, channel_multiplier=TC))
            me.wait()
            pool.affine_select(out=ident[:, :], in_=ident[:, :], compare_op=ALU.not_equal, fill=1.0, base=0,
                               pattern=[[-1, P]], channel_multiplier=1).then_inc(consts_ready, 1)

            def stage(to, of, at, w):
                me.mark(pool.tensor_copy(to[:, 0:w], of[:, bass.ds(at, w)]))

            pool.wait_ge(edges_ready, 1)
            pool.wait_ge(bigs_stored, 16)

            def enter_rows(c):
                at, w = cols(0, c), width(c)
                used(pool, row_entered, c.before(RING), 16 * C)
                stage(idx[c.slot], rep_i, at, w)
                stage(rid[c.slot], rowid, at, w)
                me.wait()
                stand_alone(pool)
                for j in range(w):
                    pool.indirect_dma_start(
                        out=row_of, out_offset=bass.IndirectOffsetOnAxis(ap=idx[c.slot][:, j:j + 1], axis=0),
                        in_=rid[c.slot][:, j:j + 1], in_offset=None, bounds_check=last_node,
                        oob_is_err=False).then_inc(row_entered[c.slot], 16)

            each_chunk(pool, CHUNKS, RING, enter_rows, [me])
            enter_rows(SEAM)
            for k in range(RING):
                pool.wait_ge(row_entered[k], 16 * (C * len(range(k, CHUNKS, RING)) + int(k == SEAM.slot)))

            def keep_rows(c):
                used(pool, row_found, c, 16 * C)
                me.mark(pool.tensor_copy(src_row[:, bass.ds(cols(0, c), C)], rst[c.slot][:, :]))

            def find_rows(c):
                stage(idx[c.slot], src_i, cols(0, c), C)
                me.wait()
                stand_alone(pool)
                for j in range(C):
                    pool.indirect_dma_start(
                        out=rst[c.slot][:, j:j + 1], out_offset=None, in_=row_of,
                        in_offset=bass.IndirectOffsetOnAxis(ap=idx[c.slot][:, j:j + 1], axis=0),
                        bounds_check=last_node, oob_is_err=False).then_inc(row_found[c.slot], 16)
                if c.before(1).exists:
                    keep_rows(c.before(1))

            each_chunk(pool, CHUNKS, RING, find_rows, [me])
            keep_rows(SEAM.before(1))

            def gather(c, w, to, indices, at, of, last_row, ix, signal):
                stage(ix[c.slot], indices, at, w)
                me.wait()
                stand_alone(pool)
                for j in range(w):
                    pool.indirect_dma_start(
                        out=to[c.slot][:, j, 0:D], out_offset=None, in_=of,
                        in_offset=bass.IndirectOffsetOnAxis(ap=ix[c.slot][:, j:j + 1], axis=0),
                        bounds_check=last_row, oob_is_err=False).then_inc(signal[c.slot][0], 16)

            def gather_x(c):
                s, old = S[0], c.before(RING)
                done(pool, s.front, old)
                done(pool, s.seam_added, old)
                gather(c, C, V, src_i, cols(0, c), x, last_node, idx, s.gathered)
                done(pool, s.updated, old)
                gather(c, C, XD, dst_i, cols(0, c), x, last_node, idx2, s.gathered)

            each_chunk(pool, CHUNKS, RING, gather_x, [me])
            done(pool, S[0].updated, SEAM.before(RING))
            gather(SEAM, 1, XD, dst_i, 0, x, last_node, idx2, S[0].gathered)

            def scatter(c):
                s, at, w = S[4], cols(4, c), width(c)
                done(pool, s.updated, c)
                used(pool, s.scattered, c.before(RING), 16 * C)
                stage(idx2[c.slot], out_i, at, w)
                me.wait()
                stand_alone(pool)
                for j in range(w):
                    pool.indirect_dma_start(
                        out=out, out_offset=bass.IndirectOffsetOnAxis(ap=idx2[c.slot][:, j:j + 1], axis=0),
                        in_=OT[c.slot][:, j, :], in_offset=None, bounds_check=last_node,
                        oob_is_err=False).then_inc(s.scattered[c.slot], 16)

            for r in range(1, 5):
                for k in range(RING):
                    signal, base = S[r - 1].stored[k]
                    pool.wait_ge(signal, base + 16 * len(range(k, CHUNKS + 1, RING)))
                if r == 4:
                    for k in range(2):
                        pool.wait_ge(d_stored[k], 16 * len(range(k, DCHUNKS + 1, 2)))

                def step(c):
                    used(pool, S[r].v_loaded, c)
                    gather(c, C, V, src_row, cols(r, c), table[r], last_entry, idx, S[r].gathered)
                    if r == 4 and c.before(3).exists:
                        scatter(c.before(3))

                each_chunk(pool, CHUNKS, RING, step, [me])
            for k in (3, 2, 1):
                scatter(SEAM.before(k))
            scatter(SEAM)

        def groups(n):
            return [(g, g * G, min(G, n - g * G)) for g in range(-(-n // G))]

        def by_rows(psum, m):
            return psum[:, 0:m * D].rearrange("p (m d) -> p m d", d=D)

        @block.tensor
        def _(pe):
            pe.wait_ge(consts_ready, 1)
            pe.wait_ge(edges_ready, 1)
            pe.matmul(psS[:, 0:P], ones[:, :], MB[0][:, 0, :], start=True, stop=True).then_inc(firsts_done, 1)
            pe.wait_ge(w1c_ready, 1)
            pe.matmul(psQV[0:D, 0:D], centre[0:D, :], w1c[0:D, :], start=True, stop=True).then_inc(w1x_done, 1)

            def turn(to, of, n):
                for j in range(n):
                    last = pe.transpose(to[0:D, j * P:(j + 1) * P], of[:, j, :], ident[:, :])
                return last

            def times(to, xt, w, n, k=D + 1):
                for j in range(n):
                    last = pe.matmul(to[:, j * D:(j + 1) * D], xt[0:k, j * P:(j + 1) * P], w[0:k, :],
                                     start=True, stop=True)
                return last

            pe.wait_ge(prep_done, 1)

            def dense(c, n=DC):
                used(pe, d_loaded, c)
                parts = groups(n)
                for g, at, m in parts:
                    i = c.n * DG + g
                    count(pe, d_evac, i - 1)
                    turn(psT[g % 2], DX[c.slot][:, at:at + m, :], m).then_inc(d_turned, 1)
                    if g:
                        multiply(c, *parts[g - 1])
                multiply(c, *parts[-1])

            def multiply(c, g, at, m):
                i = c.n * DG + g
                pe.wait_ge(d_evac, i + 1)
                count(pe, d_read, i - 3)
                times(dY[g % 4], XT[g % 4], w1x, m, D).then_inc(d_mult, 1)

            each_chunk(pe, DCHUNKS, 2, dense)
            dense(Chunk(DCHUNKS, 2, DCHUNKS % 2, DCHUNKS // 2 + 1), 2)

            def seam(r, c, values, w):
                s = S[r]
                done(pe, s.mask_ready, c)
                for j in range(C):
                    first_of_all = isinstance(c.n, int) and c.n == 0 and j == 0
                    last = pe.matmul(psS[:, 0:w], MB[c.parity][:, j, :], values[:, j, 0:w], start=first_of_all, stop=False)
                last.then_inc(s.seam_added, 1)

            for r in ROUNDS:
                s = S[r]
                w = {0: D + 1, 1: 2 * D, 2: D, 3: D, 4: W4}[r]

                def turn_groups(c, q, of, n):
                    for g, at, m in groups(n):
                        count(pe, s.evac, c.n * s.groups + q + g - 1)
                        turn(psT[(q + g) % 2], of[:, at:at + m, 0:D], m).then_inc(s.turned, 1)

                def evacuated(c, q):
                    pe.wait_ge(s.evac, c.n * s.groups + q + 1)

                def am(c):
                    n = width(c)
                    done(pe, s.am_ready, c)
                    turn_groups(c, 0, AM[c.parity], n)
                    done(pe, s.arg, c.before(1))
                    for g, at, m in groups(n):
                        evacuated(c, g)
                        times(psU[g], XT[g], {0: w0, 1: w1}[r], m).then_inc(s.mult, 1)

                def x1(c):
                    done(pe, s.front, c)
                    turn_groups(c, 2, PL1[c.parity], C)
                    seam(r, c, V[c.slot], w)
                    done(pe, s.updated, c.before(1))
                    for g, at, m in groups(C):
                        evacuated(c, 2 + g)
                        times(psY[g], XT[2 + g], w1c, m).then_inc(s.mult, 1)

                def attend(c):
                    used(pe, s.gathered, c, 16 * C)
                    turn_groups(c, 0, V[c.slot], C)
                    used(pe, s.xd_loaded, c, 32)
                    turn_groups(c, 2, XE[c.slot], C)
                    done(pe, s.xb_ready, c)
                    turn_groups(c, 4, XB[c.parity], C)
                    done(pe, s.ke_read, c.before(1), 2)
                    for g, at, m in groups(C):
                        count(pe, s.v_copied, c.n * 2 + g)
                        evacuated(c, 4 + g)
                        times(psQV, XT[4 + g], wq, m).then_inc(s.q_mult, 1)
                        times(psK[g], XT[g], wkv[:, 0:D], m)
                        times(psE[g], XT[2 + g], we, m).then_inc(s.ke_mult, 1)
                        pe.wait_ge(s.q_copied, c.n * 2 + g + 1)
                        times(psQV, XT[g], wkv[:, D:2 * D], m).then_inc(s.v_mult, 1)

                def attended(c):
                    if c.exists:
                        done(pe, s.msg_ready, c)
                        seam(r, c, MS[c.parity], w)

                def step(c):
                    if r == 0:
                        am(c)
                        x1(c)
                    if r == 1:
                        done(pe, s.msg_ready, c)
                        seam(r, c, MS[c.parity], w)
                        am(c)
                    if r in (2, 3):
                        done(pe, s.front, c)
                        seam(r, c, V[c.slot], w)
                    if r == 4:
                        attended(c.before(2))
                        attend(c)

                each_chunk(pe, CHUNKS, RING, step)
                final = SEAM.before(1)
                if r == 4:
                    attended(SEAM.before(2))
                    attended(final)
                done(pe, s.updated, final)
                if r < 4:
                    pe.matmul(psS[:, 0:w], eq_tail[:, :], AG[final.parity][:, C - 1, 0:w], start=False,
                              stop=True).then_inc(s.seam_total, 1)
                else:
                    pe.matmul(psS[:, 0:w], eq_head[:, :], AG[final.parity][:, 0, 0:w], start=False,
                              stop=True).then_inc(s.seam_total, 1)
                if r in (0, 1):
                    am(SEAM)

        @block.scalar
        def _(act):
            me = Steps(act, act_step)
            act.preload_act_table_set("natural_log_exp_and_others")

            def root(sm, n, signal):
                me.mark(act.activation(sm.ln[:, 0:n], sm.arg[:, 0:n], ACT.Ln))
                me.wait()
                act.activation(sm.guess[:, 0:n], sm.ln[:, 0:n], ACT.Exp, scale=-0.5).then_inc(signal, 1)

            act.wait_ge(arg_ready, 1)
            root(first, COLS, root_ready)

            def dense_turned(c, parts):
                for g, at, m in parts:
                    i = c.n * DG + g
                    act.wait_ge(d_turned, i + 1)
                    count(act, d_mult, i - 3)
                    act.activation(XT[g % 4][0:D, 0:m * P], psT[g % 2][0:D, 0:m * P], ACT.Copy).then_inc(d_evac, 1)

            def dense_root(c, n=DC):
                if c.exists:
                    done(act, y_arg, c)
                    root(second, n, y_root)

            def dense_out(c, n=DC):
                if not c.exists:
                    return
                done(act, d_scale, c)
                used(act, d_stored, c.before(2))
                for j in range(n):
                    last = act.activation(DO[c.slot][:, j, :], DY[c.slot][:, j, :], ACT.Copy,
                                          scale=second.root[:, j:j + 1])
                last.then_inc(d_out, 1)

            def dense_square(c, n=DC):
                act.wait_ge(d_read, c.n * DG + len(groups(n)))
                act.activation(DSQ[:, 0:n, :], DY[c.slot][:, 0:n, :], ACT.Square).then_inc(d_sq, 1)

            def dense(c, n=DC):
                dense_turned(c, groups(n)[:4])
                done(act, d_arg, c)
                root(first, n, d_root)
                dense_root(c.before(1))
                dense_turned(c, groups(n)[4:])
                dense_out(c.before(1))
                dense_square(c, n)

            each_chunk(act, DCHUNKS, 2, dense, [me])
            last_dense = Chunk(DCHUNKS, 2, DCHUNKS % 2, DCHUNKS // 2 + 1)
            dense(last_dense, 2)
            dense_root(last_dense, 2)
            dense_out(last_dense, 2)
            for k in range(2):
                act.wait_ge(d_stored[k], 16 * len(range(k, DCHUNKS + 1, 2)))

            def masks(r, c):
                s = S[r]
                done(act, s.seam_added, c.before(2))
                for j in range(C):
                    m, eq = (head, eq_head) if r < 4 else (tail, eq_tail)
                    last = act.activation(MB[c.parity][:, j, :], eq[:, :], ACT.Copy, scale=m[:, bass.ds(cols(r, c) + j, 1)])
                last.then_inc(s.mask_ready, 1)

            for r in ROUNDS:
                s = S[r]

                if r:
                    act.wait_ge(S[r - 1].seam_total, 1)

                def evac(c, q, n):
                    for g, at, m in groups(n):
                        i = c.n * s.groups + q + g
                        act.wait_ge(s.turned, i + 1)
                        if r == 4:
                            done(act, s.v_mult, c.before(1), 2)
                        else:
                            count(act, s.mult, i - s.groups + 1)
                        act.activation(XT[q + g][0:D, 0:m * P], psT[(q + g) % 2][0:D, 0:m * P], ACT.Copy).then_inc(s.evac, 1)

                def root_of(c):
                    if c.exists:
                        done(act, s.arg, c)
                        root(second, 3 * C if r == 0 and c is not SEAM else width(c), s.root)

                def normalise(c):
                    if c.exists:
                        done(act, s.norm_ready, c)
                        used(act, s.scattered if r == 4 else s.stored, c.before(RING), 16 * C if r == 4 else 16)
                        for j in range(width(c)):
                            last = act.activation(OT[c.slot][:, j, :], UB[c.parity][:, j, :], ACT.Identity,
                                                  scale=second.by[:, j:j + 1], bias=second.shift[:, j:j + 1])
                        last.then_inc(s.updated, 1)

                def step(c):
                    if r == 0:
                        root_of(c.before(1))
                        done(act, s.x1_arg, c)
                        root(first, C, s.x1_root)
                        masks(r, c)
                        evac(c, 0, C)
                        evac(c, 2, C)
                        for g, at, m in groups(C):
                            act.wait_ge(s.mult, c.n * 4 + 3 + g)
                            squared = act.activation(SQ[:, at:at + m, :], by_rows(psY[g], m), ACT.Square)
                        squared.then_inc(s.squared, 1)
                    if r == 1:
                        used(act, s.gathered, c, 16 * C)
                        done(act, s.msg_ready, c.before(2))
                        done(act, s.seam_added, c.before(2))
                        act.activation(MM[c.parity][:, :, :], V[c.slot][:, :, 0:D], ACT.Relu).then_inc(s.relu_done, 1)
                        done(act, s.relu_done, c)
                        act.activation(MS[c.parity][:, :, D:2 * D], MM[c.parity][:, :, :], ACT.Exp
                                       ).then_inc(s.exp_ready, 1)
                        root_of(c.before(1))
                        masks(r, c)
                        evac(c, 0, C)
                        normalise(c.before(1))
                    if r == 2:
                        masks(r, c)
                    if r == 3:
                        masks(r, c)
                        root_of(c.before(1))
                        normalise(c.before(1))
                    if r == 4:
                        root_of(c.before(2))
                        used(act, s.xd_loaded, c, 32)
                        done(act, s.xb_ready, c.before(2))
                        for j in range(C):
                            last = act.activation(XA[c.parity][:, j, :], XD[c.slot][:, j, :], ACT.Copy,
                                                  scale=own[:, bass.ds(cols(r, c) + j, 1)])
                        last.then_inc(s.scaled, 1)
                        exponent(c.before(1))
                        masks(r, c)
                        evac(c, 0, C)
                        evac(c, 2, C)
                        normalise(c.before(2))
                        evac(c, 4, C)
                        done(act, s.msg_ready, c.before(2))
                        for g, at, m in groups(C):
                            k = c.n * 2 + g + 1
                            act.wait_ge(s.q_mult, k)
                            act.activation(QS[c.parity][:, at:at + m, :], by_rows(psQV, m), ACT.Copy).then_inc(s.q_copied, 1)
                            act.wait_ge(s.v_mult, k)
                            act.activation(VS[c.parity][:, at:at + m, :], by_rows(psQV, m), ACT.Copy).then_inc(s.v_copied, 1)

                def exponent(c):
                    if c.exists:
                        done(act, s.score_ready, c)
                        done(act, s.seam_added, c.before(2))
                        act.activation(MS[c.parity][:, :, D:W4], SC2[:, :, :], ACT.Exp).then_inc(s.exp_ready, 1)

                each_chunk(act, CHUNKS, RING, step, [me])
                final = SEAM.before(1)
                if r == 4:
                    root_of(SEAM.before(2))
                    exponent(final)
                    normalise(SEAM.before(2))
                if r in (0, 1, 3, 4):
                    root_of(final)
                if r in (1, 3, 4):
                    normalise(final)
                if r == 0:
                    act.wait_ge(s.deg_arg, 1)
                    root(first, 1, s.deg_root)
                if r in (0, 1):
                    evac(SEAM, 0, 1)
                if r in (0, 1, 3, 4):
                    root_of(SEAM)
                if r in (1, 3, 4):
                    normalise(SEAM)

        @block.vector
        def _(dve):
            me = Steps(dve, dve_step)

            def wide(a, at, n, w=D):
                return a[:, bass.ds(at, n)].unsqueeze(2).to_broadcast([P, n, w])

            def stats(sm, rows, n, lo=0):
                me.wait()
                for j in range(n):
                    last = dve.bn_stats(out=sm.st[:, j, :], in_=rows[:, j, 0:D])
                me.mark(last)
                me.wait()
                even, odd = sm.st[:, 0:n, 1], sm.st[:, 0:n, 4]
                me.mark(dve.tensor_tensor(sm.t[:, 0, 0:n], even, odd, ALU.subtract))
                me.mark(dve.tensor_tensor(sm.mean[:, lo:lo + n], even, odd, ALU.add))
                me.mark(dve.scalar_tensor_tensor(out=sm.t[:, 1, 0:n], in0=sm.st[:, 0:n, 2], scalar=D * EPS,
                                                 in1=sm.st[:, 0:n, 5], op0=ALU.add, op1=ALU.add))
                me.wait()
                me.mark(dve.scalar_tensor_tensor(out=sm.t[:, 2, 0:n], in0=sm.t[:, 0, 0:n], scalar=0.25,
                                                 in1=sm.t[:, 0, 0:n], op0=ALU.mult, op1=ALU.mult))
                me.wait()
                return dve.scalar_tensor_tensor(out=sm.arg[:, lo:lo + n], in0=sm.t[:, 1, 0:n], scalar=1.0 / D,
                                                in1=sm.t[:, 2, 0:n], op0=ALU.mult, op1=ALU.add)

            def refine(sm, n, signal, value):
                dve.wait_ge(signal, value)
                me.wait()
                me.mark(dve.tensor_tensor(sm.t[:, 3, 0:n], sm.guess[:, 0:n], sm.guess[:, 0:n], ALU.mult))
                me.wait()
                me.mark(dve.scalar_tensor_tensor(out=sm.t[:, 4, 0:n], in0=sm.t[:, 3, 0:n], scalar=-0.5,
                                                 in1=sm.arg[:, 0:n], op0=ALU.mult, op1=ALU.mult))
                me.wait()
                return dve.scalar_tensor_tensor(out=sm.root[:, 0:n], in0=sm.t[:, 4, 0:n], scalar=1.5,
                                                in1=sm.guess[:, 0:n], op0=ALU.add, op1=ALU.mult)

            me.mark(dve.memset(ones[:, :], 1.0))
            for k in range(6):
                me.mark(dve.memset(XT[k][D:D + 1, :], 1.0))
            for k in range(RING):
                me.mark(dve.memset(V[k][:, :, D:D + 1], 1.0))
                me.mark(dve.memset(XD[k][:, :, :], 0.0))
                me.mark(dve.memset(XE[k][:, :, :], 0.0))
            me.mark(dve.memset(xnext[:, :], 0.0))
            dve.wait_ge(loaded, 16 * 16)
            dve.wait_ge(consts_ready, 1)
            me.mark(dve.tensor_copy(dst_f[:, :], dst_i[:, :]))
            me.mark(dve.tensor_scalar(centre[0:D, :], ident[0:D, 0:D], -1.0 / D, None, ALU.add))
            me.mark(dve.tensor_tensor(w1c[0:D, :], w1[0:D, :], ident[0:D, 0:D], ALU.add))
            me.mark(dve.tensor_copy(w1c[D:D + 1, :], w1[D:D + 1, :]))
            me.mark(dve.tensor_reduce(second.t[:, 0, 0:1], b1c[:, :], AX, ALU.add))
            me.wait()
            me.mark(dve.tensor_reduce(wsum[0:D + 1, :], w1c[0:D + 1, :], AX, ALU.add))
            me.mark(dve.tensor_scalar(second.t[:, 1, 0:1], second.t[:, 0, 0:1], 1.0 / D, None, ALU.mult))
            me.wait()
            me.mark(dve.tensor_scalar(b1c[:, :], b1c[:, :], second.t[:, 1, 0:1], None, ALU.subtract))
            me.mark(dve.tensor_scalar(second.t[0:D + 1, 2, 0:1], wsum[0:D + 1, :], 1.0 / D, None, ALU.mult))
            me.wait()
            me.send(dve.tensor_scalar(w1c[0:D + 1, :], w1c[0:D + 1, :], second.t[0:D + 1, 2, 0:1], None,
                                      ALU.subtract), w1c_ready, 1)
            me.wait()
            d, d0, dn = dst_f[:, 0:COLS], dst_f[:, 0:1], dst_f[:, COLS:TC]
            me.mark(dve.memset(keep_fwd[:, 0:1], 0.0))
            me.mark(dve.memset(keep_rev[:, COLS - 1:COLS], 0.0))
            me.mark(dve.tensor_tensor(keep_fwd[:, 1:COLS], dst_f[:, 1:COLS], dst_f[:, 0:COLS - 1], ALU.is_equal))
            me.mark(dve.tensor_tensor(keep_rev[:, 0:COLS - 1], dst_f[:, 0:COLS - 1], dst_f[:, 1:COLS], ALU.is_equal))
            me.mark(dve.tensor_scalar(head[:, :], d, d0, None, ALU.is_equal))
            me.mark(dve.tensor_scalar(tail[:, :], d, dst_f[:, COLS - 1:COLS], None, ALU.is_equal))
            me.mark(dve.tensor_scalar(MB[0][:, 0, :], ident[:, :], d0, None, ALU.mult))
            me.mark(dve.tensor_tensor(tmp_a[:, 0:COLS], d, dst_f[:, 1:TC], ALU.not_equal))
            me.mark(dve.tensor_scalar(tmp_b[:, 0:COLS], d, d0, None, ALU.not_equal))
            me.wait()
            me.mark(dve.tensor_tensor(own[:, :], tmp_a[:, 0:COLS], tmp_b[:, 0:COLS], ALU.mult))
            me.wait()
            me.mark(dve.tensor_tensor(pull[:, :], tmp_b[:, 0:COLS], own[:, :], ALU.subtract))
            me.wait()
            me.mark(dve.tensor_scalar(tmp_b[:, 0:COLS], d, float(-BIG), None, ALU.add))
            me.wait()
            me.mark(dve.tensor_tensor(tmp_a[:, 0:COLS], tmp_b[:, 0:COLS], own[:, :], ALU.mult))
            me.mark(dve.tensor_tensor(first.t[:, 0, 0:1], d0, dn, ALU.not_equal))
            me.wait()
            me.mark(dve.tensor_tensor(tmp_a[:, COLS:TC], tmp_b[:, 0:1], first.t[:, 0, 0:1], ALU.mult))
            me.wait()
            me.mark(dve.tensor_scalar(rep_i[:, :], tmp_a[:, :], float(BIG), None, ALU.add))
            me.wait()
            me.mark(dve.tensor_scalar(first.t[:, 1, 0:COLS], d, dn, None, ALU.not_equal))
            me.mark(dve.tensor_scalar(first.t[:, 2, 0:COLS], keep_fwd[:, :], -1.0, 1.0, ALU.mult, ALU.add))
            me.wait()
            me.mark(dve.tensor_tensor(first.t[:, 3, 0:COLS], first.t[:, 1, 0:COLS], first.t[:, 2, 0:COLS], ALU.mult))
            me.wait()
            me.mark(dve.tensor_tensor(tmp_a[:, 0:COLS], tmp_b[:, 0:COLS], first.t[:, 3, 0:COLS], ALU.mult))
            me.wait()
            me.mark(dve.memset(tmp_a[:, 0:1], 0.0))
            me.wait()
            me.mark(dve.tensor_scalar(out_i[:, :], tmp_a[:, :], float(BIG), None, ALU.add))
            me.wait()
            me.send(dve.tensor_copy(first.t[:, 4, 0:1], d0), edges_ready, 1)
            dve.wait_ge(firsts_done, 1)
            me.mark(dve.tensor_scalar(eq_head[:, :], psS[:, 0:P], d0, None, ALU.is_equal))
            me.mark(dve.tensor_scalar(MB[1][:, 0, :], psS[:, 0:P], dst_f[:, COLS - 1:COLS], None, ALU.is_equal))
            me.mark(dve.tensor_tensor(first.t[:, 5, 0:1], dst_f[:, COLS - 1:COLS], d0, ALU.not_equal))
            me.wait()
            me.mark(dve.tensor_scalar(eq_tail[:, :], MB[1][:, 0, :], first.t[:, 5, 0:1], None, ALU.mult))
            me.mark(dve.memset(first.t[:, 0, :], 1.0))
            me.mark(dve.memset(deg[:, COLS:TC], 1.0))
            me.wait()
            me.mark(dve.tensor_tensor_scan(deg[:, 0:COLS], keep_fwd[:, :], first.t[:, 0, 0:COLS], 0.0,
                                           ALU.mult, ALU.add))

            def degree_values(at, n):
                rs = first.root
                me.wait()
                me.mark(dve.reciprocal(rdeg[:, at:at + n], deg[:, at:at + n]))
                me.mark(dve.tensor_copy(dinv[:, at:at + n], rs[:, 0:n]))
                me.mark(dve.tensor_tensor(dinv2[:, at:at + n], rs[:, 0:n], rs[:, 0:n], ALU.mult))
                me.mark(dve.tensor_tensor(sdeg[:, at:at + n], rs[:, 0:n], first.arg[:, 0:n], ALU.mult))
                me.wait()

            me.wait()
            me.send(dve.tensor_scalar(first.arg[:, 0:COLS], deg[:, 0:COLS], 1.0, None, ALU.add), arg_ready, 1)
            dve.wait_ge(w1x_done, 1)
            me.mark(refine(first, COLS, root_ready, 1))
            degree_values(0, COLS)
            me.send(dve.tensor_copy(w1x[0:D, :], psQV[0:D, 0:D]), prep_done, 1)

            def dense(c, n=DC):
                used(dve, d_loaded, c)
                me.send(stats(first, DX[c.slot], n), d_arg, c.n + 1)
                dense_scale(c.before(1))
                me.mark(refine(first, n, d_root, c.n + 1))
                dense_scaled(c.before(1))
                done(dve, d_out, c.before(2))
                me.wait()
                for g, at, m in groups(n):
                    i = c.n * DG + g
                    dve.wait_ge(d_mult, i + 1)
                    for j in range(m):
                        last = dve.scalar_tensor_tensor(
                            out=DY[c.slot][:, at + j, :], in0=dY[g % 4][:, j * D:(j + 1) * D],
                            scalar=first.root[:, at + j:at + j + 1], in1=b1c[:, :], op0=ALU.mult, op1=ALU.add)
                    me.send(last, d_read, i + 1)

            def dense_scale(c, n=DC):
                if c.exists:
                    done(dve, d_sq, c)
                    me.wait()
                    me.mark(dve.tensor_reduce(second.t[:, 5, 0:n], DSQ[:, 0:n, :], AX, ALU.add))
                    me.wait()
                    me.send(dve.tensor_scalar(second.arg[:, 0:n], second.t[:, 5, 0:n], (1 + EPS / 2) ** 2 / D,
                                              EPS ** 3 / 4, ALU.mult, ALU.add), y_arg, c.n + 1)

            def dense_scaled(c, n=DC):
                if c.exists:
                    me.send(refine(second, n, y_root, c.n + 1), d_scale, c.n + 1)

            each_chunk(dve, DCHUNKS, 2, dense, [me])
            last_dense = Chunk(DCHUNKS, 2, DCHUNKS % 2, DCHUNKS // 2 + 1)
            dense(last_dense, 2)
            dense_scale(last_dense, 2)
            dense_scaled(last_dense, 2)
            for k in range(2):
                dve.wait_ge(d_stored[k], 16 * len(range(k, DCHUNKS + 1, 2)))
            me.mark(dve.memset(AG[0][:, :, :], 0.0))
            me.mark(dve.memset(AG[1][:, :, :], 0.0))

            for r in ROUNDS:
                s = S[r]
                w = {0: D + 1, 1: 2 * D, 2: D, 3: D, 4: W4}[r]

                def running(c, values, signal=None):
                    keep = keep_fwd if r < 4 else keep_rev
                    b = c.parity
                    order = list(range(C)) if r < 4 else list(reversed(range(C)))
                    for j in order:
                        if r < 4:
                            prev = AG[b][:, j - 1, 0:w] if j else AG[1 - b][:, C - 1, 0:w]
                        else:
                            prev = AG[b][:, j + 1, 0:w] if j < C - 1 else AG[1 - b][:, 0, 0:w]
                        me.wait()
                        summed = dve.scalar_tensor_tensor(out=AG[b][:, j, 0:w], in0=prev,
                                                          scalar=keep[:, bass.ds(cols(r, c) + j, 1)],
                                                          in1=values[:, j, 0:w], op0=ALU.mult, op1=ALU.add)
                        if signal and j == order[-1]:
                            me.send(summed, signal, c.n + 1)
                        else:
                            me.mark(summed)

                def dst_input(c, ag):
                    b, n, at = c.parity, width(c), cols(r, c)
                    done(dve, s.turned, c.before(2), s.groups, 2 - s.groups)
                    me.wait()
                    if r == 0:
                        me.send(dve.tensor_tensor(AM[b][:, 0:n, :], ag[:, 0:n, 0:D], wide(rdeg, at, n), ALU.mult), s.am_ready, c.n + 1)
                    else:
                        used(dve, s.xd_loaded, c)
                        me.mark(dve.reciprocal(U3[:, 0:n, :], ag[:, 0:n, D:2 * D]))
                        me.wait()
                        me.mark(dve.tensor_tensor(U2[:, 0:n, :], ag[:, 0:n, 0:D], U3[:, 0:n, :], ALU.mult))
                        me.wait()
                        me.send(dve.tensor_tensor(AM[b][:, 0:n, :], U2[:, 0:n, :], XD[c.slot][:, 0:n, :], ALU.add), s.am_ready, c.n + 1)

                def hop(c, ag):
                    n, at, b = width(c), cols(r, c), c.parity
                    used(dve, s.xd_loaded, c, 16 if r == 2 else 32)
                    me.wait()
                    me.mark(dve.tensor_tensor(U2[:, 0:n, :], ag[:, 0:n, 0:D], XD[c.slot][:, 0:n, :], ALU.add))
                    if r == 2:
                        used(dve, s.stored, c.before(RING))
                        me.wait()
                        me.send(dve.tensor_tensor(OT[c.slot][:, 0:n, :], U2[:, 0:n, :], wide(dinv2, at, n), ALU.mult), s.updated, c.n + 1)
                    else:
                        me.mark(dve.tensor_tensor(U3[:, 0:n, :], XE[c.slot][:, 0:n, :], wide(sdeg, at, n), ALU.mult))
                        me.wait()
                        me.mark(dve.tensor_tensor(AM[0][:, 0:n, :], U2[:, 0:n, :], wide(dinv, at, n), ALU.mult))
                        done(dve, s.updated, c.before(2))
                        me.wait()
                        me.mark(dve.tensor_tensor(UB[b][:, 0:n, :], U3[:, 0:n, :], AM[0][:, 0:n, :], ALU.add))
                        me.send(stats(second, UB[b], n), s.arg, c.n + 1)

                def shifts(n, lo=0, scale=None):
                    by = second.root
                    me.wait()
                    if scale is not None:
                        me.mark(dve.tensor_tensor(second.by[:, lo:lo + n], second.root[:, lo:lo + n], scale, ALU.mult))
                        by = second.by
                        me.wait()
                    elif r:
                        me.mark(dve.tensor_copy(second.by[:, lo:lo + n], second.root[:, lo:lo + n]))
                    return dve.scalar_tensor_tensor(out=second.shift[:, lo:lo + n], in0=second.mean[:, lo:lo + n],
                                                    scalar=-0.5, in1=by[:, lo:lo + n], op0=ALU.mult, op1=ALU.mult)

                def normalised(c):
                    if c.exists:
                        n = width(c)
                        me.mark(refine(second, n, s.root, c.n + 1))
                        scale = dinv[:, bass.ds(cols(r, c), n)] if r == 1 else None
                        me.send(shifts(n, 0, scale), s.norm_ready, c.n + 1)

                def product_added(c):
                    if not c.exists:
                        return
                    b, n, lo = c.parity, width(c), 0
                    if r == 0 and c is not SEAM:
                        lo = 2 * C
                        done(dve, s.squared, c)
                        me.wait()
                        me.mark(dve.tensor_reduce(second.t[:, 5, 0:n], SQ[:, :, :], AX, ALU.add))
                        me.wait()
                        me.mark(dve.tensor_scalar(second.arg[:, 0:C], second.t[:, 5, 0:C], 1.0 / D, EPS, ALU.mult, ALU.add))
                        me.mark(dve.tensor_scalar(second.arg[:, C:2 * C], second.t[:, 5, 0:C], (1 + EPS / 4) / D, EPS * EPS / 4,
                                                  ALU.mult, ALU.add))
                    if r == 0 and c is SEAM:
                        dve.wait_ge(s.gathered[c.slot][0], (c.turn - 1) * 2 * 16 * C + 16)
                    done(dve, s.updated, c.before(2))
                    me.wait()
                    for g, at, m in groups(n):
                        dve.wait_ge(s.mult, c.n * s.groups + g + 1)
                        me.mark(dve.tensor_tensor(UB[b][:, at:at + m, :], by_rows(psU[g], m), XD[c.slot][:, at:at + m, :],
                                                  ALU.add))
                    me.send(stats(second, UB[b], n, lo), s.arg, c.n + 1)

                def finished(c):
                    if not c.exists:
                        return
                    b, n = c.parity, width(c)
                    lo = 0 if c is SEAM else 2 * C
                    me.mark(refine(second, lo + n, s.root, c.n + 1))
                    me.mark(shifts(n, lo))
                    if c is not SEAM:
                        plain_free(c)
                        for g, at, m in groups(n):
                            y = by_rows(psY[g], m)
                            me.mark(dve.tensor_tensor(PL2[b][:, at:at + m, :], y, wide(second.root, at, m), ALU.mult))
                            me.mark(dve.tensor_tensor(PL4[b][:, at:at + m, :], y, wide(second.root, C + at, m), ALU.mult))
                    used(dve, s.stored, c.before(RING))
                    me.wait()
                    for j in range(n):
                        last = dve.tensor_scalar(OT[c.slot][:, j, :], UB[b][:, j, :], second.root[:, lo + j:lo + j + 1],
                                                 second.shift[:, lo + j:lo + j + 1], ALU.mult, ALU.add)
                    me.send(last, s.updated, c.n + 1)

                def plain_free(c):
                    old = c.before(2)
                    if old.exists:
                        turn = old.n // 2 + 1 if isinstance(old.n, int) else (c.turn - 1) * 2 + (c.slot - 2) // 2 + 1
                        dve.wait_ge(s.plain_stored[old.parity], turn * 48)

                def scored(c):
                    if not c.exists:
                        return
                    b = c.parity
                    me.wait()
                    for g, at, m in groups(C):
                        k = c.n * 2 + g + 1
                        dve.wait_ge(s.ke_mult, k)
                        dve.wait_ge(s.q_copied, k)
                        me.mark(dve.tensor_tensor(U2[:, at:at + m, :], by_rows(psK[g], m), QS[b][:, at:at + m, :], ALU.mult))
                    for g, at, m in groups(C):
                        me.wait()
                        me.send(dve.tensor_tensor(U3[:, at:at + m, :], by_rows(psE[g], m), U2[:, at:at + m, :], ALU.mult),
                                s.ke_read, c.n * 2 + g + 1)
                    me.wait()
                    me.mark(dve.tensor_reduce(SC[:, :, :].rearrange("p m h -> p (m h)"),
                                              U3[:, :, :].rearrange("p m (h e) -> p (m h) e", e=HD), AX, ALU.add))
                    me.wait()
                    me.mark(dve.tensor_scalar(SC[:, :, :], SC[:, :, :], float(HD) ** -0.5, 5.0, ALU.mult, ALU.min))
                    me.wait()
                    me.send(dve.tensor_scalar(SC2[:, :, :], SC[:, :, :], -5.0, None, ALU.max), s.score_ready, c.n + 1)

                def dst_rows(c):
                    b = c.parity
                    done(dve, s.scaled, c)
                    done(dve, s.turned, c.before(2), 6)
                    me.wait()
                    for j in range(C):
                        me.mark(dve.scalar_tensor_tensor(out=XA[b][:, j, :], in0=xseam[:, :],
                                                         scalar=head[:, bass.ds(cols(r, c) + j, 1)],
                                                         in1=XA[b][:, j, :], op0=ALU.mult, op1=ALU.add))
                    for j in reversed(range(C)):
                        prev = XB[b][:, j + 1, :] if j < C - 1 else XB[1 - b][:, 0, :]
                        me.wait()
                        row = dve.scalar_tensor_tensor(out=XB[b][:, j, :], in0=prev,
                                                       scalar=pull[:, bass.ds(cols(r, c) + j, 1)],
                                                       in1=XA[b][:, j, :], op0=ALU.mult, op1=ALU.add)
                        if j:
                            me.mark(row)
                        else:
                            me.send(row, s.xb_ready, c.n + 1)

                def per_head(row):
                    return row.rearrange("p (h e) -> p h e", e=HD)

                def messages(c):
                    if not c.exists:
                        return
                    b = c.parity
                    done(dve, s.exp_ready, c)
                    dve.wait_ge(s.v_copied, (c.n + 1) * 2)
                    me.wait()
                    for j in range(C):
                        last = dve.tensor_tensor(per_head(MS[b][:, j, 0:D]), per_head(VS[b][:, j, :]),
                                                 MS[b][:, j, D:W4].unsqueeze(2).to_broadcast([P, HEADS, HD]), ALU.mult)
                    me.send(last, s.msg_ready, c.n + 1)
                    running(c, MS[b])
                    attended(c, AG[b])

                def attended(c, sums):
                    b, n = c.parity, width(c)
                    me.wait()
                    me.mark(dve.tensor_scalar(SC[:, 0:n, :], sums[:, 0:n, D:W4], 1e-6, None, ALU.add))
                    me.wait()
                    me.mark(dve.reciprocal(ZR[:, 0:n, :], SC[:, 0:n, :]))
                    me.wait()
                    for j in range(n):
                        last = dve.tensor_tensor(per_head(U2[:, j, :]), per_head(sums[:, j, 0:D]),
                                                 ZR[:, j, :].unsqueeze(2).to_broadcast([P, HEADS, HD]), ALU.mult)
                    me.mark(last)
                    done(dve, s.updated, c.before(2))
                    me.wait()
                    xb = xseam[:, :].unsqueeze(1) if c is SEAM else XB[b][:, :, :]
                    me.mark(dve.tensor_tensor(UB[b][:, 0:n, :], U2[:, 0:n, :], xb, ALU.add))
                    me.send(stats(second, UB[b], n), s.arg, c.n + 1)

                def step(c):
                    if r == 0:
                        product_added(c.before(1))
                        used(dve, s.gathered, c, 2 * 16 * C)
                        me.send(stats(first, V[c.slot], C), s.x1_arg, c.n + 1)
                        running(c, V[c.slot])
                        dst_input(c, AG[c.parity])
                        finished(c.before(1))
                        me.mark(refine(first, C, s.x1_root, c.n + 1))
                        me.wait()
                        me.mark(dve.scalar_tensor_tensor(out=first.shift[:, 0:C], in0=first.mean[:, 0:C], scalar=-0.5,
                                                         in1=first.root[:, 0:C], op0=ALU.mult, op1=ALU.mult))
                        plain_free(c)
                        done(dve, s.turned, c.before(2), 4)
                        me.wait()
                        for j in range(C):
                            last = dve.tensor_scalar(PL1[c.parity][:, j, :], V[c.slot][:, j, 0:D], first.root[:, j:j + 1],
                                                     first.shift[:, j:j + 1], ALU.mult, ALU.add)
                        me.send(last, s.front, c.n + 1)
                    if r == 1:
                        product_added(c.before(1))
                        done(dve, s.exp_ready, c)
                        me.wait()
                        b = c.parity
                        me.send(dve.scalar_tensor_tensor(out=MS[b][:, :, 0:D], in0=MM[b][:, :, :], scalar=1e-7,
                                                         in1=MS[b][:, :, D:2 * D], op0=ALU.add, op1=ALU.mult), s.msg_ready, c.n + 1)
                        running(c, MS[b])
                        dst_input(c, AG[b])
                        normalised(c.before(1))
                    if r in (2, 3):
                        used(dve, s.gathered, c, 16 * C)
                        running(c, V[c.slot], s.front)
                        if r == 3:
                            normalised(c.before(1))
                        hop(c, AG[c.parity])
                    if r == 4:
                        scored(c.before(1))
                        normalised(c.before(2))
                        dst_rows(c)
                        messages(c.before(1))

                if r == 4:
                    dve.wait_ge(s.seam_loaded, 32)
                    me.mark(dve.tensor_copy(XB[1][:, 0, :], xnext[:, :]))
                each_chunk(dve, CHUNKS, RING, step, [me])
                final = SEAM.before(1)
                if r in (0, 1):
                    product_added(final)
                if r == 0:
                    finished(final)
                if r in (1, 3):
                    normalised(final)
                if r == 4:
                    scored(final)
                    normalised(SEAM.before(2))
                    messages(final)
                    normalised(final)

                dve.wait_ge(s.seam_total, 1)
                me.mark(dve.tensor_copy(SG[:, 0, 0:w], psS[:, 0:w]))
                me.wait()
                if r == 0:
                    me.mark(dve.tensor_copy(deg[:, COLS:TC], SG[:, 0, D:D + 1]))
                    me.wait()
                    me.send(dve.tensor_scalar(first.arg[:, 0:1], SG[:, 0, D:D + 1], 1.0, None, ALU.add), s.deg_arg, 1)
                    me.mark(refine(first, 1, s.deg_root, 1))
                    degree_values(COLS, 1)
                if r in (0, 1):
                    dst_input(SEAM, SG)
                    product_added(SEAM)
                if r == 0:
                    finished(SEAM)
                if r in (2, 3):
                    hop(SEAM, SG)
                if r == 4:
                    attended(SEAM, SG)
                if r in (1, 3, 4):
                    normalised(SEAM)



_INS = ["x", "src", "dst", "edge_attr_96", "L0_gnn_W", "L0_gnn_b", "L1_gnn_W", "L1_gnn_b", "L3_gnn_Wq", "L3_gnn_bq",
        "L3_gnn_Wk", "L3_gnn_bk", "L3_gnn_We", "L3_gnn_be", "L3_gnn_Wv", "L3_gnn_bv"]


def kernel(**inputs):
    import numpy as _np
    import concourse.bacc as _bacc
    from concourse import mybir as _mybir
    from concourse.bass_utils import run_bass_kernel_spmd as _run

    nc = _bacc.Bacc("TRN2", target_bir_lowering=False, num_devices=1)
    arrays, args = {}, []
    for name in _INS:
        a = _np.ascontiguousarray(inputs[name])
        arrays[f"in_{name}"] = a
        args.append(nc.dram_tensor(f"in_{name}", a.shape, _mybir.dt.from_np(a.dtype), kind="ExternalInput").ap())
    result = nc.dram_tensor("out_dram", (N, D), _mybir.dt.float32, kind="ExternalOutput").ap()
    build(nc, *args, result)
    r = _run(nc, [arrays], core_ids=[0])
    return r.results[0]["out_dram"]
```

```python
from contextlib import ExitStack

import concourse.bass as bass
from concourse import mybir

F32 = mybir.dt.float32
I32 = mybir.dt.int32
ALU = mybir.AluOpType
ACT = mybir.ActivationFunctionType
AX = mybir.AxisListType.X

P = 128
N, D, E = 100000, 96, 25000
COLS = 200
EP = E // COLS
TC = COLS + 1
C = 8
G = 4
CHUNKS = COLS // C
RING = 4
HEADS, HD = 8, D // 8
W4 = D + HEADS
EPS = 1e-5
BIG = 1 << 20
DC = 30
DG = -(-DC // G)
DCOLS = N // P // DC * DC
DCHUNKS = DCOLS // DC
DREST = N - P * DCOLS
DRP = DREST // 2
assert CHUNKS % RING
assert EP * COLS == E and DRP * 2 == DREST and DRP <= P
ROUNDS = range(5)


class Chunk:

    def __init__(self, n, ring, slot, turn):
        self.n, self.ring, self.slot, self.turn = n, ring, slot, turn

    def before(self, k=1):
        slot = (self.slot - k) % self.ring
        return Chunk(self.n - k, self.ring, slot, self.turn - (1 if slot > self.slot or k == self.ring else 0))

    def after(self):
        slot = (self.slot + 1) % self.ring
        return Chunk(self.n + 1, self.ring, slot, self.turn + (1 if slot == 0 else 0))

    @property
    def exists(self):
        return not isinstance(self.n, int) or self.n >= 0

    @property
    def parity(self):
        return self.slot % 2


def each_chunk(eng, count, ring, step, steps=()):
    before = [s.count for s in steps]
    for n in range(ring):
        if n == ring - 1:
            before = [s.count for s in steps]
        step(Chunk(n, ring, n, 1))
    per = [(s.count - b) * ring for s, b in zip(steps, before)]
    turns = count // ring
    with eng.Fori(1, turns) as i:
        for s, stride in zip(steps, per):
            s.enter(i, stride)
        for slot in range(ring):
            step(Chunk(i * ring + slot, ring, slot, i + 1))
        for s in steps:
            s.leave(turns - 1)
    for n in range(turns * ring, count):
        step(Chunk(n, ring, n % ring, n // ring + 1))


class Steps:

    def __init__(self, eng, sem):
        self.eng, self.sem, self.count, self.offset, self.base, self.stride = eng, sem, 0, None, 0, 0
        self.sent = None

    def enter(self, i, stride):
        self.base, self.stride = self.count, stride
        self.offset = (i - 1) * stride
        self.sent = None

    def leave(self, turns):
        assert self.count - self.base == self.stride, (self.count - self.base, self.stride)
        self.count, self.offset, self.sent = self.base + turns * self.stride, None, None

    def mark(self, instruction):
        instruction.then_inc(self.sem, 1)
        self.count += 1
        self.sent = None

    def send(self, instruction, signal, value):
        instruction.then_inc(signal, 1)
        self.sent = signal, value

    def wait(self, but=0):
        if self.sent:
            self.eng.wait_ge(*self.sent)
            return
        value = (self.count if self.offset is None else self.offset + self.count) - but
        self.eng.wait_ge(self.sem, value)


def build(nc, x, src, dst, edge_attr, W0, b0, W1, b1, Wq, bq, Wk, bk, We, be, Wv, bv, out):
    with ExitStack() as ctx:
        def sb(name, shape, dt=F32):
            return ctx.enter_context(nc.sbuf_tensor(name, shape, dt))

        def sem(name):
            return ctx.enter_context(nc.semaphore(name))

        def ring_sems(name, n=RING):
            return [sem(f"{name}_{i}") for i in range(n)]

        table = {r: nc.dram_tensor(f"table{r}", (P * TC, D), F32).ap() for r in (1, 2, 3, 4)}
        table_v = {r: t.rearrange("(p t) d -> p t d", t=TC) for r, t in table.items()}
        plain = {r: nc.dram_tensor(f"plain{r}", (P, COLS, D), F32).ap() for r in (1, 2, 4)}
        row_of = nc.dram_tensor("row_of", (N, 1), I32).ap()

        ident = sb("ident", [P, P])
        ones = sb("ones", [P, P])
        w0 = sb("w0", [P, D])
        w1 = sb("w1", [P, D])
        w1c = sb("w1c", [P, D])
        wkv = sb("wkv", [P, 2 * D])
        wq = sb("wq", [P, D])
        we = sb("we", [P, D])
        wsum = sb("wsum", [P, 1])

        src_i = sb("src_i", [P, COLS], I32)
        dst_i = sb("dst_i", [P, TC], I32)
        dst_f = sb("dst_f", [P, TC])
        keep_fwd = sb("keep_fwd", [P, COLS])
        keep_rev = sb("keep_rev", [P, COLS])
        head = sb("head", [P, COLS])
        tail = sb("tail", [P, COLS])
        own = sb("own", [P, COLS])
        pull = sb("pull", [P, COLS])
        tmp_a = sb("tmp_a", [P, TC])
        tmp_b = sb("tmp_b", [P, TC])
        rep_i = sb("rep_i", [P, TC], I32)
        out_i = sb("out_i", [P, TC], I32)
        rowid = sb("rowid", [P, TC], I32)
        head_row = sb("head_row", [P, 1], I32)
        src_row = sb("src_row", [P, COLS], I32)
        eq_head = sb("eq_head", [P, P])
        eq_tail = sb("eq_tail", [P, P])
        deg = sb("deg", [P, TC])
        rdeg = sb("rdeg", [P, TC])
        dinv = sb("dinv", [P, TC])
        dinv2 = sb("dinv2", [P, TC])
        sdeg = sb("sdeg", [P, TC])
        bigs = sb("bigs", [P, N // EP], I32)

        V = [sb(f"V{k}", [P, C, D + 1]) for k in range(RING)]
        XD = [sb(f"XD{k}", [P, C, D]) for k in range(RING)]
        XE = [sb(f"XE{k}", [P, C, D]) for k in range(RING)]
        OT = [sb(f"OT{k}", [P, C, D]) for k in range(RING)]
        kc = [sb(f"kc{k}", [P, C]) for k in range(2)]
        pc = sb("pc", [P, C])
        mc = [sb(f"mc{k}", [P, C]) for k in range(2)]
        oc = [sb(f"oc{k}", [P, C]) for k in range(2)]
        idx = [sb(f"idx{k}", [P, C], I32) for k in range(RING)]
        idx2 = [sb(f"idx2{k}", [P, C], I32) for k in range(RING)]
        rid = [sb(f"rid{k}", [P, C], I32) for k in range(RING)]
        rst = [sb(f"rst{k}", [P, C], I32) for k in range(RING)]
        DX = [sb(f"DX{k}", [P, DC, D]) for k in range(2)]

        space = sb("space", [P, 19200])
        place = [0]

        def carve(rows, width, again=False):
            if again:
                place[0] = 0
            at = place[0]
            place[0] += rows * width
            assert place[0] <= space.shape[1], place
            return space[:, at:at + rows * width].rearrange("p (t d) -> p t d", d=width)

        DY = [carve(DC, D, again=k == 0) for k in range(2)]
        DO = [carve(DC, D) for k in range(2)]
        DSQ = carve(DC, D)
        AG = [carve(C, 2 * D, again=k == 0) for k in range(2)]
        MS = [carve(C, 2 * D) for k in range(2)]
        MM = [carve(C, D) for k in range(2)]
        AM = [carve(C, D) for k in range(2)]
        PL1 = [MS[k][:, :, 0:D] for k in range(2)]
        PL2 = [MS[k][:, :, D:2 * D] for k in range(2)]
        PL4 = [carve(C, D) for k in range(2)]
        UB = [carve(C, D) for k in range(2)]
        U2 = carve(C, D)
        U3 = carve(C, D)
        SQ = carve(C, D)
        MB = [carve(C, P) for k in range(2)]
        SC = carve(C, HEADS)
        SC2 = carve(C, HEADS)
        ZR = carve(C, HEADS)
        SG = carve(1, 2 * D)
        XA, XB = AM, [carve(C, D) for k in range(2)]
        QS, VS = MM, PL4
        LZ, GZ = XB
        XT = [sb(f"XT{k}", [P, G * P]) for k in range(6)]
        xseam = sb("xseam", [P, D])
        xnext = sb("xnext", [P, D])
        b1c = sb("b1c", [P, D])
        w1x = sb("w1x", [P, D])
        centre = sb("centre", [P, D])

        class Small:

            def __init__(self, name, n):
                self.st = sb(f"{name}_st", [P, DC, 6])
                self.t = sb(f"{name}_t", [P, 6, n])
                self.mean, self.shift = sb(f"{name}_mean", [P, n]), sb(f"{name}_shift", [P, n])
                self.arg, self.ln = sb(f"{name}_arg", [P, n]), sb(f"{name}_ln", [P, n])
                self.guess, self.root = sb(f"{name}_guess", [P, n]), sb(f"{name}_root", [P, n])
                self.by = sb(f"{name}_by", [P, n])

        first, second = Small("first", TC), Small("second", 32)

        bank = [ctx.enter_context(nc.psum_tensor(f"bank{i}", [P, 512], F32)) for i in range(8)]
        psT = [bank[0], bank[1]]
        psS = bank[2]
        psU = [bank[3], bank[4]]
        psY = [bank[5], bank[6]]
        psX = [[bank[3], bank[4]], [bank[5], bank[6]]]
        psK, psE, psQV = [bank[3], bank[4]], [bank[5], bank[6]], bank[7]
        dY = [bank[2], bank[3], bank[4], bank[5]]

        dve_step, act_step, pool_step = sem("dve_step"), sem("act_step"), sem("pool_step")
        passed = {nc.sync.engine: sem("sp_passed"), nc.gpsimd.engine: sem("pool_passed")}
        loaded = sem("loaded")
        bigs_ready, bigs_stored = sem("bigs_ready"), sem("bigs_stored")
        consts_ready = sem("consts_ready")
        tiles_set = sem("tiles_set")
        edges_ready = sem("edges_ready")
        firsts_done = sem("firsts_done")
        prep_done = sem("prep_done")
        arg_ready, root_ready = sem("arg_ready"), sem("root_ready")
        centre_ready, w1c_ready, w1x_done = sem("centre_ready"), sem("w1c_ready"), sem("w1x_done")
        row_entered = ring_sems("row_entered")
        row_found = ring_sems("row_found")
        d_loaded, d_stored = ring_sems("d_loaded", 2), ring_sems("d_stored", 2)
        d_arg, d_root = sem("d_arg"), sem("d_root")
        y_arg, y_root = sem("y_arg"), sem("y_root")
        d_turned, d_evac, d_mult, d_read = sem("d_turned"), sem("d_evac"), sem("d_mult"), sem("d_read")
        d_sq, d_scale, d_out = sem("d_sq"), sem("d_scale"), sem("d_out")
        v_loaded, xd_loaded = ring_sems("v_loaded"), ring_sems("xd_loaded")
        gathered, stored = ring_sems("gathered"), ring_sems("stored")

        class Round:

            def __init__(self, r):
                def s(name):
                    return sem(f"{name}{r}")
                turns = [len(range(k, CHUNKS, RING)) for k in range(RING)]
                seam = [int(k == CHUNKS % RING) for k in range(RING)]

                def ongoing(sems, per, seams):
                    return [(sems[k], sum(per[q] * turns[k] + seams[q] * seam[k] for q in range(r)))
                            for k in range(RING)]
                self.v_loaded = ongoing(v_loaded, [0, 16, 16, 16, 16], [0] * 5)
                self.xd_loaded = ongoing(xd_loaded, [0, 16, 16, 32, 32], [0, 16, 16, 32, 0])
                self.gathered = ongoing(gathered, [2 * 16 * C] + [16 * C] * 4, [16, 0, 0, 0, 0])
                self.stored = ongoing(stored, [16] * 4 + [0], [16] * 4 + [0])
                self.mask_ready = s("mask_ready")
                self.front = s("front")
                self.seam_added = s("seam_added")
                self.seam_total = s("seam_total")
                self.updated = s("updated")
                if r in (0, 1, 3, 4):
                    self.arg, self.root = s("arg"), s("root")
                if r != 2:
                    self.norm_ready = s("norm_ready")
                if r in (0, 1, 4):
                    self.turned, self.evac = s("turned"), s("evac")
                    self.groups = {0: 4, 1: 2, 4: 6}[r]
                if r in (3, 4):
                    self.scaled = s("scaled")
                if r in (0, 1):
                    self.am_ready, self.mult = s("am_ready"), s("mult")
                if r == 0:
                    self.x1_arg, self.x1_root = s("x1_arg"), s("x1_root")
                    self.squared = s("squared")
                    self.x1_norm = s("x1_norm")
                    self.plain_stored = ring_sems("plain_stored", 2)
                    self.deg_arg, self.deg_root = s("deg_arg"), s("deg_root")
                if r == 1:
                    self.relu_done, self.exp_ready = s("relu_done"), s("exp_ready")
                    self.z_ready, self.z_guess = s("z_ready"), s("z_guess")
                    self.msg_ready = s("msg_ready")
                if r == 4:
                    self.xb_ready = s("xb_ready")
                    self.q_mult, self.ke_mult, self.v_mult = s("q_mult"), s("ke_mult"), s("v_mult")
                    self.q_copied, self.v_copied, self.ke_read = s("q_copied"), s("v_copied"), s("ke_read")
                    self.score_ready, self.exp_ready = s("score_ready"), s("exp_ready")
                    self.msg_ready = s("msg_ready")
                    self.seam_loaded = s("seam_loaded")
                    self.head_entered = s("head_entered")
                    self.scattered = ring_sems("scattered")

        S = [Round(r) for r in ROUNDS]
        SEAM = Chunk(CHUNKS, RING, CHUNKS % RING, CHUNKS // RING + 1)

        def cols(r, c):
            if c is SEAM:
                return COLS
            return C * c.n if r < 4 else (COLS - C) - C * c.n

        def width(c):
            return 1 if c is SEAM else C

        def stand_alone(eng):
            if eng.engine in passed:
                eng.sem_inc(passed[eng.engine], 1)

        def done(eng, s, c, per=1, more=0):
            if c.exists:
                eng.wait_ge(s, (c.n + 1) * per + more)
                stand_alone(eng)

        def count(eng, s, value):
            if not isinstance(value, int) or value > 0:
                eng.wait_ge(s, value)
                stand_alone(eng)

        def used(eng, s, c, per=16):
            if c.exists:
                signal, base = s[c.slot] if isinstance(s[c.slot], tuple) else (s[c.slot], 0)
                eng.wait_ge(signal, c.turn * per + base)
                stand_alone(eng)

        block = ctx.enter_context(nc.Block())

        @block.sync
        def _(sp):
            sp.wait_ge(tiles_set, 1)
            sp.dma_start(src_i[0:EP, :], src.rearrange("(p t) -> p t", t=COLS)).then_inc(loaded, 16)
            sp.dma_start(dst_i[0:EP, 0:COLS], dst.rearrange("(p t) -> p t", t=COLS)).then_inc(loaded, 16)
            sp.dma_start(dst_i[0:EP - 1, COLS:TC],
                         dst.rearrange("(p t) -> p t", t=COLS)[1:EP, 0:1],
                         allow_slow_non_contiguous=True).then_inc(loaded, 16)
            for tile, lo, w, b in ((w0, 0, W0, b0), (w1, 0, W1, b1), (wkv, 0, Wk, bk), (wkv, D, Wv, bv),
                                   (wq, 0, Wq, bq), (we, 0, We, be)):
                sp.dma_start(tile[0:D, lo:lo + D], w).then_inc(loaded, 16)
                sp.dma_start(tile[D:D + 1, lo:lo + D], b.rearrange("(o d) -> o d", o=1)).then_inc(loaded, 16)
            sp.dma_start(b1c[:, :], b1.rearrange("(o d) -> o d", o=1).to_broadcast([P, D])).then_inc(loaded, 16)
            sp.wait_ge(bigs_ready, 1)
            sp.dma_start(row_of.rearrange("(p t) o -> p (t o)", p=EP), bigs[0:EP, :]).then_inc(bigs_stored, 16)

            xv = x[0:P * DCOLS, :].rearrange("(p t) d -> p t d", t=DCOLS)
            ov = out[0:P * DCOLS, :].rearrange("(p t) d -> p t d", t=DCOLS)

            def dense_store(c):
                done(sp, d_out, c)
                sp.dma_start(ov[:, bass.ds(c.n * DC, DC), :], DO[c.slot]).then_inc(d_stored[c.slot], 16)

            def dense_free(c):
                done(sp, d_arg, c)
                done(sp, d_turned, c, DG)

            def dense(c):
                dense_free(c.before(2))
                sp.dma_start(DX[c.slot][:, :, :], xv[:, bass.ds(c.n * DC, DC), :]).then_inc(d_loaded[c.slot], 16)
                if c.before(2).exists:
                    dense_store(c.before(2))

            each_chunk(sp, DCHUNKS, 2, dense)
            last = Chunk(DCHUNKS, 2, DCHUNKS % 2, DCHUNKS // 2 + 1)
            dense_free(last.before(2))
            sp.dma_start(DX[last.slot][0:DRP, 0:2, :],
                         x[P * DCOLS:N, :].rearrange("(p t) d -> p t d", t=2)).then_inc(d_loaded[last.slot], 16)
            dense_store(last.before(2))
            dense_store(last.before(1))
            done(sp, d_out, last)
            sp.dma_start(out[P * DCOLS:N, :].rearrange("(p t) d -> p t d", t=2),
                         DO[last.slot][0:DRP, 0:2, :]).then_inc(d_stored[last.slot], 16)

            ea = edge_attr.rearrange("(p t) d -> p t d", t=COLS)

            def store(r, c):
                s = S[r]
                at, w = cols(r, c), width(c)
                done(sp, s.updated, c)
                sp.dma_start(table_v[r + 1][:, bass.ds(at, w), :], OT[c.slot][:, 0:w, :]).then_inc(s.stored[c.slot][0], 16)
                if r == 0 and c is not SEAM:
                    for rr, tile in ((1, PL1), (2, PL2), (4, PL4)):
                        sp.dma_start(plain[rr][:, bass.ds(at, C), :],
                                     tile[c.parity]).then_inc(s.plain_stored[c.parity], 16)

            def load(r, c):
                s, old = S[r], c.before(RING)
                at = cols(r, c)
                if c is not SEAM:
                    if r in (2, 3):
                        done(sp, s.front, old)
                        done(sp, s.seam_added, old)
                    if r == 1:
                        done(sp, s.relu_done, old)
                    if r == 4:
                        done(sp, s.turned, old, 6)
                    sp.dma_start(V[c.slot][:, :, 0:D], plain[{1: 1, 2: 2, 3: 2, 4: 4}[r]][:, bass.ds(at, C), :]
                                 ).then_inc(s.v_loaded[c.slot][0], 16)
                if r < 4 or c is not SEAM:
                    if r == 4:
                        done(sp, s.scaled, old)
                    else:
                        done(sp, s.updated, old)
                    w = width(c)
                    sp.dma_start(XD[c.slot][:, 0:w, :], table_v[r][:, bass.ds(at, w), :]
                                 ).then_inc(s.xd_loaded[c.slot][0], 16)
                    if r == 3:
                        sp.dma_start(XE[c.slot][:, 0:w, :], table_v[2][:, bass.ds(at, w), :]
                                     ).then_inc(s.xd_loaded[c.slot][0], 16)
                    if r == 4:
                        sp.dma_start(XE[c.slot][0:EP, :, :], ea[:, bass.ds(at, C), :]
                                     ).then_inc(s.xd_loaded[c.slot][0], 16)

            for r in ROUNDS:
                if r:
                    for k in range(RING):
                        signal, base = S[r - 1].stored[k]
                        sp.wait_ge(signal, base + 16 * len(range(k, CHUNKS + 1, RING)))
                    if r == 1:
                        for k in range(2):
                            sp.wait_ge(S[0].plain_stored[k], 16 * 3 * len(range(k, CHUNKS, 2)))
                if r == 4:
                    sp.wait_ge(S[4].head_entered, 16)
                    seam_rows = table_v[4][:, COLS:TC, :].rearrange("p t d -> p (t d)")
                    sp.dma_start(xseam[:, :], seam_rows).then_inc(S[4].seam_loaded, 16)
                    sp.dma_start(xnext[0:P - 1, :], seam_rows[1:P, :]).then_inc(S[4].seam_loaded, 16)

                def step(c):
                    if r:
                        load(r, c)
                    if r < 4 and c.before(4).exists:
                        store(r, c.before(4))

                each_chunk(sp, CHUNKS, RING, step)
                if r:
                    load(r, SEAM)
                if r < 4:
                    for k in (4, 3, 2, 1):
                        store(r, SEAM.before(k))
                    store(r, SEAM)
            for k in range(2):
                sp.wait_ge(d_stored[k], 16 * len(range(k, DCHUNKS + 1, 2)))
            for k in range(RING):
                full, seams = len(range(k, CHUNKS, RING)), int(k == SEAM.slot)
                sp.wait_ge(S[4].scattered[k], 16 * (C * full + seams))

        @block.gpsimd
        def _(pool):
            me = Steps(pool, pool_step)
            last_node, last_entry = pool.to_reg(N - 1), pool.to_reg(P * TC - 1)
            me.mark(pool.memset(src_i[:, :], 0))
            me.wait()
            pool.memset(dst_i[:, :], BIG).then_inc(tiles_set, 1)
            pool.wait_ge(tiles_set, 1)
            pool.memset(bigs[:, :], BIG).then_inc(bigs_ready, 1)
            pool.wait_ge(bigs_ready, 1)
            me.mark(pool.memset(ident[:, :], 0.0))
            me.wait()
            me.mark(pool.iota(rowid[:, :], pattern=[[1, TC]], base=0, channel_multiplier=TC))
            me.wait()
            pool.affine_select(out=ident[:, :], in_=ident[:, :], compare_op=ALU.not_equal, fill=1.0, base=0,
                               pattern=[[-1, P]], channel_multiplier=1).then_inc(consts_ready, 1)

            def stage(to, of, at, w):
                me.mark(pool.tensor_copy(to[:, 0:w], of[:, bass.ds(at, w)]))

            pool.wait_ge(edges_ready, 1)
            pool.wait_ge(bigs_stored, 16)

            def enter_rows(c):
                at, w = cols(0, c), width(c)
                used(pool, row_entered, c.before(RING), 16 * C)
                stage(idx[c.slot], rep_i, at, w)
                stage(rid[c.slot], rowid, at, w)
                me.wait()
                stand_alone(pool)
                for j in range(w):
                    pool.indirect_dma_start(
                        out=row_of, out_offset=bass.IndirectOffsetOnAxis(ap=idx[c.slot][:, j:j + 1], axis=0),
                        in_=rid[c.slot][:, j:j + 1], in_offset=None, bounds_check=last_node,
                        oob_is_err=False).then_inc(row_entered[c.slot], 16)

            each_chunk(pool, CHUNKS, RING, enter_rows, [me])
            enter_rows(SEAM)
            for k in range(RING):
                pool.wait_ge(row_entered[k], 16 * (C * len(range(k, CHUNKS, RING)) + int(k == SEAM.slot)))

            def keep_rows(c):
                used(pool, row_found, c, 16 * C)
                me.mark(pool.tensor_copy(src_row[:, bass.ds(cols(0, c), C)], rst[c.slot][:, :]))

            def find_rows(c):
                stage(idx[c.slot], src_i, cols(0, c), C)
                me.wait()
                stand_alone(pool)
                for j in range(C):
                    pool.indirect_dma_start(
                        out=rst[c.slot][:, j:j + 1], out_offset=None, in_=row_of,
                        in_offset=bass.IndirectOffsetOnAxis(ap=idx[c.slot][:, j:j + 1], axis=0),
                        bounds_check=last_node, oob_is_err=False).then_inc(row_found[c.slot], 16)
                if c.before(1).exists:
                    keep_rows(c.before(1))

            each_chunk(pool, CHUNKS, RING, find_rows, [me])
            keep_rows(SEAM.before(1))

            def gather(c, w, to, indices, at, of, last_row, ix, signal):
                stage(ix[c.slot], indices, at, w)
                me.wait()
                stand_alone(pool)
                for j in range(w):
                    pool.indirect_dma_start(
                        out=to[c.slot][:, j, 0:D], out_offset=None, in_=of,
                        in_offset=bass.IndirectOffsetOnAxis(ap=ix[c.slot][:, j:j + 1], axis=0),
                        bounds_check=last_row, oob_is_err=False).then_inc(signal[c.slot][0], 16)

            def gather_x(c):
                s, old = S[0], c.before(RING)
                done(pool, s.front, old)
                done(pool, s.seam_added, old)
                gather(c, C, V, src_i, cols(0, c), x, last_node, idx, s.gathered)
                done(pool, s.updated, old)
                gather(c, C, XD, dst_i, cols(0, c), x, last_node, idx2, s.gathered)

            each_chunk(pool, CHUNKS, RING, gather_x, [me])
            done(pool, S[0].updated, SEAM.before(RING))
            gather(SEAM, 1, XD, dst_i, 0, x, last_node, idx2, S[0].gathered)

            def scatter(c):
                s, at, w = S[4], cols(4, c), width(c)
                done(pool, s.updated, c)
                used(pool, s.scattered, c.before(RING), 16 * C)
                stage(idx2[c.slot], out_i, at, w)
                me.wait()
                stand_alone(pool)
                for j in range(w):
                    pool.indirect_dma_start(
                        out=out, out_offset=bass.IndirectOffsetOnAxis(ap=idx2[c.slot][:, j:j + 1], axis=0),
                        in_=OT[c.slot][:, j, :], in_offset=None, bounds_check=last_node,
                        oob_is_err=False).then_inc(s.scattered[c.slot], 16)

            for r in range(1, 5):
                for k in range(RING):
                    signal, base = S[r - 1].stored[k]
                    pool.wait_ge(signal, base + 16 * len(range(k, CHUNKS + 1, RING)))
                if r == 4:
                    stand_alone(pool)
                    pool.indirect_dma_start(
                        out=table[4], out_offset=bass.IndirectOffsetOnAxis(ap=head_row[:, 0:1], axis=0),
                        in_=OT[SEAM.slot][:, 0, :], in_offset=None, bounds_check=last_entry,
                        oob_is_err=False).then_inc(S[4].head_entered, 16)
                    pool.wait_ge(S[4].head_entered, 16)
                    for k in range(2):
                        pool.wait_ge(d_stored[k], 16 * len(range(k, DCHUNKS + 1, 2)))

                def step(c):
                    used(pool, S[r].v_loaded, c)
                    gather(c, C, V, src_row, cols(r, c), table[r], last_entry, idx, S[r].gathered)
                    if r == 4 and c.before(3).exists:
                        scatter(c.before(3))

                each_chunk(pool, CHUNKS, RING, step, [me])
            for k in (3, 2, 1):
                scatter(SEAM.before(k))
            scatter(SEAM)

        def groups(n):
            return [(g, g * G, min(G, n - g * G)) for g in range(-(-n // G))]

        def by_rows(psum, m):
            return psum[:, 0:m * D].rearrange("p (m d) -> p m d", d=D)

        def plain_free(eng, s, c):
            old = c.before(2)
            if old.exists:
                turn = old.n // 2 + 1 if isinstance(old.n, int) else (c.turn - 1) * 2 + (c.slot - 2) // 2 + 1
                eng.wait_ge(s.plain_stored[old.parity], turn * 48)

        @block.tensor
        def _(pe):
            pe.wait_ge(consts_ready, 1)
            pe.wait_ge(edges_ready, 1)
            pe.matmul(psS[:, 0:P], ones[:, :], MB[0][:, 0, :], start=True, stop=True).then_inc(firsts_done, 1)
            pe.wait_ge(w1c_ready, 1)
            pe.matmul(psQV[0:D, 0:D], centre[0:D, :], w1c[0:D, :], start=True, stop=True).then_inc(w1x_done, 1)

            def turn(to, of, n):
                for j in range(n):
                    last = pe.transpose(to[0:D, j * P:(j + 1) * P], of[:, j, :], ident[:, :])
                return last

            def times(to, xt, w, n, k=D + 1):
                for j in range(n):
                    last = pe.matmul(to[:, j * D:(j + 1) * D], xt[0:k, j * P:(j + 1) * P], w[0:k, :],
                                     start=True, stop=True)
                return last

            def keep_warm(n):
                for _ in range(n):
                    pe.transpose(psQV[:, 0:P], ident[:, :], ident[:, :])

            pe.wait_ge(prep_done, 1)

            def dense(c, n=DC):
                used(pe, d_loaded, c)
                parts = groups(n)
                for g, at, m in parts:
                    i = c.n * DG + g
                    count(pe, d_evac, i - 1)
                    turn(psT[g % 2], DX[c.slot][:, at:at + m, :], m).then_inc(d_turned, 1)
                    keep_warm(4)
                    if g:
                        multiply(c, *parts[g - 1])
                multiply(c, *parts[-1])

            def multiply(c, g, at, m):
                i = c.n * DG + g
                pe.wait_ge(d_evac, i + 1)
                count(pe, d_read, i - 3)
                times(dY[g % 4], XT[g % 4], w1x, m, D).then_inc(d_mult, 1)

            each_chunk(pe, DCHUNKS, 2, dense)
            dense(Chunk(DCHUNKS, 2, DCHUNKS % 2, DCHUNKS // 2 + 1), 2)

            def seam(r, c, values, w):
                s = S[r]
                done(pe, s.mask_ready, c)
                for j in range(C):
                    first_of_all = isinstance(c.n, int) and c.n == 0 and j == 0
                    last = pe.matmul(psS[:, 0:w], MB[c.parity][:, j, :], values[:, j, 0:w], start=first_of_all, stop=False)
                last.then_inc(s.seam_added, 1)

            for r in ROUNDS:
                s = S[r]
                w = {0: D + 1, 1: 2 * D, 2: D, 3: D, 4: W4}[r]

                def turn_groups(c, q, of, n):
                    for g, at, m in groups(n):
                        count(pe, s.evac, c.n * s.groups + q + g - 1)
                        turn(psT[(q + g) % 2], of[:, at:at + m, 0:D], m).then_inc(s.turned, 1)

                def evacuated(c, q):
                    pe.wait_ge(s.evac, c.n * s.groups + q + 1)

                def am(c):
                    n = width(c)
                    if not c.exists:
                        return
                    done(pe, s.am_ready, c)
                    turn_groups(c, 0, AM[c.parity], n)
                    if r == 0:
                        done(pe, s.arg, c.before(1))
                        for g, at, m in groups(n):
                            evacuated(c, g)
                            times(psU[g], XT[g], w0, m).then_inc(s.mult, 1)
                        return
                    for g, at, m in groups(n):
                        to = psX[c.parity][g]
                        evacuated(c, g)
                        for j in range(m):
                            last = pe.matmul(to[:, j * D:(j + 1) * D], XT[g][0:D + 1, j * P:(j + 1) * P], w1[0:D + 1, :],
                                             start=False, stop=j == m - 1)
                        last.then_inc(s.mult, 1)

                def dst_rows(c):
                    used(pe, s.xd_loaded, c)
                    done(pe, s.updated, c.before(2))
                    for g, at, m in groups(width(c)):
                        pe.matmul(psX[c.parity][g][:, 0:m * D], ident[:, :],
                                  XD[c.slot][:, at:at + m, :].rearrange("p m d -> p (m d)"), start=True, stop=False)

                def x1(c):
                    done(pe, s.front, c)
                    turn_groups(c, 2, PL1[c.parity], C)
                    done(pe, s.norm_ready, c.before(1))
                    for g, at, m in groups(C):
                        evacuated(c, 2 + g)
                        times(psY[g], XT[2 + g], w1c, m).then_inc(s.mult, 1)
                    seam(r, c, V[c.slot], w)

                def attend(c):
                    used(pe, s.gathered, c, 16 * C)
                    turn_groups(c, 0, V[c.slot], C)
                    used(pe, s.xd_loaded, c, 32)
                    turn_groups(c, 2, XE[c.slot], C)
                    done(pe, s.xb_ready, c)
                    turn_groups(c, 4, XB[c.parity], C)
                    done(pe, s.ke_read, c.before(1), 2)
                    for g, at, m in groups(C):
                        if g == 0:
                            done(pe, s.v_copied, c.before(1), 2)
                        else:
                            pe.wait_ge(s.q_copied, c.n * 2 + g)
                        evacuated(c, 4 + g)
                        times(psQV, XT[4 + g], wq, m).then_inc(s.q_mult, 1)
                        times(psK[g], XT[g], wkv[:, 0:D], m)
                        times(psE[g], XT[2 + g], we, m).then_inc(s.ke_mult, 1)
                    for g, at, m in groups(C):
                        if g == 0:
                            done(pe, s.q_copied, c, 2)
                        else:
                            pe.wait_ge(s.v_copied, c.n * 2 + g)
                        times(psQV, XT[g], wkv[:, D:2 * D], m).then_inc(s.v_mult, 1)

                def attended(c):
                    if c.exists:
                        done(pe, s.msg_ready, c)
                        seam(r, c, MS[c.parity], w)

                def step(c):
                    if r == 0:
                        am(c)
                        x1(c)
                    if r == 1:
                        am(c.before(1))
                        done(pe, s.msg_ready, c)
                        seam(r, c, MS[c.parity], w)
                        dst_rows(c)
                    if r in (2, 3):
                        done(pe, s.front, c)
                        seam(r, c, V[c.slot], w)
                    if r == 4:
                        attended(c.before(2))
                        attend(c)

                each_chunk(pe, CHUNKS, RING, step)
                final = SEAM.before(1)
                if r == 4:
                    attended(SEAM.before(2))
                    attended(final)
                if r == 1:
                    am(final)
                done(pe, s.updated, final)
                if r < 4:
                    pe.matmul(psS[:, 0:w], eq_tail[:, :], AG[final.parity][:, C - 1, 0:w], start=False,
                              stop=True).then_inc(s.seam_total, 1)
                else:
                    pe.matmul(psS[:, 0:w], eq_head[:, :], AG[final.parity][:, 0, 0:w], start=False,
                              stop=True).then_inc(s.seam_total, 1)
                if r == 1:
                    dst_rows(SEAM)
                if r in (0, 1):
                    am(SEAM)

        @block.scalar
        def _(act):
            me = Steps(act, act_step)
            act.preload_act_table_set("natural_log_exp_and_others")

            def root(sm, n, signal):
                me.mark(act.activation(sm.ln[:, 0:n], sm.arg[:, 0:n], ACT.Ln))
                me.wait()
                act.activation(sm.guess[:, 0:n], sm.ln[:, 0:n], ACT.Exp, scale=-0.5).then_inc(signal, 1)

            act.wait_ge(arg_ready, 1)
            root(first, COLS, root_ready)

            def dense_turned(c, parts):
                for g, at, m in parts:
                    i = c.n * DG + g
                    act.wait_ge(d_turned, i + 1)
                    count(act, d_mult, i - 3)
                    act.activation(XT[g % 4][0:D, 0:m * P], psT[g % 2][0:D, 0:m * P], ACT.Copy).then_inc(d_evac, 1)

            def dense_root(c, n=DC):
                if c.exists:
                    done(act, y_arg, c)
                    root(second, n, y_root)

            OUT = 4

            def dense_out(c, lo, n, signal=None):
                for j in range(lo, min(lo + n, DC if c is not last_dense else 2)):
                    last = act.activation(DO[c.slot][:, j, :], DY[c.slot][:, j, :], ACT.Copy,
                                          scale=second.root[:, j:j + 1])
                if signal:
                    last.then_inc(signal, 1)

            def dense_square(c, n=DC):
                act.wait_ge(d_read, c.n * DG + len(groups(n)))
                act.activation(DSQ[:, 0:n, :], DY[c.slot][:, 0:n, :], ACT.Square).then_inc(d_sq, 1)

            def dense(c, n=DC):
                parts, old = groups(n), c.before(1)
                dense_turned(c, parts[:2])
                if old.exists:
                    dense_square(old)
                done(act, d_arg, c)
                root(first, n, d_root)
                dense_turned(c, parts[2:4])
                dense_root(old)
                if old.exists:
                    done(act, d_scale, old)
                    used(act, d_stored, old.before(2))
                for g, at, m in parts[4:]:
                    dense_turned(c, [(g, at, m)])
                    if old.exists:
                        dense_out(old, OUT * (g - 4), OUT)
                if old.exists:
                    dense_out(old, OUT * max(len(parts) - 4, 0), DC, d_out)

            last_dense = Chunk(DCHUNKS, 2, DCHUNKS % 2, DCHUNKS // 2 + 1)
            each_chunk(act, DCHUNKS, 2, dense, [me])
            dense(last_dense, 2)
            dense_square(last_dense, 2)
            dense_root(last_dense, 2)
            done(act, d_scale, last_dense)
            used(act, d_stored, last_dense.before(2))
            dense_out(last_dense, 0, 2, d_out)
            for k in range(2):
                act.wait_ge(d_stored[k], 16 * len(range(k, DCHUNKS + 1, 2)))

            def masks(r, c):
                s = S[r]
                m, eq = (head, eq_head) if r < 4 else (tail, eq_tail)
                done(act, s.seam_added, c.before(2))
                me.mark(act.activation(mc[c.parity][:, :], m[:, bass.ds(cols(r, c), C)], ACT.Copy))
                me.wait()
                for j in range(C):
                    last = act.activation(MB[c.parity][:, j, :], eq[:, :], ACT.Copy, scale=mc[c.parity][:, j:j + 1])
                last.then_inc(s.mask_ready, 1)

            for r in ROUNDS:
                s = S[r]

                if r:
                    act.wait_ge(S[r - 1].seam_total, 1)

                def evac(c, q, n):
                    for g, at, m in groups(n):
                        i = c.n * s.groups + q + g
                        act.wait_ge(s.turned, i + 1)
                        if r == 4:
                            done(act, s.v_mult, c.before(1), 2)
                        else:
                            count(act, s.mult, i - s.groups + 1)
                        act.activation(XT[q + g][0:D, 0:m * P], psT[(q + g) % 2][0:D, 0:m * P], ACT.Copy).then_inc(s.evac, 1)

                def root_of(c):
                    if c.exists:
                        done(act, s.arg, c)
                        root(second, 3 * C if r == 0 and c is not SEAM else width(c), s.root)

                def normalise(c):
                    if c.exists:
                        done(act, s.norm_ready, c)
                        used(act, s.scattered if r == 4 else s.stored, c.before(RING), 16 * C if r == 4 else 16)
                        lo = 2 * C if r == 0 and c is not SEAM else 0
                        by = second.by if r == 1 else second.root
                        for j in range(width(c)):
                            row = UB[c.parity][:, j, :] if r != 1 else psX[c.parity][j // G][:, j % G * D:(j % G + 1) * D]
                            last = act.activation(OT[c.slot][:, j, :], row, ACT.Identity,
                                                  scale=by[:, lo + j:lo + j + 1], bias=second.shift[:, lo + j:lo + j + 1])
                        last.then_inc(s.updated, 1)

                def plain1(c):
                    done(act, s.x1_norm, c)
                    done(act, s.turned, c.before(2), 4)
                    plain_free(act, s, c)
                    for j in range(C):
                        last = act.activation(PL1[c.parity][:, j, :], V[c.slot][:, j, 0:D], ACT.Identity,
                                              scale=first.root[:, j:j + 1], bias=first.shift[:, j:j + 1])
                    last.then_inc(s.front, 1)

                def exponents(c):
                    used(act, s.gathered, c, 16 * C)
                    done(act, s.msg_ready, c.before(2))
                    done(act, s.seam_added, c.before(2))
                    act.activation(MM[c.parity][:, :, :], V[c.slot][:, :, 0:D], ACT.Relu).then_inc(s.relu_done, 1)
                    done(act, s.relu_done, c)
                    act.activation(MS[c.parity][:, :, D:2 * D], MM[c.parity][:, :, :], ACT.Exp
                                   ).then_inc(s.exp_ready, 1)

                def inverse(c, sums):
                    n = width(c)
                    done(act, s.z_ready, c)
                    me.mark(act.activation(LZ[:, 0:n, :], sums[:, 0:n, D:2 * D], ACT.Ln))
                    me.wait()
                    act.activation(GZ[:, 0:n, :], LZ[:, 0:n, :], ACT.Exp, scale=-1.0).then_inc(s.z_guess, 1)

                def layer2_rows(c):
                    n, b = width(c), c.parity
                    done(act, s.arg, c.before(2))
                    me.mark(act.activation(oc[b][:, 0:n], sdeg[:, bass.ds(cols(r, c), n)], ACT.Copy))
                    used(act, s.xd_loaded, c, 32)
                    me.wait()
                    for j in range(n):
                        last = act.activation(MM[b][:, j, :], XE[c.slot][:, j, :], ACT.Copy, scale=oc[b][:, j:j + 1])
                    last.then_inc(s.scaled, 1)

                def own_rows(c):
                    done(act, s.xb_ready, c.before(2))
                    me.mark(act.activation(oc[c.parity][:, :], own[:, bass.ds(cols(r, c), C)], ACT.Copy))
                    used(act, s.xd_loaded, c, 32)
                    me.wait()
                    for j in range(C):
                        last = act.activation(XA[c.parity][:, j, :], XD[c.slot][:, j, :], ACT.Copy, scale=oc[c.parity][:, j:j + 1])
                    last.then_inc(s.scaled, 1)

                def step(c):
                    if r == 0:
                        done(act, s.x1_arg, c)
                        root(first, C, s.x1_root)
                        evac(c, 0, C)
                        root_of(c.before(1))
                        plain1(c)
                        evac(c, 2, C)
                        normalise(c.before(1))
                        for g, at, m in groups(C):
                            act.wait_ge(s.mult, c.n * 4 + 3 + g)
                            squared = act.activation(SQ[:, at:at + m, :], by_rows(psY[g], m), ACT.Square)
                        squared.then_inc(s.squared, 1)
                        masks(r, c)
                    if r == 1:
                        exponents(c)
                        if c.before(1).exists:
                            evac(c.before(1), 0, C)
                        masks(r, c)
                        inverse(c, AG[c.parity])
                        normalise(c.before(2))
                        root_of(c.before(1))
                    if r == 2:
                        masks(r, c)
                    if r == 3:
                        normalise(c.before(2))
                        layer2_rows(c)
                        root_of(c.before(1))
                        masks(r, c)
                    if r == 4:
                        root_of(c.before(2))
                        exponent(c.before(1))
                        if not isinstance(c.n, int) or c.n + 1 < CHUNKS:
                            own_rows(c.after())
                        evac(c, 0, C)
                        evac(c, 2, C)
                        evac(c, 4, C)
                        done(act, s.msg_ready, c.before(2))
                        copied(c, 0, s.q_mult, QS, s.q_copied)
                        normalise(c.before(2))
                        copied(c, 1, s.q_mult, QS, s.q_copied)
                        masks(r, c)
                        copied(c, 0, s.v_mult, VS, s.v_copied)
                        copied(c, 1, s.v_mult, VS, s.v_copied)

                def copied(c, g, written, to, signal):
                    act.wait_ge(written, c.n * 2 + g + 1)
                    act.activation(to[c.parity][:, g * G:(g + 1) * G, :], by_rows(psQV, G), ACT.Copy).then_inc(signal, 1)

                def exponent(c):
                    if c.exists:
                        done(act, s.score_ready, c)
                        done(act, s.seam_added, c.before(2))
                        act.activation(MS[c.parity][:, :, D:W4], SC2[:, :, :], ACT.Exp).then_inc(s.exp_ready, 1)

                if r == 4:
                    own_rows(Chunk(0, RING, 0, 1))
                each_chunk(act, CHUNKS, RING, step, [me])
                final = SEAM.before(1)
                if r == 4:
                    root_of(SEAM.before(2))
                    exponent(final)
                if r == 1:
                    evac(final, 0, C)
                if r in (1, 3, 4):
                    normalise(SEAM.before(2))
                if r != 2:
                    root_of(final)
                    normalise(final)
                if r == 3:
                    layer2_rows(SEAM)
                if r == 0:
                    act.wait_ge(s.deg_arg, 1)
                    root(first, 1, s.deg_root)
                if r == 1:
                    inverse(SEAM, SG)
                if r in (0, 1):
                    evac(SEAM, 0, 1)
                if r != 2:
                    root_of(SEAM)
                    normalise(SEAM)

        @block.vector
        def _(dve):
            me = Steps(dve, dve_step)

            def wide(a, at, n, w=D):
                return a[:, bass.ds(at, n)].unsqueeze(2).to_broadcast([P, n, w])

            def stats(sm, rows, n, lo=0):
                me.wait()
                for j in range(n):
                    last = dve.bn_stats(out=sm.st[:, j, :], in_=rows[:, j, 0:D])
                me.mark(last)
                return variance(sm, n, lo)

            def variance(sm, n, lo=0):
                me.wait()
                even, odd = sm.st[:, 0:n, 1], sm.st[:, 0:n, 4]
                me.mark(dve.tensor_tensor(sm.t[:, 0, 0:n], even, odd, ALU.subtract))
                me.mark(dve.tensor_tensor(sm.mean[:, lo:lo + n], even, odd, ALU.add))
                me.mark(dve.scalar_tensor_tensor(out=sm.t[:, 1, 0:n], in0=sm.st[:, 0:n, 2], scalar=D * EPS,
                                                 in1=sm.st[:, 0:n, 5], op0=ALU.add, op1=ALU.add))
                me.wait(but=2)
                me.mark(dve.scalar_tensor_tensor(out=sm.t[:, 2, 0:n], in0=sm.t[:, 0, 0:n], scalar=0.25,
                                                 in1=sm.t[:, 0, 0:n], op0=ALU.mult, op1=ALU.mult))
                me.wait()
                return dve.scalar_tensor_tensor(out=sm.arg[:, lo:lo + n], in0=sm.t[:, 1, 0:n], scalar=1.0 / D,
                                                in1=sm.t[:, 2, 0:n], op0=ALU.mult, op1=ALU.add)

            def refine(sm, n, signal, value):
                dve.wait_ge(signal, value)
                me.wait()
                me.mark(dve.tensor_tensor(sm.t[:, 3, 0:n], sm.guess[:, 0:n], sm.guess[:, 0:n], ALU.mult))
                me.wait()
                me.mark(dve.scalar_tensor_tensor(out=sm.t[:, 4, 0:n], in0=sm.t[:, 3, 0:n], scalar=-0.5,
                                                 in1=sm.arg[:, 0:n], op0=ALU.mult, op1=ALU.mult))
                me.wait()
                return dve.scalar_tensor_tensor(out=sm.root[:, 0:n], in0=sm.t[:, 4, 0:n], scalar=1.5,
                                                in1=sm.guess[:, 0:n], op0=ALU.add, op1=ALU.mult)

            me.mark(dve.memset(ones[:, :], 1.0))
            for k in range(6):
                me.mark(dve.memset(XT[k][D:D + 1, :], 1.0))
            for k in range(RING):
                me.mark(dve.memset(V[k][:, :, D:D + 1], 1.0))
                me.mark(dve.memset(XD[k][:, :, :], 0.0))
                me.mark(dve.memset(XE[k][:, :, :], 0.0))
            me.mark(dve.memset(xnext[:, :], 0.0))
            dve.wait_ge(loaded, 16 * 16)
            dve.wait_ge(consts_ready, 1)
            me.mark(dve.tensor_copy(dst_f[:, :], dst_i[:, :]))
            me.mark(dve.tensor_scalar(centre[0:D, :], ident[0:D, 0:D], -1.0 / D, None, ALU.add))
            me.mark(dve.tensor_tensor(w1c[0:D, :], w1[0:D, :], ident[0:D, 0:D], ALU.add))
            me.mark(dve.tensor_copy(w1c[D:D + 1, :], w1[D:D + 1, :]))
            me.mark(dve.tensor_reduce(second.t[:, 0, 0:1], b1c[:, :], AX, ALU.add))
            me.wait()
            me.mark(dve.tensor_reduce(wsum[0:D + 1, :], w1c[0:D + 1, :], AX, ALU.add))
            me.mark(dve.tensor_scalar(second.t[:, 1, 0:1], second.t[:, 0, 0:1], 1.0 / D, None, ALU.mult))
            me.wait()
            me.mark(dve.tensor_scalar(b1c[:, :], b1c[:, :], second.t[:, 1, 0:1], None, ALU.subtract))
            me.mark(dve.tensor_scalar(second.t[0:D + 1, 2, 0:1], wsum[0:D + 1, :], 1.0 / D, None, ALU.mult))
            me.wait()
            me.send(dve.tensor_scalar(w1c[0:D + 1, :], w1c[0:D + 1, :], second.t[0:D + 1, 2, 0:1], None,
                                      ALU.subtract), w1c_ready, 1)
            me.wait()
            d, d0, dn = dst_f[:, 0:COLS], dst_f[:, 0:1], dst_f[:, COLS:TC]
            me.mark(dve.memset(keep_fwd[:, 0:1], 0.0))
            me.mark(dve.memset(keep_rev[:, COLS - 1:COLS], 0.0))
            me.mark(dve.tensor_tensor(keep_fwd[:, 1:COLS], dst_f[:, 1:COLS], dst_f[:, 0:COLS - 1], ALU.is_equal))
            me.mark(dve.tensor_tensor(keep_rev[:, 0:COLS - 1], dst_f[:, 0:COLS - 1], dst_f[:, 1:COLS], ALU.is_equal))
            me.mark(dve.tensor_scalar(head[:, :], d, d0, None, ALU.is_equal))
            me.mark(dve.tensor_scalar(tail[:, :], d, dst_f[:, COLS - 1:COLS], None, ALU.is_equal))
            me.mark(dve.tensor_scalar(MB[0][:, 0, :], ident[:, :], d0, None, ALU.mult))
            me.mark(dve.tensor_tensor(tmp_a[:, 0:COLS], d, dst_f[:, 1:TC], ALU.not_equal))
            me.mark(dve.tensor_scalar(tmp_b[:, 0:COLS], d, d0, None, ALU.not_equal))
            me.wait()
            me.mark(dve.tensor_tensor(own[:, :], tmp_a[:, 0:COLS], tmp_b[:, 0:COLS], ALU.mult))
            me.wait()
            me.mark(dve.tensor_scalar(tmp_b[:, 0:COLS], d, float(-BIG), None, ALU.add))
            me.wait()
            me.mark(dve.tensor_tensor(tmp_a[:, 0:COLS], tmp_b[:, 0:COLS], own[:, :], ALU.mult))
            me.mark(dve.tensor_tensor(first.t[:, 0, 0:1], d0, dn, ALU.not_equal))
            me.wait()
            me.mark(dve.tensor_tensor(tmp_a[:, COLS:TC], tmp_b[:, 0:1], first.t[:, 0, 0:1], ALU.mult))
            me.wait()
            me.mark(dve.tensor_scalar(rep_i[:, :], tmp_a[:, :], float(BIG), None, ALU.add))
            me.wait()
            me.mark(dve.tensor_scalar(first.t[:, 1, 0:COLS], d, dn, None, ALU.not_equal))
            me.mark(dve.tensor_scalar(first.t[:, 2, 0:COLS], keep_fwd[:, :], -1.0, 1.0, ALU.mult, ALU.add))
            me.wait()
            me.mark(dve.tensor_tensor(first.t[:, 3, 0:COLS], first.t[:, 1, 0:COLS], first.t[:, 2, 0:COLS], ALU.mult))
            me.wait()
            me.mark(dve.tensor_tensor(tmp_a[:, 0:COLS], tmp_b[:, 0:COLS], first.t[:, 3, 0:COLS], ALU.mult))
            me.wait()
            me.mark(dve.memset(tmp_a[:, 0:1], 0.0))
            me.wait()
            me.mark(dve.tensor_scalar(out_i[:, :], tmp_a[:, :], float(BIG), None, ALU.add))
            me.wait()
            me.send(dve.tensor_copy(first.t[:, 4, 0:1], d0), edges_ready, 1)
            me.mark(dve.tensor_copy(tmp_a[:, 0:COLS], head[:, :]))
            me.mark(dve.tensor_reduce(second.t[:, 3, 0:1], head[:, :], AX, ALU.add))
            me.mark(dve.tensor_copy(second.t[:, 4, 0:1], rowid[:, 0:1]))
            me.wait()
            me.mark(dve.tensor_tensor(tmp_a[:, 0:COLS - 1], head[:, 0:COLS - 1], head[:, 1:COLS], ALU.subtract))
            me.mark(dve.scalar_tensor_tensor(out=head_row[:, :], in0=second.t[:, 3, 0:1], scalar=-1.0,
                                             in1=second.t[:, 4, 0:1], op0=ALU.add, op1=ALU.add))
            me.wait()
            me.mark(dve.tensor_tensor(own[:, :], own[:, :], tmp_a[:, 0:COLS], ALU.add))
            me.wait()
            me.mark(dve.tensor_scalar(pull[:, :], own[:, :], -1.0, 1.0, ALU.mult, ALU.add))
            dve.wait_ge(firsts_done, 1)
            me.mark(dve.tensor_scalar(eq_head[:, :], psS[:, 0:P], d0, None, ALU.is_equal))
            me.mark(dve.tensor_scalar(MB[1][:, 0, :], psS[:, 0:P], dst_f[:, COLS - 1:COLS], None, ALU.is_equal))
            me.mark(dve.tensor_tensor(first.t[:, 5, 0:1], dst_f[:, COLS - 1:COLS], d0, ALU.not_equal))
            me.wait()
            me.mark(dve.tensor_scalar(eq_tail[:, :], MB[1][:, 0, :], first.t[:, 5, 0:1], None, ALU.mult))
            me.mark(dve.memset(first.t[:, 0, :], 1.0))
            me.mark(dve.memset(deg[:, COLS:TC], 1.0))
            me.wait()
            me.mark(dve.tensor_tensor_scan(deg[:, 0:COLS], keep_fwd[:, :], first.t[:, 0, 0:COLS], 0.0,
                                           ALU.mult, ALU.add))

            def degree_values(at, n):
                rs = first.root
                me.wait()
                me.mark(dve.reciprocal(rdeg[:, at:at + n], deg[:, at:at + n]))
                me.mark(dve.tensor_copy(dinv[:, at:at + n], rs[:, 0:n]))
                me.mark(dve.tensor_tensor(dinv2[:, at:at + n], rs[:, 0:n], rs[:, 0:n], ALU.mult))
                me.mark(dve.tensor_tensor(sdeg[:, at:at + n], rs[:, 0:n], first.arg[:, 0:n], ALU.mult))
                me.wait()

            me.wait()
            me.send(dve.tensor_scalar(first.arg[:, 0:COLS], deg[:, 0:COLS], 1.0, None, ALU.add), arg_ready, 1)
            dve.wait_ge(w1x_done, 1)
            me.mark(refine(first, COLS, root_ready, 1))
            degree_values(0, COLS)
            me.send(dve.tensor_copy(w1x[0:D, :], psQV[0:D, 0:D]), prep_done, 1)

            def dense(c, n=DC):
                used(dve, d_loaded, c)
                me.send(stats(first, DX[c.slot], n), d_arg, c.n + 1)
                dense_scale(c.before(1))
                me.mark(refine(first, n, d_root, c.n + 1))
                dense_scaled(c.before(1))
                done(dve, d_out, c.before(2))
                me.wait()
                for g, at, m in groups(n):
                    i = c.n * DG + g
                    dve.wait_ge(d_mult, i + 1)
                    for j in range(m):
                        last = dve.scalar_tensor_tensor(
                            out=DY[c.slot][:, at + j, :], in0=dY[g % 4][:, j * D:(j + 1) * D],
                            scalar=first.root[:, at + j:at + j + 1], in1=b1c[:, :], op0=ALU.mult, op1=ALU.add)
                    me.send(last, d_read, i + 1)

            def dense_scale(c, n=DC):
                if c.exists:
                    done(dve, d_sq, c)
                    me.wait()
                    me.mark(dve.tensor_reduce(second.t[:, 5, 0:n], DSQ[:, 0:n, :], AX, ALU.add))
                    me.wait()
                    me.send(dve.tensor_scalar(second.arg[:, 0:n], second.t[:, 5, 0:n], (1 + EPS / 2) ** 2 / D,
                                              EPS ** 3 / 4, ALU.mult, ALU.add), y_arg, c.n + 1)

            def dense_scaled(c, n=DC):
                if c.exists:
                    me.send(refine(second, n, y_root, c.n + 1), d_scale, c.n + 1)

            each_chunk(dve, DCHUNKS, 2, dense, [me])
            last_dense = Chunk(DCHUNKS, 2, DCHUNKS % 2, DCHUNKS // 2 + 1)
            dense(last_dense, 2)
            dense_scale(last_dense, 2)
            dense_scaled(last_dense, 2)
            for k in range(2):
                dve.wait_ge(d_stored[k], 16 * len(range(k, DCHUNKS + 1, 2)))
            me.mark(dve.memset(AG[0][:, :, :], 0.0))
            me.mark(dve.memset(AG[1][:, :, :], 0.0))

            for r in ROUNDS:
                s = S[r]
                w = {0: D + 1, 1: 2 * D, 2: D, 3: D, 4: W4}[r]

                def keep_of(c):
                    keep = keep_fwd if r < 4 else keep_rev
                    me.mark(dve.tensor_copy(kc[c.parity][:, :], keep[:, bass.ds(cols(r, c), C)]))

                def running(c, values, signal=None, between=None):
                    b = c.parity
                    for j in range(C):
                        prev = AG[b][:, j - 1, 0:w] if j else AG[1 - b][:, C - 1, 0:w]
                        me.wait()
                        summed = dve.scalar_tensor_tensor(out=AG[b][:, j, 0:w], in0=prev, scalar=kc[b][:, j:j + 1],
                                                          in1=values[:, j, 0:w], op0=ALU.mult, op1=ALU.add)
                        if signal and j == C - 1:
                            me.send(summed, signal, c.n + 1)
                        else:
                            me.mark(summed)
                        if between:
                            between(j)

                def dst_input(c, ag):
                    b, n, at = c.parity, width(c), cols(r, c)
                    done(dve, s.turned, c.before(2), s.groups, 2 - s.groups)
                    if r == 0:
                        me.wait()
                        me.send(dve.tensor_tensor(AM[b][:, 0:n, :], ag[:, 0:n, 0:D], wide(rdeg, at, n), ALU.mult), s.am_ready, c.n + 1)
                    else:
                        used(dve, s.xd_loaded, c)
                        done(dve, s.z_guess, c)
                        me.wait()
                        me.mark(dve.tensor_tensor(U3[:, 0:n, :], ag[:, 0:n, D:2 * D], GZ[:, 0:n, :], ALU.mult))
                        me.wait()
                        me.mark(dve.scalar_tensor_tensor(out=U2[:, 0:n, :], in0=U3[:, 0:n, :], scalar=-2.0,
                                                         in1=GZ[:, 0:n, :], op0=ALU.add, op1=ALU.mult))
                        me.wait()
                        me.mark(dve.tensor_tensor(U3[:, 0:n, :], ag[:, 0:n, 0:D], U2[:, 0:n, :], ALU.mult))
                        me.wait()
                        me.send(dve.tensor_tensor(AM[b][:, 0:n, :], XD[c.slot][:, 0:n, :], U3[:, 0:n, :], ALU.subtract), s.am_ready, c.n + 1)

                def hop(c, ag):
                    n, at, b = width(c), cols(r, c), c.parity
                    used(dve, s.xd_loaded, c, 16 if r == 2 else 32)
                    me.wait()
                    me.mark(dve.tensor_tensor(U2[:, 0:n, :], ag[:, 0:n, 0:D], XD[c.slot][:, 0:n, :], ALU.add))
                    if r == 2:
                        used(dve, s.stored, c.before(RING))
                        me.wait()
                        me.send(dve.tensor_tensor(OT[c.slot][:, 0:n, :], U2[:, 0:n, :], wide(dinv2, at, n), ALU.mult), s.updated, c.n + 1)
                    else:
                        me.wait()
                        me.mark(dve.tensor_tensor(AM[0][:, 0:n, :], U2[:, 0:n, :], wide(dinv, at, n), ALU.mult))
                        done(dve, s.updated, c.before(2))
                        done(dve, s.scaled, c)
                        me.wait()
                        added = dve.tensor_tensor(UB[b][:, 0:n, :], MM[b][:, 0:n, :], AM[0][:, 0:n, :], ALU.add)
                        me.mark(added)
                        if c is SEAM:
                            me.send(stats(second, UB[b], n), s.arg, c.n + 1)

                def shifts(n, lo=0, scale=None):
                    by = second.root
                    me.wait()
                    if scale is not None:
                        me.mark(dve.tensor_tensor(second.by[:, lo:lo + n], second.root[:, lo:lo + n], scale, ALU.mult))
                        by = second.by
                        me.wait()
                    return dve.scalar_tensor_tensor(out=second.shift[:, lo:lo + n], in0=second.mean[:, lo:lo + n],
                                                    scalar=-0.5, in1=by[:, lo:lo + n], op0=ALU.mult, op1=ALU.mult)

                def normalised(c):
                    if c.exists:
                        n = width(c)
                        me.mark(refine(second, n, s.root, c.n + 1))
                        scale = dinv[:, bass.ds(cols(r, c), n)] if r == 1 else None
                        me.send(shifts(n, 0, scale), s.norm_ready, c.n + 1)

                def product_added(c):
                    if not c.exists:
                        return
                    b, n = c.parity, width(c)
                    lo = 2 * C if r == 0 and c is not SEAM else 0
                    if r == 0 and c is SEAM:
                        dve.wait_ge(s.gathered[c.slot][0], (c.turn - 1) * 2 * 16 * C + 16)
                    if r == 1:
                        me.wait()
                        for g, at, m in groups(n):
                            dve.wait_ge(s.mult, c.n * s.groups + g + 1)
                            for j in range(m):
                                last = dve.bn_stats(out=second.st[:, at + j, :], in_=psX[b][g][:, j * D:(j + 1) * D])
                        me.mark(last)
                        me.send(variance(second, n), s.arg, c.n + 1)
                        return
                    done(dve, s.updated, c.before(2))
                    me.wait()
                    for g, at, m in groups(n):
                        dve.wait_ge(s.mult, c.n * s.groups + g + 1)
                        me.mark(dve.tensor_tensor(UB[b][:, at:at + m, :], by_rows(psU[g], m), XD[c.slot][:, at:at + m, :],
                                                  ALU.add))
                    variances = stats(second, UB[b], n, lo)
                    if not lo:
                        me.send(variances, s.arg, c.n + 1)
                        return
                    me.mark(variances)
                    done(dve, s.squared, c)
                    me.mark(dve.tensor_reduce(second.t[:, 5, 0:n], SQ[:, :, :], AX, ALU.add))
                    me.wait()
                    me.mark(dve.tensor_scalar(second.arg[:, 0:C], second.t[:, 5, 0:C], 1.0 / D, EPS, ALU.mult, ALU.add))
                    me.send(dve.tensor_scalar(second.arg[:, C:2 * C], second.t[:, 5, 0:C], (1 + EPS / 4) / D, EPS * EPS / 4,
                                              ALU.mult, ALU.add), s.arg, c.n + 1)

                def finished(c):
                    if not c.exists:
                        return
                    b, n = c.parity, width(c)
                    lo = 0 if c is SEAM else 2 * C
                    me.mark(refine(second, lo + n, s.root, c.n + 1))
                    if c is not SEAM:
                        plain_free(dve, s, c)
                        me.wait()
                        for g, at, m in groups(n):
                            y = by_rows(psY[g], m)
                            me.mark(dve.tensor_tensor(PL2[b][:, at:at + m, :], y, wide(second.root, at, m), ALU.mult))
                            me.mark(dve.tensor_tensor(PL4[b][:, at:at + m, :], y, wide(second.root, C + at, m), ALU.mult))
                    me.send(shifts(n, lo), s.norm_ready, c.n + 1)

                def scored(c):
                    if not c.exists:
                        return
                    b = c.parity
                    me.wait()
                    for g, at, m in groups(C):
                        k = c.n * 2 + g + 1
                        dve.wait_ge(s.ke_mult, k)
                        dve.wait_ge(s.q_copied, k)
                        me.mark(dve.tensor_tensor(U2[:, at:at + m, :], by_rows(psK[g], m), QS[b][:, at:at + m, :], ALU.mult))
                    for g, at, m in groups(C):
                        me.wait()
                        me.send(dve.tensor_tensor(U3[:, at:at + m, :], by_rows(psE[g], m), U2[:, at:at + m, :], ALU.mult),
                                s.ke_read, c.n * 2 + g + 1)
                    me.wait()
                    me.mark(dve.tensor_reduce(SC[:, :, :].rearrange("p m h -> p (m h)"),
                                              U3[:, :, :].rearrange("p m (h e) -> p (m h) e", e=HD), AX, ALU.add))
                    me.wait()
                    me.mark(dve.tensor_scalar(SC[:, :, :], SC[:, :, :], float(HD) ** -0.5, 5.0, ALU.mult, ALU.min))
                    me.wait()
                    me.send(dve.tensor_scalar(SC2[:, :, :], SC[:, :, :], -5.0, None, ALU.max), s.score_ready, c.n + 1)

                def dst_rows(c):
                    b, at = c.parity, cols(r, c)
                    me.wait()
                    me.mark(dve.tensor_copy(pc[:, :], pull[:, bass.ds(at, C)]))
                    done(dve, s.scaled, c)
                    done(dve, s.turned, c.before(2), 6)
                    for j in reversed(range(C)):
                        prev = XB[b][:, j + 1, :] if j < C - 1 else XB[1 - b][:, 0, :]
                        me.wait()
                        row = dve.scalar_tensor_tensor(out=XB[b][:, j, :], in0=prev, scalar=pc[:, j:j + 1],
                                                       in1=XA[b][:, j, :], op0=ALU.mult, op1=ALU.add)
                        if j:
                            me.mark(row)
                        else:
                            me.send(row, s.xb_ready, c.n + 1)

                def per_head(row):
                    return row.rearrange("p (h e) -> p h e", e=HD)

                def messages(c):
                    if not c.exists:
                        return
                    b = c.parity
                    done(dve, s.exp_ready, c)
                    dve.wait_ge(s.v_copied, (c.n + 1) * 2)
                    keep_of(c)
                    me.wait()

                    def message(j):
                        made = dve.tensor_tensor(per_head(MS[b][:, j, 0:D]), per_head(VS[b][:, j, :]),
                                                 MS[b][:, j, D:W4].unsqueeze(2).to_broadcast([P, HEADS, HD]), ALU.mult)
                        if j:
                            me.mark(made)
                        else:
                            me.send(made, s.msg_ready, c.n + 1)

                    message(C - 1)
                    for j in reversed(range(C)):
                        prev = AG[b][:, j + 1, 0:w] if j < C - 1 else AG[1 - b][:, 0, 0:w]
                        if j:
                            message(j - 1)
                        me.wait(but=1 if j > 1 else 0)
                        me.mark(dve.scalar_tensor_tensor(out=AG[b][:, j, 0:w], in0=prev, scalar=kc[b][:, j:j + 1],
                                                         in1=MS[b][:, j, 0:w], op0=ALU.mult, op1=ALU.add))
                    attended(c, AG[b])

                def attended(c, sums):
                    b, n = c.parity, width(c)
                    me.wait()
                    me.mark(dve.tensor_scalar(SC[:, 0:n, :], sums[:, 0:n, D:W4], 1e-6, None, ALU.add))
                    me.wait()
                    me.mark(dve.reciprocal(ZR[:, 0:n, :], SC[:, 0:n, :]))
                    me.wait()
                    for j in range(n):
                        last = dve.tensor_tensor(per_head(U2[:, j, :]), per_head(sums[:, j, 0:D]),
                                                 ZR[:, j, :].unsqueeze(2).to_broadcast([P, HEADS, HD]), ALU.mult)
                    me.mark(last)
                    done(dve, s.updated, c.before(2))
                    me.wait()
                    xb = xseam[:, :].unsqueeze(1) if c is SEAM else XB[b][:, :, :]
                    me.mark(dve.tensor_tensor(UB[b][:, 0:n, :], U2[:, 0:n, :], xb, ALU.add))
                    me.send(stats(second, UB[b], n), s.arg, c.n + 1)

                def step(c):
                    b = c.parity
                    if r < 4:
                        keep_of(c)
                    if r == 0:
                        used(dve, s.gathered, c, 2 * 16 * C)

                        def column_stats(j):
                            bn = dve.bn_stats(out=first.st[:, j, :], in_=V[c.slot][:, j, 0:D])
                            if j == C - 1:
                                me.mark(bn)

                        running(c, V[c.slot], None, column_stats)
                        dst_input(c, AG[b])
                        me.send(variance(first, C), s.x1_arg, c.n + 1)
                        product_added(c.before(1))
                        me.mark(refine(first, C, s.x1_root, c.n + 1))
                        me.wait()
                        me.send(dve.scalar_tensor_tensor(out=first.shift[:, 0:C], in0=first.mean[:, 0:C], scalar=-0.5,
                                                         in1=first.root[:, 0:C], op0=ALU.mult, op1=ALU.mult), s.x1_norm, c.n + 1)
                        finished(c.before(1))
                    if r == 1:
                        done(dve, s.exp_ready, c)
                        me.wait()
                        me.send(dve.scalar_tensor_tensor(out=MS[b][:, :, 0:D], in0=MM[b][:, :, :], scalar=1e-7,
                                                         in1=MS[b][:, :, D:2 * D], op0=ALU.add, op1=ALU.mult), s.msg_ready, c.n + 1)
                        running(c, MS[b], s.z_ready)
                        product_added(c.before(1))
                        dst_input(c, AG[b])
                        normalised(c.before(1))
                    if r in (2, 3):
                        used(dve, s.gathered, c, 16 * C)
                        old = c.before(1)

                        def old_stats(j):
                            bn = dve.bn_stats(out=second.st[:, j, :], in_=UB[old.parity][:, j, :])
                            if j == C - 1:
                                me.mark(bn)

                        if r == 2 or not old.exists:
                            running(c, V[c.slot], s.front)
                        else:
                            running(c, V[c.slot], s.front, old_stats)
                            me.send(variance(second, C), s.arg, old.n + 1)
                        hop(c, AG[b])
                        if r == 3:
                            normalised(old)
                    if r == 4:
                        dst_rows(c)
                        scored(c.before(1))
                        normalised(c.before(2))
                        messages(c.before(1))

                if r == 4:
                    dve.wait_ge(s.seam_loaded, 32)
                    me.mark(dve.tensor_copy(XB[1][:, 0, :], xnext[:, :]))
                each_chunk(dve, CHUNKS, RING, step, [me])
                final = SEAM.before(1)
                if r in (0, 1):
                    product_added(final)
                if r == 0:
                    finished(final)
                if r == 3:
                    me.send(stats(second, UB[final.parity], C), s.arg, final.n + 1)
                if r in (1, 3):
                    normalised(final)
                if r == 4:
                    scored(final)
                    normalised(SEAM.before(2))
                    messages(final)
                    normalised(final)

                dve.wait_ge(s.seam_total, 1)
                me.mark(dve.tensor_copy(SG[:, 0, 0:w], psS[:, 0:w]))
                me.wait()
                if r == 0:
                    me.mark(dve.tensor_copy(deg[:, COLS:TC], SG[:, 0, D:D + 1]))
                    me.wait()
                    me.send(dve.tensor_scalar(first.arg[:, 0:1], SG[:, 0, D:D + 1], 1.0, None, ALU.add), s.deg_arg, 1)
                    me.mark(refine(first, 1, s.deg_root, 1))
                    degree_values(COLS, 1)
                if r == 1:
                    me.send(dve.tensor_copy(second.t[:, 0, 0:1], SG[:, 0, D:D + 1]), s.z_ready, SEAM.n + 1)
                if r in (0, 1):
                    dst_input(SEAM, SG)
                    product_added(SEAM)
                if r == 0:
                    finished(SEAM)
                if r in (2, 3):
                    hop(SEAM, SG)
                if r == 4:
                    attended(SEAM, SG)
                if r in (1, 3, 4):
                    normalised(SEAM)



_INS = ["x", "src", "dst", "edge_attr_96", "L0_gnn_W", "L0_gnn_b", "L1_gnn_W", "L1_gnn_b", "L3_gnn_Wq", "L3_gnn_bq",
        "L3_gnn_Wk", "L3_gnn_bk", "L3_gnn_We", "L3_gnn_be", "L3_gnn_Wv", "L3_gnn_bv"]


def kernel(**inputs):
    import numpy as _np
    import concourse.bacc as _bacc
    from concourse import mybir as _mybir
    from concourse.bass_utils import run_bass_kernel_spmd as _run

    nc = _bacc.Bacc("TRN2", target_bir_lowering=False, num_devices=1)
    arrays, args = {}, []
    for name in _INS:
        a = _np.ascontiguousarray(inputs[name])
        arrays[f"in_{name}"] = a
        args.append(nc.dram_tensor(f"in_{name}", a.shape, _mybir.dt.from_np(a.dtype), kind="ExternalInput").ap())
    result = nc.dram_tensor("out_dram", (N, D), _mybir.dt.float32, kind="ExternalOutput").ap()
    build(nc, *args, result)
    r = _run(nc, [arrays], core_ids=[0])
    return r.results[0]["out_dram"]
```
